# Optimizing a Trainium2 kernel written in Bass

```python
import numpy as np
import jax
import jax.numpy as jnp

def _softmax(x, axis=-1):
    return jax.nn.softmax(x, axis=axis)

def _gelu(x):
    return jax.nn.gelu(x, approximate=True)

def _silu(x):
    return jax.nn.silu(x)

def _sigmoid(x):
    return jax.nn.sigmoid(x)

def _layernorm(x, axis=-1, eps=1e-05):
    m = jnp.mean(x, axis=axis, keepdims=True)
    v = jnp.var(x, axis=axis, keepdims=True)
    return (x - m) / jnp.sqrt(v + eps)

def _scatter_add(tgt, idx, src, axis=0):
    return tgt.at[idx].add(src)

def _segment_sum(src, seg, n):
    return jax.ops.segment_sum(src, seg, n)
kernel_name = 'mk_perceiver_d1_seqx_r2_07664c'

def setup_inputs(seed: int=0):
    np.random.seed(seed)
    _w = jnp.asarray

    def _rec_inputs():
        import jax
        import jax.numpy as jnp
        _rk = jax.random.key(seed)
        x = -0.0002928 + 1 * jax.random.normal(jax.random.fold_in(_rk, 1), (8, 64, 512), jnp.float32)
        _lenS = 64 - jax.random.randint(jax.random.fold_in(_rk, 7), (8,), 0, max(1, 64 // 4) + 1, jnp.int32)
        _lenS2 = 1601 - jax.random.randint(jax.random.fold_in(_rk, 8), (8,), 0, max(1, 1601 // 4) + 1, jnp.int32)
        _ctx_1024P = jax.random.normal(jax.random.fold_in(_rk, 11), (8, 16, 512), jnp.float32)
        _ctx_1024c = jax.random.dirichlet(jax.random.fold_in(_rk, 511), 0.3 * jnp.ones((16,), jnp.float32), (8, 1601))
        _ctx_1024t = jnp.einsum('bsk,bkd->bsd', _ctx_1024c, _ctx_1024P)
        _ctx_1024t = _ctx_1024t * jax.lax.rsqrt(jnp.mean(jnp.square(_ctx_1024t)) + 1e-12) * 0.953939
        ctx_1024 = -1.39393e-06 + 0.999914 * (_ctx_1024t + 0.3 * jax.random.normal(jax.random.fold_in(_rk, 611), (8, 1601, 512), jnp.float32))
        _validS = jnp.arange(64)[None, :] < _lenS[:, None]
        _validS2 = jnp.arange(1601)[None, :] < _lenS2[:, None]
        _causal = jnp.tril(jnp.ones((64, 64), dtype=bool))
        mask_Bx1xSxS2_ik1 = jnp.where(jnp.broadcast_to(_validS2[:, None, None, :], (8, 1, 64, 1601)), 1, 0).astype(jnp.int32)
        return (x, ctx_1024, mask_Bx1xSxS2_ik1)
    x, ctx_1024, mask_Bx1xSxS2_ik1 = _rec_inputs()

    def _L0_xattn_setup():
        import jax, jax.numpy as jnp
        import numpy as np
        D_MODEL = 512
        H = 16
        D_K = D_MODEL // H
        B = 2
        S = 1024

        def _split_heads(x):
            b, s, _ = x.shape
            return x.reshape(b, s, H, D_K).transpose(0, 2, 1, 3)
        key = jax.random.key(seed)
        ks = jax.random.split(key, 13)
        scale = 1.0 / np.sqrt(D_MODEL)
        inp = {'Q': jax.random.normal(ks[0], (B, S, D_MODEL), jnp.float32), 'K': jax.random.normal(ks[1], (B, S, D_MODEL), jnp.float32), 'V': jax.random.normal(ks[2], (B, S, D_MODEL), jnp.float32), 'mask': jax.random.randint(ks[3], (B, 1, S, S), 0, 2, jnp.int32), 'WQ_w': jax.random.normal(ks[4], (D_MODEL, D_MODEL), jnp.float32) * scale, 'WQ_b': jax.random.normal(ks[5], (D_MODEL,), jnp.float32) * scale, 'WK_w': jax.random.normal(ks[6], (D_MODEL, D_MODEL), jnp.float32) * scale, 'WK_b': jax.random.normal(ks[7], (D_MODEL,), jnp.float32) * scale, 'WV_w': jax.random.normal(ks[8], (D_MODEL, D_MODEL), jnp.float32) * scale, 'WV_b': jax.random.normal(ks[9], (D_MODEL,), jnp.float32) * scale, 'WO_w': jax.random.normal(ks[10], (D_MODEL, D_MODEL), jnp.float32) * scale, 'WO_b': jax.random.normal(ks[11], (D_MODEL,), jnp.float32) * scale}
        return inp
    _L0_xattn_all = _L0_xattn_setup()
    _L0_xattn_in = {k: v for k, v in _L0_xattn_all.items() if k in ('WQ_w', 'WQ_b', 'WK_w', 'WK_b', 'WV_w', 'WV_b', 'WO_w', 'WO_b')}
    del _L0_xattn_all

    def _L0_attn_setup():
        import jax, jax.numpy as jnp
        import numpy as np
        H = 16
        E = 512
        D = E // H
        M = 512
        EPS = 1e-12
        key = jax.random.key(seed)
        ks = jax.random.split(key, 12)
        s = 0.02
        B, S = (8, 512)
        return {'hidden_states': jax.random.normal(ks[0], (B, S, E), jnp.float32), 'Wq': jax.random.normal(ks[1], (E, E), jnp.float32) * s, 'bq': jnp.zeros((E,), jnp.float32), 'Wk': jax.random.normal(ks[2], (E, E), jnp.float32) * s, 'bk': jnp.zeros((E,), jnp.float32), 'Wv': jax.random.normal(ks[3], (E, E), jnp.float32) * s, 'bv': jnp.zeros((E,), jnp.float32), 'dist_emb': jax.random.normal(ks[4], (2 * M - 1, D), jnp.float32) * s, 'Wo': jax.random.normal(ks[5], (E, E), jnp.float32) * s, 'bo': jnp.zeros((E,), jnp.float32), 'ln_gamma': jnp.ones((E,), jnp.float32), 'ln_beta': jnp.zeros((E,), jnp.float32)}
    _L0_attn_all = _L0_attn_setup()
    _L0_attn_in = {k: v for k, v in _L0_attn_all.items() if k in ('Wq', 'bq', 'Wk', 'bk', 'Wv', 'bv', 'dist_emb', 'Wo', 'bo', 'ln_gamma', 'ln_beta')}
    del _L0_attn_all

    def _L0_ffn_setup():
        import jax, jax.numpy as jnp
        import numpy as np
        B, S, D = (2, 512, 512)
        L, H = (256, 16)
        HD = L // H
        F, E, K = (1024, 8, 2)
        THETA = 10000.0
        EPS = 1e-05

        def _rmsnorm(x, g):
            return x * g * jax.lax.rsqrt(jnp.mean(x * x, axis=-1, keepdims=True) + EPS)

        def _rope(t, pos):
            inv_freq = 1.0 / THETA ** (jnp.arange(0, HD, 2, dtype=jnp.float32) / HD)
            ang = pos[:, None].astype(jnp.float32) * inv_freq[None, :]
            cos, sin = (jnp.cos(ang), jnp.sin(ang))
            t1, t2 = (t[..., 0::2], t[..., 1::2])
            r1 = t1 * cos - t2 * sin
            r2 = t1 * sin + t2 * cos
            return jnp.stack([r1, r2], axis=-1).reshape(t.shape)

        def _forward(x, g1, g2, w_down, wq, wk, wv, w_up, router_w, w1, w2, w3):
            b, s, _ = x.shape
            pos = jnp.arange(s)
            h = _rmsnorm(x, g1)
            c = h @ w_down
            split = lambda t: t.reshape(b, s, H, HD).transpose(0, 2, 1, 3)
            q = _rope(split(c @ wq), pos)
            k = _rope(split(c @ wk), pos)
            v = split(c @ wv)
            scores = jnp.einsum('bhqd,bhkd->bhqk', q, k) / jnp.sqrt(jnp.float32(HD))
            causal = jnp.tril(jnp.ones((s, s), bool))
            scores = jnp.where(causal, scores, -jnp.inf)
            attn = jax.nn.softmax(scores, axis=-1)
            o = jnp.einsum('bhqk,bhkd->bhqd', attn, v).transpose(0, 2, 1, 3).reshape(b, s, L)
            x = x + o @ w_up
            res = x
            t = _rmsnorm(x, g2).reshape(-1, D)
            probs = jax.nn.softmax(t @ router_w, axis=-1)
            vals, idx = jax.lax.top_k(probs, K)
            w = vals / jnp.sum(vals, axis=-1, keepdims=True)
            gate = jnp.sum(jax.nn.one_hot(idx, E, dtype=t.dtype) * w[..., None], axis=1)
            hid = jax.nn.silu(jnp.einsum('td,edf->tef', t, w1)) * jnp.einsum('td,edf->tef', t, w3)
            y_e = jnp.einsum('tef,efd->ted', hid, w2)
            y = jnp.einsum('ted,te->td', y_e, gate)
            return res + y.reshape(b, s, D)
        key = jax.random.key(seed)
        ks = jax.random.split(key, 12)
        g = lambda k, shape, scale: jax.random.normal(k, shape, dtype=jnp.float32) * scale
        return {'x': g(ks[0], (B, S, D), 1.0), 'g1': jnp.ones((D,), jnp.float32), 'g2': jnp.ones((D,), jnp.float32), 'w_down': g(ks[1], (D, L), 0.02), 'wq': g(ks[2], (L, L), 0.02), 'wk': g(ks[3], (L, L), 0.02), 'wv': g(ks[4], (L, L), 0.02), 'w_up': g(ks[5], (L, D), 0.02), 'router_w': g(ks[6], (D, E), 0.02), 'w1': g(ks[7], (E, D, F), 0.02), 'w3': g(ks[8], (E, D, F), 0.02), 'w2': g(ks[9], (E, F, D), 0.02)}
    _L0_ffn_all = _L0_ffn_setup()
    _L0_ffn_in = {k: v for k, v in _L0_ffn_all.items() if k in ('g1', 'g2', 'w_down', 'wq', 'wk', 'wv', 'w_up', 'router_w', 'w1', 'w2', 'w3')}
    del _L0_ffn_all
    return {'x': x, 'ctx_1024': ctx_1024, 'mask_Bx1xSxS2_ik1': mask_Bx1xSxS2_ik1, 'L0_xattn_WQ_w': _L0_xattn_in['WQ_w'], 'L0_xattn_WQ_b': _L0_xattn_in['WQ_b'], 'L0_xattn_WK_w': _L0_xattn_in['WK_w'], 'L0_xattn_WK_b': _L0_xattn_in['WK_b'], 'L0_xattn_WV_w': _L0_xattn_in['WV_w'], 'L0_xattn_WV_b': _L0_xattn_in['WV_b'], 'L0_xattn_WO_w': _L0_xattn_in['WO_w'], 'L0_xattn_WO_b': _L0_xattn_in['WO_b'], 'L0_attn_Wq': _L0_attn_in['Wq'], 'L0_attn_bq': _L0_attn_in['bq'], 'L0_attn_Wk': _L0_attn_in['Wk'], 'L0_attn_bk': _L0_attn_in['bk'], 'L0_attn_Wv': _L0_attn_in['Wv'], 'L0_attn_bv': _L0_attn_in['bv'], 'L0_attn_dist_emb': _L0_attn_in['dist_emb'], 'L0_attn_Wo': _L0_attn_in['Wo'], 'L0_attn_bo': _L0_attn_in['bo'], 'L0_attn_ln_gamma': _L0_attn_in['ln_gamma'], 'L0_attn_ln_beta': _L0_attn_in['ln_beta'], 'L0_ffn_g1': _L0_ffn_in['g1'], 'L0_ffn_g2': _L0_ffn_in['g2'], 'L0_ffn_w_down': _L0_ffn_in['w_down'], 'L0_ffn_wq': _L0_ffn_in['wq'], 'L0_ffn_wk': _L0_ffn_in['wk'], 'L0_ffn_wv': _L0_ffn_in['wv'], 'L0_ffn_w_up': _L0_ffn_in['w_up'], 'L0_ffn_router_w': _L0_ffn_in['router_w'], 'L0_ffn_w1': _L0_ffn_in['w1'], 'L0_ffn_w2': _L0_ffn_in['w2'], 'L0_ffn_w3': _L0_ffn_in['w3']}

def reference(x, ctx_1024, mask_Bx1xSxS2_ik1, L0_xattn_WQ_w, L0_xattn_WQ_b, L0_xattn_WK_w, L0_xattn_WK_b, L0_xattn_WV_w, L0_xattn_WV_b, L0_xattn_WO_w, L0_xattn_WO_b, L0_attn_Wq, L0_attn_bq, L0_attn_Wk, L0_attn_bk, L0_attn_Wv, L0_attn_bv, L0_attn_dist_emb, L0_attn_Wo, L0_attn_bo, L0_attn_ln_gamma, L0_attn_ln_beta, L0_ffn_g1, L0_ffn_g2, L0_ffn_w_down, L0_ffn_wq, L0_ffn_wk, L0_ffn_wv, L0_ffn_w_up, L0_ffn_router_w, L0_ffn_w1, L0_ffn_w2, L0_ffn_w3):
    import jax
    import jax.numpy as jnp

    def _L0_xattn_ref(Q, K, V, mask, WQ_w, WQ_b, WK_w, WK_b, WV_w, WV_b, WO_w, WO_b):
        import jax, jax.numpy as jnp
        import numpy as np
        D_MODEL = 512
        H = 16
        D_K = D_MODEL // H
        B = 2
        S = 1024

        def _split_heads(x):
            b, s, _ = x.shape
            return x.reshape(b, s, H, D_K).transpose(0, 2, 1, 3)
        q = _split_heads(Q @ WQ_w.T + WQ_b)
        k = _split_heads(K @ WK_w.T + WK_b)
        v = _split_heads(V @ WV_w.T + WV_b)
        scores = jnp.einsum('bhqd,bhkd->bhqk', q, k) / jnp.sqrt(jnp.float32(D_K))
        scores = jnp.where(mask == 0, jnp.float32(1e-09), scores)
        attn = jax.nn.softmax(scores, axis=-1)
        out = jnp.einsum('bhqk,bhkd->bhqd', attn, v)
        out = out.transpose(0, 2, 1, 3).reshape(Q.shape[0], -1, D_MODEL)
        return out @ WO_w.T + WO_b

    def _L0_attn_ref(hidden_states, Wq, bq, Wk, bk, Wv, bv, dist_emb, Wo, bo, ln_gamma, ln_beta):
        import jax, jax.numpy as jnp
        import numpy as np
        H = 16
        E = 512
        D = E // H
        M = 512
        EPS = 1e-12
        B, S, _ = hidden_states.shape

        def heads(x):
            return x.reshape(B, S, H, D).transpose(0, 2, 1, 3)
        q = heads(hidden_states @ Wq + bq)
        k = heads(hidden_states @ Wk + bk)
        v = heads(hidden_states @ Wv + bv)
        scores = jnp.einsum('bhqd,bhkd->bhqk', q, k)
        pos_l = jnp.arange(S)[:, None]
        pos_r = jnp.arange(S)[None, :]
        dist_idx = pos_l - pos_r + M - 1
        pos_emb = dist_emb[dist_idx]
        rel_q = jnp.einsum('bhld,lrd->bhlr', q, pos_emb)
        rel_k = jnp.einsum('bhrd,lrd->bhlr', k, pos_emb)
        scores = (scores + rel_q + rel_k) / jnp.sqrt(jnp.asarray(D, scores.dtype))
        probs = jax.nn.softmax(scores, axis=-1)
        ctx = jnp.einsum('bhqk,bhkd->bhqd', probs, v)
        ctx = ctx.transpose(0, 2, 1, 3).reshape(B, S, E)
        h = ctx @ Wo + bo + hidden_states
        mu = jnp.mean(h, axis=-1, keepdims=True)
        var = jnp.mean(jnp.square(h - mu), axis=-1, keepdims=True)
        out = (h - mu) * jax.lax.rsqrt(var + EPS) * ln_gamma + ln_beta
        return out

    def _L0_ffn_ref(x, g1, g2, w_down, wq, wk, wv, w_up, router_w, w1, w2, w3):
        import jax, jax.numpy as jnp
        import numpy as np
        B, S, D = (2, 512, 512)
        L, H = (256, 16)
        HD = L // H
        F, E, K = (1024, 8, 2)
        THETA = 10000.0
        EPS = 1e-05

        def _rmsnorm(x, g):
            return x * g * jax.lax.rsqrt(jnp.mean(x * x, axis=-1, keepdims=True) + EPS)

        def _rope(t, pos):
            inv_freq = 1.0 / THETA ** (jnp.arange(0, HD, 2, dtype=jnp.float32) / HD)
            ang = pos[:, None].astype(jnp.float32) * inv_freq[None, :]
            cos, sin = (jnp.cos(ang), jnp.sin(ang))
            t1, t2 = (t[..., 0::2], t[..., 1::2])
            r1 = t1 * cos - t2 * sin
            r2 = t1 * sin + t2 * cos
            return jnp.stack([r1, r2], axis=-1).reshape(t.shape)

        def _forward(x, g1, g2, w_down, wq, wk, wv, w_up, router_w, w1, w2, w3):
            b, s, _ = x.shape
            pos = jnp.arange(s)
            h = _rmsnorm(x, g1)
            c = h @ w_down
            split = lambda t: t.reshape(b, s, H, HD).transpose(0, 2, 1, 3)
            q = _rope(split(c @ wq), pos)
            k = _rope(split(c @ wk), pos)
            v = split(c @ wv)
            scores = jnp.einsum('bhqd,bhkd->bhqk', q, k) / jnp.sqrt(jnp.float32(HD))
            causal = jnp.tril(jnp.ones((s, s), bool))
            scores = jnp.where(causal, scores, -jnp.inf)
            attn = jax.nn.softmax(scores, axis=-1)
            o = jnp.einsum('bhqk,bhkd->bhqd', attn, v).transpose(0, 2, 1, 3).reshape(b, s, L)
            x = x + o @ w_up
            res = x
            t = _rmsnorm(x, g2).reshape(-1, D)
            probs = jax.nn.softmax(t @ router_w, axis=-1)
            vals, idx = jax.lax.top_k(probs, K)
            w = vals / jnp.sum(vals, axis=-1, keepdims=True)
            gate = jnp.sum(jax.nn.one_hot(idx, E, dtype=t.dtype) * w[..., None], axis=1)
            hid = jax.nn.silu(jnp.einsum('td,edf->tef', t, w1)) * jnp.einsum('td,edf->tef', t, w3)
            y_e = jnp.einsum('tef,efd->ted', hid, w2)
            y = jnp.einsum('ted,te->td', y_e, gate)
            return res + y.reshape(b, s, D)
        return _forward(x, g1, g2, w_down, wq, wk, wv, w_up, router_w, w1, w2, w3)
    x = x + _L0_xattn_ref(_layernorm(x, axis=-1), ctx_1024, ctx_1024, mask_Bx1xSxS2_ik1, L0_xattn_WQ_w, L0_xattn_WQ_b, L0_xattn_WK_w, L0_xattn_WK_b, L0_xattn_WV_w, L0_xattn_WV_b, L0_xattn_WO_w, L0_xattn_WO_b)
    x = x + _L0_attn_ref(_layernorm(x, axis=-1), L0_attn_Wq, L0_attn_bq, L0_attn_Wk, L0_attn_bk, L0_attn_Wv, L0_attn_bv, L0_attn_dist_emb, L0_attn_Wo, L0_attn_bo, L0_attn_ln_gamma, L0_attn_ln_beta)
    x = x + _L0_ffn_ref(_layernorm(x, axis=-1), L0_ffn_g1, L0_ffn_g2, L0_ffn_w_down, L0_ffn_wq, L0_ffn_wk, L0_ffn_wv, L0_ffn_w_up, L0_ffn_router_w, L0_ffn_w1, L0_ffn_w2, L0_ffn_w3)
    return x

_drawn_inputs = setup_inputs


def setup_inputs(seed=0):
    import zlib

    import numpy as np

    out = dict(_drawn_inputs(seed))
    spreads = {'L0_attn_bq': (0.0, 0.8),
     'L0_attn_bk': (0.0, 0.8),
     'L0_attn_bv': (0.0, 0.379),
     'L0_attn_bo': (0.0, 0.1),
     'L0_attn_ln_gamma': (1.0, 0.2),
     'L0_attn_ln_beta': (0.0, 0.1),
     'L0_ffn_g1': (1.0, 0.6),
     'L0_ffn_g2': (1.0, 0.6)}
    factors = {'L0_xattn_WQ_b': 7.615,
     'L0_xattn_WK_b': 8.0,
     'L0_attn_Wq': 8.0,
     'L0_attn_Wk': 8.0,
     'L0_attn_dist_emb': 8.0,
     'L0_ffn_w_down': 7.126,
     'L0_ffn_wq': 8.0,
     'L0_ffn_wk': 8.0,
     'L0_ffn_wv': 6.993,
     'L0_ffn_w_up': 7.008,
     'L0_ffn_router_w': 3.789,
     'L0_ffn_w1': 3.39,
     'L0_ffn_w2': 3.319,
     'L0_ffn_w3': 3.314}
    for name, (base, spread) in spreads.items():
        noise = np.random.default_rng([zlib.crc32(name.encode()), seed]).standard_normal(out[name].shape)
        drawn = base * np.exp(spread * noise) if base else spread * noise
        out[name] = jnp.asarray(drawn.astype(out[name].dtype))
    for name, factor in factors.items():
        out[name] = (out[name] * factor).astype(out[name].dtype)
    return out
```

```python
from contextlib import ExitStack

import numpy as np

import concourse.bass as bass
from concourse import mybir

F32 = mybir.dt.float32
F32R = mybir.dt.float32r
F16 = mybir.dt.float16
BF16 = mybir.dt.bfloat16
I32 = mybir.dt.int32
U32 = mybir.dt.uint32
ALU = mybir.AluOpType
ACT = mybir.ActivationFunctionType
AX = mybir.AxisListType

P = 128
B, S, D = 8, 64, 512
T = B * S
NT = T // P
NK = D // P
KEYS = 1601
H = 16
NP = H // 2
DH = D // H
KC = 402
NC = 4
KPAD = NC * KC
NKT = -(-KEYS // P)
TAIL = KEYS - (NKT - 1) * P
SCALE = float(DH) ** -0.5
MASKED = 1e-9 / SCALE
LOWEST = -3.0e38
V_SCALE = 16.0
P_SCALE = 32768.0

C_IDENT = 0
C_HEAD32 = C_IDENT + P
C_HEAD16 = C_HEAD32 + 4
C_PARITY = C_HEAD16 + 8
C_COS = C_PARITY + 2
C_SIN = C_COS + 8
C_CAUSAL = C_SIN + 8
C_IOTA = C_CAUSAL + S
C_ALL = C_IOTA + 8


def constants():
    c = np.zeros((P, C_ALL), np.float32)
    p = np.arange(P)
    c[:, C_IDENT:C_IDENT + P] = np.eye(P)
    c[:, C_HEAD32:C_HEAD32 + 4] = p[:, None] // 32 == np.arange(4)
    c[:, C_HEAD16:C_HEAD16 + 8] = p[:, None] // 16 == np.arange(8)
    c[:, C_PARITY:C_PARITY + 2] = p[:, None] // S == np.arange(2)
    freq = (1.0 / np.float32(10000.0) ** (np.arange(0, 16, 2, dtype=np.float32) / 16)).astype(np.float32)
    ang = (p % S).astype(np.float32)[:, None] * freq
    c[:, C_COS:C_COS + 8] = np.cos(ang)
    c[:, C_SIN:C_SIN + 8] = np.sin(ang)
    c[:, C_CAUSAL:C_CAUSAL + S] = np.where(np.arange(S) <= (p % S)[:, None], 0.0, -1.0e30)
    c[:, C_IOTA:C_IOTA + 8] = np.arange(8)
    return c


class Chain:

    def __init__(self, eng, sem):
        self.eng, self.sem, self.n = eng, sem, 0

    def link(self, ins):
        self.n += 1
        ins.then_inc(self.sem, 1)
        self.eng.wait_ge(self.sem, self.n)


def dve_moments(nc, chain, x, stats, moments):
    for t in range(NT):
        last = nc.vector.bn_stats(stats[:, t, :], x[:, t, :])
        if t < NT - 1:
            last.then_inc(chain.sem, 1)
            chain.n += 1
    chain.link(last)
    for t in range(NT):
        last = nc.vector.bn_aggr(moments[:, t, :], stats[:, t, :])
        if t < NT - 1:
            last.then_inc(chain.sem, 1)
            chain.n += 1
    chain.link(last)


def query_stage(nc, io, keep):
    with ExitStack() as ctx:
        def sb(name, shape, dt=F32):
            return ctx.enter_context(nc.sbuf_tensor("q_" + name, shape, dt))

        def sem(name):
            return ctx.enter_context(nc.semaphore("q_" + name))

        x = sb("x", [P, NT, D])
        xn = sb("xn", [P, NT, D])
        xnT = sb("xnT", [P, NK, T])
        qT = sb("qT", [P, NK, T])
        wq = sb("wq", [P, NK, D])
        wk = sb("wk", [P, NK, D])
        wv = sb("wv", [P, NK, D])
        stats = sb("stats", [P, NT, 6])
        mom = sb("mom", [P, NT, 2])
        std = sb("std", [P, NT])
        rstd = sb("rstd", [P, NT])
        ps = ctx.enter_context(nc.psum_tensor("q_ps", [P, 8, 512], F32))
        const, bias = keep["const"], keep["bias"]
        x_in, wq_in, wk_in, wv_in, const_in = map(sem, ("x_in", "wq_in", "wk_in", "wv_in", "const_in"))
        dve_done, var_ready, std_ready, xn_ready = map(sem, ("dve_done", "var_ready", "std_ready", "xn_ready"))
        xnT_ps, xnT_ready, q_ps, q_ready, q_out = map(sem, ("xnT_ps", "xnT_ready", "q_psum", "q_ready", "q_out"))
        w_hi = sem("w_hi")
        with nc.Block() as block:

            @block.sync
            def _(sp):
                sp.dma_start(x[:], io["x"].rearrange("(t p) d -> p t d", p=P)).then_inc(x_in, 16)
                sp.dma_start(const[:], io["const"]).then_inc(const_in, 16)
                sp.dma_start(bias[:], io["bias_col"]).then_inc(const_in, 16)
                sp.dma_start(wq[:], io["wqT"].rearrange("(k p) n -> p k n", p=P)).then_inc(wq_in, 16)
                sp.dma_start(wk[:], io["wkT"].rearrange("(k p) n -> p k n", p=P)).then_inc(wk_in, 16)
                sp.dma_start(wv[:], io["wvT"].rearrange("(k p) n -> p k n", p=P)).then_inc(wv_in, 16)
                for c in range(NK):
                    sp.wait_ge(q_ready, c + 1)
                    sp.dma_start(io["qT"][:, c, :], qT[:, c, :]).then_inc(q_out, 16)
                sp.wait_ge(q_out, 16 * NK)

            @block.vector
            def _(dve):
                chain = Chain(dve, dve_done)
                dve.wait_ge(x_in, 16)
                dve_moments(nc, chain, x, stats, mom)
                nc.vector.tensor_scalar_add(std[:], mom[:, :, 1], 1e-5).then_inc(var_ready, 1)
                dve.wait_ge(std_ready, 1)
                chain.link(nc.vector.reciprocal(rstd[:], std[:]))
                for t in range(NT):
                    nc.vector.tensor_scalar(xn[:, t, :], x[:, t, :], mom[:, t, 0:1], rstd[:, t:t + 1],
                                            ALU.subtract, ALU.mult).then_inc(xn_ready, 1)
                for k in range(NK):
                    dve.wait_ge(xnT_ps, k + 1)
                    nc.vector.tensor_copy(xnT[:, k, :], ps[:, k, :]).then_inc(xnT_ready, 1)
                for n, (w, hl) in enumerate(((wk, keep["wk"]), (wv, keep["wv"]))):
                    dve.wait_ge(w_hi, n + 1)
                    chain.link(nc.vector.tensor_tensor(hl[:, 1], w[:], hl[:, 0].bitcast(F32), ALU.subtract))

            @block.scalar
            def _(act):
                act.wait_ge(var_ready, 1)
                nc.scalar.activation(std[:], std[:], ACT.Sqrt).then_inc(std_ready, 1)
                act.wait_ge(wk_in, 16)
                nc.scalar.activation(keep["wk"][:, 0], wk[:], ACT.Copy).then_inc(w_hi, 1)
                act.wait_ge(wv_in, 16)
                nc.scalar.activation(keep["wv"][:, 0], wv[:], ACT.Copy).then_inc(w_hi, 1)
                act.wait_ge(const_in, 32)
                for c in range(NK):
                    act.wait_ge(q_ps, c + 1)
                    nc.scalar.activation(qT[:, c, :], ps[:, 4 + c, :], ACT.Identity,
                                         bias=bias[:, BQ + c:BQ + c + 1]).then_inc(q_ready, 1)

            @block.tensor
            def _(pe):
                pe.wait_ge(const_in, 32)
                pe.wait_ge(xn_ready, NT)
                for k in range(NK):
                    for t in range(NT):
                        last = nc.tensor.transpose(ps[:, k, t * P:(t + 1) * P], xn[:, t, k * P:(k + 1) * P],
                                                   const[:, C_IDENT:C_IDENT + P])
                    last.then_inc(xnT_ps, 1)
                pe.wait_ge(wq_in, 16)
                pe.wait_ge(xnT_ready, NK)
                for c in range(NK):
                    for k in range(NK):
                        last = nc.tensor.matmul(ps[:, 4 + c, :], wq[:, k, c * P:(c + 1) * P], xnT[:, k, :],
                                                start=(k == 0), stop=(k == NK - 1))
                    last.then_inc(q_ps, 1)


BQ, BK, BV, B2Q, B2K = 0, 4, 8, 12, 16
B_ALL = 20


NG = -(-NKT // 4)


def transposed(p, before=()):
    out = [("PT", p, 0), ("PT", p, 1), ("PV", p, 0), ("PT", p, 2), ("PV", p, 1), ("PT", p, 3), ("PV", p, 2)]
    return out + list(before) + [("PV", p, 3), ("O", p)]


def batch_steps(more):
    def split(j):
        return [("C", j)] if more else []

    out = [("S", 0), ("M", 0), ("E", 0)] + [("V", kt) for kt in range(NKT)]
    out += [("S", 1), ("M", 1), ("E", 1)] + [("K", 1, j) for j in range(NC)]
    out += transposed(0, [("S", 2)]) + transposed(1, [("M", 2), ("E", 2), ("S", 3)])
    out += [("M", 3), ("E", 3)] + [("K", 2, j) for j in range(NC)]
    out += transposed(2, [("S", 4)]) + transposed(3, [("M", 4), ("E", 4), ("S", 5)])
    out += [("M", 5), ("E", 5)] + [("K", 3, 0), ("K", 3, 1), ("K", 3, 2)] + split(0) + [("K", 3, 3)] + split(1)
    out += transposed(4, [("S", 6)]) + split(2) + transposed(5, [("M", 6), ("E", 6), ("S", 7)]) + split(3)
    out += [("M", 7), ("E", 7)]
    if more:
        out += [("K", 0, j) for j in range(NC)]
    return out + transposed(6) + transposed(7)


RING = 3
FIRST_JOBS = NC


def job_index(more):
    return {s: n for n, s in enumerate(s for s in batch_steps(more) if s[0] in ("V", "K", "PT"))}


JOB_INDEX = {more: job_index(more) for more in (True, False)}
NJ = len(JOB_INDEX[True])


def cross_attention(nc, io, keep):
    with ExitStack() as ctx:
        def sb(name, shape, dt=F32):
            return ctx.enter_context(nc.sbuf_tensor("x_" + name, shape, dt))

        def sem(name):
            return ctx.enter_context(nc.semaphore("x_" + name))

        SLOTS = 3
        ctx_raw = sb("ctx_raw", [P, SLOTS, NK, KC])
        ctx_s = sb("ctx_s", [P, 2, NK, KPAD], F32R)
        kT = sb("kT", [P, 2, KPAD], F32R)
        v = sb("v", [P, 2, NKT, D], F16)
        prob = sb("prob", [P, 2, KPAD])
        probT = sb("probT", [P, 2, 2, NKT, P], F16)
        q_raw = sb("q_raw", [P, NK, S])
        q_s = sb("q_s", [P, 2, H, S], F32R)
        mask_raw = sb("mask_raw", [P, KPAD], I32)
        mask01 = sb("mask01", [P, KPAD], BF16)
        mask_add = sb("mask_add", [P, KPAD])
        out_b = sb("out_b", [S, D])
        biggest = sb("biggest", [P, 2])
        negmax = sb("negmax", [P, 2])
        total = sb("total", [P, 2])
        rtotal = sb("rtotal", [P, 2])
        ps_s = ctx.enter_context(nc.psum_tensor("x_ps_s", [P, NC, 512], F32))
        ring = ctx.enter_context(nc.psum_tensor("x_ring", [P, RING, 512], F32))
        ps_o = ctx.enter_context(nc.psum_tensor("x_ps_o", [P, 512], F32))
        ctx_in = [sem(f"ctx_in{i}") for i in range(SLOTS)]
        q_in, mask_in, out_stored, out_free = map(sem, ("q_in", "mask_in", "out_stored", "out_free"))
        mask_ready, q_hi, q_ready, ctx_hi, ctx_ready = map(sem, ("mask_ready", "q_hi", "q_ready", "ctx_hi", "ctx_ready"))
        scores, scores_read, max_done, max_ready, exp_done = map(
            sem, ("scores", "scores_read", "max_done", "max_ready", "exp_done"))
        job_done, job_hi, job_lo = map(sem, ("job_done", "job_hi", "job_lo"))
        o_done, o_read, rtotal_ready, total_scaled, mask_used, pads = map(
            sem, ("o_done", "o_read", "rtotal_ready", "total_scaled", "mask_used", "pads"))
        const, bias = keep["const"], keep["bias"]
        wk, wv = keep["wk"], keep["wv"]
        ident = const[:, C_IDENT:C_IDENT + P]
        ctxT = io["ctxT"].rearrange("b (k p) s -> b p k s", p=P)

        def jobs_before(b, step, more=True):
            return FIRST_JOBS + b * NJ + JOB_INDEX[more][step]

        def piece(b, j):
            return b * NC + j

        def tile_keys(kt):
            return P if kt < NKT - 1 else TAIL

        def group(g):
            return range(4 * g, min(4 * g + 4, NKT))

        with nc.Block() as block:

            def batches(eng, first, body):
                first()
                with eng.Fori(0, B - 1) as b:
                    body(b, True)
                body(B - 1, False)

            @block.sync
            def _(sp):
                def context(b, j, slot):
                    sp.dma_start(ctx_raw[:, slot], ctxT[b, :, :, j * KC:(j + 1) * KC]).then_inc(ctx_in[slot], 16)

                def small(b):
                    sp.dma_start(q_raw[:], io["qT"][:, :, bass.ds(b * S, S)]).then_inc(q_in, 16)

                def mask(b):
                    for half in range(2):
                        sp.dma_start(mask_raw[half * S:(half + 1) * S, :], io["mask"][b, :, :]).then_inc(mask_in, 16)

                small(0)
                mask(0)
                sp.sem_inc(out_free, 1)
                for j in range(NC):
                    if j >= SLOTS:
                        sp.wait_ge(ctx_ready, piece(0, j - SLOTS) + 1)
                    context(0, j, j % SLOTS)
                with sp.Fori(0, B - 1) as b:
                    sp.wait_ge(ctx_ready, piece(b, NC - 1) + 1)
                    for j in range(SLOTS):
                        context(b + 1, j, j)
                    sp.wait_ge(q_ready, b + 1)
                    small(b + 1)
                    sp.wait_ge(mask_ready, 2 * b + 2)
                    mask(b + 1)
                    sp.wait_ge(ctx_ready, piece(b + 1, NC - 1 - SLOTS) + 1)
                    context(b + 1, NC - 1, 0)
                    sp.wait_ge(o_read, 2 * NP * b + 2 * NP)
                    sp.dma_start(io["attn"][b, :, :], out_b[:]).then_inc(out_stored, 16)
                    sp.wait_ge(out_stored, 16 * b + 16)
                    sp.sem_inc(out_free, 1)
                sp.wait_ge(o_read, 2 * NP * B)
                sp.dma_start(io["attn"][B - 1, :, :], out_b[:]).then_inc(out_stored, 16)
                sp.wait_ge(out_stored, 16 * B)

            @block.gpsimd
            def _(pool):
                def masks(b):
                    pool.wait_ge(mask_in, 32 * b + 32)
                    if b:
                        pool.wait_ge(mask_used, NP * b)
                    nc.gpsimd.tensor_scalar(mask01[:], mask_raw[:], 0, 0, ALU.is_equal, ALU.is_equal).then_inc(mask_ready, 1)
                    nc.gpsimd.tensor_scalar(mask_add[:], mask_raw[:], 0, MASKED, ALU.is_equal,
                                            ALU.mult).then_inc(mask_ready, 1)

                for b in range(B):
                    masks(b)

            def slot_of(j):
                return j % SLOTS

            def ctx_landed(eng, b, j):
                if slot_of(j) == 0:
                    eng.wait_ge(ctx_in[0], b * 32 + (16 if j == 0 else 32))
                else:
                    eng.wait_ge(ctx_in[slot_of(j)], b * 16 + 16)

            @block.scalar
            def _(act):
                def queries(b):
                    act.wait_ge(q_in, 16 * b + 16)
                    for h in range(4):
                        nc.scalar.activation(q_s[:, 0, h::4, :], q_raw[:], ACT.Copy,
                                             scale=const[:, C_HEAD32 + h:C_HEAD32 + h + 1]).then_inc(q_hi, 1)

                def context(b, j):
                    ctx_landed(act, b, j)
                    nc.scalar.activation(ctx_s[:, 0, :, j * KC:(j + 1) * KC], ctx_raw[:, slot_of(j)],
                                         ACT.Copy).then_inc(ctx_hi, 1)

                def keys(bank, c, j):
                    nc.scalar.activation(kT[:, 0, j * KC:(j + 1) * KC], bank[:, 0:KC], ACT.Identity,
                                         bias=bias[:, BK + c:BK + c + 1]).then_inc(job_hi, 1)

                def first():
                    queries(0)
                    for j in range(NC):
                        context(0, j)
                    for j in range(NC):
                        act.wait_ge(job_done, j + 1)
                        keys(ring[:, j % RING], 0, j)

                def body(b, more):
                    for s in batch_steps(more):
                        if s in JOB_INDEX[more]:
                            act.wait_ge(job_done, jobs_before(b, s, more) + 1)
                            bank = ring[:, JOB_INDEX[more][s] % RING]
                        if s[0] == "K":
                            keys(bank, s[1], s[2])
                        elif s[0] == "V":
                            n = tile_keys(s[1])
                            nc.scalar.activation(v[0:n, 0, s[1], :], bank[0:n, :], ACT.Copy,
                                                 scale=V_SCALE).then_inc(job_hi, 1)
                        elif s[0] == "PT":
                            _, p, g = s
                            n = tile_keys(group(g)[0]) if len(group(g)) == 1 else P
                            w = P * len(group(g))
                            nc.scalar.activation(probT[0:n, p % 2, 0, 4 * g:4 * g + len(group(g)), :],
                                                 bank[0:n, 0:w].rearrange("p (a c) -> p a c", c=P), ACT.Copy,
                                                 scale=P_SCALE).then_inc(job_hi, 1)
                        elif s[0] == "C":
                            act.wait_ge(job_done, jobs_before(b, ("K", NK - 1, s[1])) + 1)
                            context(b + 1, s[1])
                        elif s[0] == "E":
                            p = s[1]
                            act.wait_ge(max_ready, NP * b + p + 1)
                            if p >= 2:
                                act.wait_ge(rtotal_ready, NP * b + p - 1)
                            nc.scalar.activation(prob[:, p % 2, :], prob[:, p % 2, :], ACT.Exp,
                                                 bias=negmax[:, p % 2:p % 2 + 1], scale=SCALE,
                                                 accum_out=total[:, p % 2:p % 2 + 1]).then_inc(exp_done, 1)
                            if p == NP - 1 and more:
                                act.wait_ge(scores, NP * b + NP)
                                queries(b + 1)
                        elif s[0] == "O":
                            p = s[1]
                            act.wait_ge(o_done, NP * b + p + 1)
                            act.wait_ge(rtotal_ready, NP * b + p + 1)
                            if p == 0:
                                act.wait_ge(out_free, b + 1)
                            for h in range(2):
                                nc.scalar.activation(
                                    out_b[:, (2 * p + h) * DH:(2 * p + h + 1) * DH],
                                    ps_o[h * S:(h + 1) * S, (p % 2) * 64 + h * DH:(p % 2) * 64 + (h + 1) * DH],
                                    ACT.Copy, scale=rtotal[h * S:(h + 1) * S, p % 2:p % 2 + 1]).then_inc(o_read, 1)

                batches(act, first, body)

            @block.vector
            def _(dve):
                def low(out, psum, hi, scale=None):
                    if scale is None:
                        return nc.vector.tensor_tensor(out, psum, hi, ALU.subtract)
                    op = ALU.add if not isinstance(scale, float) else ALU.mult
                    return nc.vector.scalar_tensor_tensor(out=out, in0=psum, scalar=scale, in1=hi, op0=op,
                                                          op1=ALU.subtract)

                def queries(b):
                    for h in range(4):
                        dve.wait_ge(q_hi, 4 * b + h + 1)
                        last = nc.vector.scalar_tensor_tensor(
                            out=q_s[:, 1, h::4, :], in0=q_raw[:], scalar=const[:, C_HEAD32 + h:C_HEAD32 + h + 1],
                            in1=q_s[:, 0, h::4, :].bitcast(F32), op0=ALU.mult, op1=ALU.subtract)
                    last.then_inc(q_ready, 1)

                def context(b, j):
                    dve.wait_ge(ctx_hi, piece(b, j) + 1)
                    cols = slice(j * KC, (j + 1) * KC)
                    low(ctx_s[:, 1, :, cols], ctx_raw[:, slot_of(j)], ctx_s[:, 0, :, cols].bitcast(F32)).then_inc(ctx_ready, 1)

                def keys(bank, c, j):
                    cols = slice(j * KC, (j + 1) * KC)
                    low(kT[:, 1, cols], bank[:, 0:KC], kT[:, 0, cols].bitcast(F32),
                        bias[:, BK + c:BK + c + 1]).then_inc(job_lo, 1)

                def first():
                    queries(0)
                    for j in range(NC):
                        context(0, j)
                    for j in range(NC):
                        dve.wait_ge(job_hi, j + 1)
                        keys(ring[:, j % RING], 0, j)

                def body(b, more):
                    for s in batch_steps(more):
                        if s in JOB_INDEX[more]:
                            dve.wait_ge(job_hi, jobs_before(b, s, more) + 1)
                            bank = ring[:, JOB_INDEX[more][s] % RING]
                        if s[0] == "K":
                            keys(bank, s[1], s[2])
                        elif s[0] == "V":
                            n = tile_keys(s[1])
                            low(v[0:n, 1, s[1], :], bank[0:n, :], v[0:n, 0, s[1], :], V_SCALE).then_inc(job_lo, 1)
                        elif s[0] == "PT":
                            _, p, g = s
                            n = tile_keys(group(g)[0]) if len(group(g)) == 1 else P
                            cols = slice(4 * g, 4 * g + len(group(g)))
                            low(probT[0:n, p % 2, 1, cols, :],
                                bank[0:n, 0:P * len(group(g))].rearrange("p (a c) -> p a c", c=P),
                                probT[0:n, p % 2, 0, cols, :], P_SCALE).then_inc(job_lo, 1)
                            if g == 0:
                                dve.wait_ge(exp_done, NP * b + p + 1)
                                k = p % 2
                                if p >= 2:
                                    dve.wait_ge(o_read, 2 * (NP * b + p - 1))
                                nc.vector.tensor_scalar_mul(rtotal[:, k:k + 1], total[:, k:k + 1],
                                                            V_SCALE * P_SCALE).then_inc(total_scaled, 1)
                                dve.wait_ge(total_scaled, NP * b + p + 1)
                                nc.vector.reciprocal(rtotal[:, k:k + 1], rtotal[:, k:k + 1]).then_inc(rtotal_ready, 1)
                        elif s[0] == "C":
                            context(b + 1, s[1])
                        elif s[0] == "S":
                            p = s[1]
                            dve.wait_ge(scores, NP * b + p + 1)
                            if p == 0:
                                dve.wait_ge(mask_ready, 2 * b + 2)
                            nc.vector.tensor_tensor(prob[:, p % 2, :].rearrange("p (c n) -> p c n", n=KC),
                                                    ps_s[:, :, 0:KC],
                                                    mask01[:].rearrange("p (c n) -> p c n", n=KC),
                                                    ALU.mult).then_inc(scores_read, 1)
                        elif s[0] == "M":
                            p = s[1]
                            k = p % 2
                            dve.wait_ge(scores_read, NP * b + p + 1)
                            nc.vector.tensor_tensor(prob[:, k, :], prob[:, k, :], mask_add[:],
                                                    ALU.add).then_inc(mask_used, 1)
                            dve.wait_ge(mask_used, NP * b + p + 1)
                            nc.vector.memset(prob[:, k, KEYS:KPAD], LOWEST).then_inc(pads, 1)
                            nc.vector.reduce_max(biggest[:, k:k + 1], prob[:, k, 0:KEYS], AX.X).then_inc(max_done, 1)
                            dve.wait_ge(pads, NP * b + p + 1)
                            dve.wait_ge(max_done, NP * b + p + 1)
                            if p >= 2:
                                dve.wait_ge(exp_done, NP * b + p - 1)
                            nc.vector.tensor_scalar_mul(negmax[:, k:k + 1], biggest[:, k:k + 1],
                                                        -SCALE).then_inc(max_ready, 1)
                        elif s[0] == "E" and s[1] == NP - 1 and more:
                            queries(b + 1)

                batches(dve, first, body)

            @block.tensor
            def _(pe):
                def three(out, a, b, start, stop):
                    for n, (i, j) in enumerate(((1, 0), (0, 1), (0, 0))):
                        last = nc.tensor.matmul(out, a(i), b(j), start=(start and n == 0), stop=(stop and n == 2))
                    return last

                def keys(bank, c, j):
                    for k in range(NK):
                        last = three(bank[:, 0:KC], lambda i: wk[:, i, k, c * P:(c + 1) * P],
                                     lambda i: ctx_s[:, i, k, j * KC:(j + 1) * KC], k == 0, k == NK - 1)
                    last.then_inc(job_done, 1)

                def first():
                    for j in range(NC):
                        pe.wait_ge(ctx_ready, piece(0, j) + 1)
                        if j >= RING:
                            pe.wait_ge(job_lo, j - RING + 1)
                        keys(ring[:, j % RING], 0, j)

                def body(b, more):
                    for s in batch_steps(more):
                        if s in JOB_INDEX[more]:
                            n = JOB_INDEX[more][s]
                            pe.wait_ge(job_lo, FIRST_JOBS + b * NJ + max(n - RING + 1, 0))
                            bank = ring[:, n % RING]
                        if s[0] == "K":
                            if s[1] == 0:
                                pe.wait_ge(ctx_ready, piece(b + 1, s[2]) + 1)
                            keys(bank, s[1], s[2])
                        elif s[0] == "V":
                            n = tile_keys(s[1])
                            for k in range(NK):
                                last = three(bank[0:n, :], lambda i: ctx_s[:, i, k, s[1] * P:s[1] * P + n],
                                             lambda i: wv[:, i, k, :], k == 0, k == NK - 1)
                            last.then_inc(job_done, 1)
                        elif s[0] == "S":
                            p = s[1]
                            if p == 0:
                                pe.wait_ge(q_ready, b + 1)
                            pe.wait_ge(job_lo, jobs_before(b, ("K", p // 2, NC - 1), more) + 1
                                       if p > 1 else FIRST_JOBS + b * NJ)
                            if p:
                                pe.wait_ge(scores_read, NP * b + p)
                            for j in range(NC):
                                last = three(ps_s[:, j, 0:KC], lambda i: q_s[:, i, 2 * p:2 * p + 2, :].rearrange("p h s -> p (h s)"),
                                             lambda i: kT[:, i, j * KC:(j + 1) * KC], True, True)
                            last.then_inc(scores, 1)
                        elif s[0] == "PT":
                            _, p, g = s
                            pe.wait_ge(exp_done, NP * b + p + 1)
                            for a, kt in enumerate(group(g)):
                                n = tile_keys(kt)
                                last = nc.tensor.transpose(bank[0:n, a * P:(a + 1) * P],
                                                           prob[:, p % 2, kt * P:kt * P + n], ident)
                            last.then_inc(job_done, 1)
                        elif s[0] == "PV":
                            _, p, g = s
                            pe.wait_ge(job_lo, jobs_before(b, ("PT", p, g), more) + 1)
                            if g == 0 and p:
                                pe.wait_ge(o_read, 2 * (NP * b + p))
                            for kt in group(g):
                                n = tile_keys(kt)
                                last = three(ps_o[:, (p % 2) * 64:(p % 2) * 64 + 64],
                                             lambda i: probT[0:n, p % 2, i, kt, :],
                                             lambda i: v[0:n, i, kt, p * 64:(p + 1) * 64],
                                             kt == 0, kt == NKT - 1)
                            if g == NG - 1:
                                last.then_inc(o_done, 1)

                batches(pe, first, body)




class Norm:

    def __init__(self, nc, ctx, name):
        def sb(tile, shape):
            return ctx.enter_context(nc.sbuf_tensor(f"{name}_{tile}", shape, F32))

        self.stats, self.mom = sb("stats", [P, NT, 6]), sb("mom", [P, NT, 2])
        self.std, self.root, self.rstd, self.square = (sb(t, [P, NT]) for t in ("std", "root", "rstd", "square"))
        self.var_ready = ctx.enter_context(nc.semaphore(name + "_var_ready"))
        self.root_ready = ctx.enter_context(nc.semaphore(name + "_root_ready"))

    def vector(self, nc, dve, chain, x, eps, about_zero=False):
        dve_moments(nc, chain, x, self.stats, self.mom)
        if about_zero:
            chain.link(nc.vector.tensor_tensor(self.square[:], self.mom[:, :, 0], self.mom[:, :, 0], ALU.mult))
            nc.vector.scalar_tensor_tensor(out=self.std[:], in0=self.square[:], scalar=eps, in1=self.mom[:, :, 1],
                                           op0=ALU.add, op1=ALU.add).then_inc(self.var_ready, 1)
        else:
            nc.vector.tensor_scalar_add(self.std[:], self.mom[:, :, 1], eps).then_inc(self.var_ready, 1)
        dve.wait_ge(self.root_ready, 1)
        chain.link(nc.vector.reciprocal(self.rstd[:], self.root[:]))

    def scalar(self, nc, act):
        act.wait_ge(self.var_ready, 1)
        nc.scalar.activation(self.root[:], self.std[:], ACT.Sqrt).then_inc(self.root_ready, 1)


def pe_transposes(nc, src, out, k, ident):
    for t in range(NT):
        last = nc.tensor.transpose(out[:, t * P:(t + 1) * P], src[:, t, k * P:(k + 1) * P], ident)
    return last


def pe_product(nc, out, lhsT, rhs, chunks):
    for k in range(chunks):
        last = nc.tensor.matmul(out, lhsT(k), rhs(k), start=(k == 0), stop=(k == chunks - 1))
    return last


R_BO, R_B2V, R_B2O, R_GAMMA, R_BETA, R_G1, R_G2 = range(7)
R_ALL = 7


def project_stage(nc, io, keep):
    with ExitStack() as ctx:
        def sb(name, shape, dt=F32):
            return ctx.enter_context(nc.sbuf_tensor("p_" + name, shape, dt))

        def sem(name):
            return ctx.enter_context(nc.semaphore("p_" + name))

        x, attn = sb("x", [P, NT, D]), sb("attn", [P, NT, D])
        attnT, hT, qT = sb("attnT", [P, NK, T]), sb("hT", [P, NK, T]), sb("qT", [P, NK, T])
        wo, w2q, w2k, w2v = (sb(n, [P, NK, D]) for n in ("wo", "w2q", "w2k", "w2v"))
        v = attn
        norm = Norm(nc, ctx, "p_norm")
        ps = ctx.enter_context(nc.psum_tensor("p_ps", [P, 8, 512], F32))
        const, bias, rows = keep["const"], keep["bias"], keep["rows"]
        x1, h, kT, qz, kz, vz = (keep[n] for n in ("x1", "h", "kT", "qz", "kz", "vz"))
        ident = const[:, C_IDENT:C_IDENT + P]
        attn_in, x_in, rows_in, weights_in = map(sem, ("attn_in", "x_in", "rows_in", "weights_in"))
        dve_done, aT_ps, aT_ready, x1_ps, h_ready = map(sem, ("dve_done", "aT_psum", "aT_ready", "x1_psum", "h_ready"))
        hT_ps, hT_ready, k_ps, k_ready, q_ps, q_ready, v_ps = map(
            sem, ("hT_psum", "hT_ready", "k_psum", "k_ready", "q_psum", "q_ready", "v_psum"))
        with nc.Block() as block:

            @block.sync
            def _(sp):
                sp.dma_start(attn[:], io["attn"].rearrange("(t two) s d -> (two s) t d", two=2)).then_inc(attn_in, 16)
                for w, name in ((wo, "woT"), (w2k, "w2k"), (w2q, "w2q"), (w2v, "w2v")):
                    sp.dma_start(w[:], io[name].rearrange("(k p) n -> p k n", p=P)).then_inc(weights_in, 16)

            @block.gpsimd
            def _(pool):
                pool.dma_start(x[:], io["x"].rearrange("(t p) d -> p t d", p=P)).then_inc(x_in, 16)
                pool.dma_start(rows[:], io["bias_row"].partition_broadcast(P)).then_inc(rows_in, 16)

            @block.tensor
            def _(pe):
                pe.wait_ge(attn_in, 16)
                for k in range(NK):
                    pe_transposes(nc, attn, ps[:, k, :], k, ident).then_inc(aT_ps, 1)
                pe.wait_ge(weights_in, 64)
                pe.wait_ge(aT_ready, NK)
                for t in range(NT):
                    pe_product(nc, ps[:, 4 + t, :], lambda k: attnT[:, k, t * P:(t + 1) * P],
                               lambda k: wo[:, k, :], NK).then_inc(x1_ps, 1)
                pe.wait_ge(h_ready, NT)
                for k in range(NK):
                    pe_transposes(nc, h, ps[:, k, :], k, ident).then_inc(hT_ps, 1)
                pe.wait_ge(hT_ready, NK)
                for c in range(NK):
                    pe_product(nc, ps[:, 4 + c, :], lambda k: w2k[:, k, c * P:(c + 1) * P],
                               lambda k: hT[:, k, :], NK).then_inc(k_ps, 1)
                for c in range(NK):
                    pe_product(nc, ps[:, c, :], lambda k: w2q[:, k, c * P:(c + 1) * P],
                               lambda k: hT[:, k, :], NK).then_inc(q_ps, 1)
                pe.wait_ge(k_ready, NK)
                for t in range(NT):
                    pe_product(nc, ps[:, 4 + t, :], lambda k: hT[:, k, t * P:(t + 1) * P],
                               lambda k: w2v[:, k, :], NK).then_inc(v_ps, 1)

            @block.scalar
            def _(act):
                for k in range(NK):
                    act.wait_ge(aT_ps, k + 1)
                    nc.scalar.activation(attnT[:, k, :], ps[:, k, :], ACT.Identity,
                                         bias=bias[:, BV + k:BV + k + 1]).then_inc(aT_ready, 1)
                norm.scalar(nc, act)
                for c in range(NK):
                    act.wait_ge(k_ps, c + 1)
                    nc.scalar.activation(kT[:, c, :], ps[:, 4 + c, :], ACT.Identity,
                                         bias=bias[:, B2K + c:B2K + c + 1]).then_inc(k_ready, 1)
                for c in range(NK):
                    act.wait_ge(q_ps, c + 1)
                    nc.scalar.activation(qT[:, c, :], ps[:, c, :], ACT.Identity,
                                         bias=bias[:, B2Q + c:B2Q + c + 1]).then_inc(q_ready, 1)

            @block.vector
            def _(dve):
                chain = Chain(dve, dve_done)
                dve.wait_ge(x_in, 16)
                dve.wait_ge(rows_in, 16)
                chain.link(nc.vector.tensor_tensor(
                    x1[:], x[:], rows[:, R_BO, :].unsqueeze(1).broadcast_to([P, NT, D]), ALU.add))
                for t in range(NT):
                    dve.wait_ge(x1_ps, t + 1)
                    chain.link(nc.vector.tensor_tensor(x1[:, t, :], x1[:, t, :], ps[:, 4 + t, :], ALU.add))
                norm.vector(nc, dve, chain, x1, 1e-5)
                for t in range(NT):
                    nc.vector.tensor_scalar(h[:, t, :], x1[:, t, :], norm.mom[:, t, 0:1], norm.rstd[:, t:t + 1],
                                            ALU.subtract, ALU.mult).then_inc(h_ready, 1)
                for k in range(NK):
                    dve.wait_ge(hT_ps, k + 1)
                    nc.vector.tensor_copy(hT[:, k, :], ps[:, k, :]).then_inc(hT_ready, 1)
                for z, src, ready in ((kz, kT, k_ready), (qz, qT, q_ready)):
                    for c in range(NK):
                        dve.wait_ge(ready, c + 1)
                        for j in range(4):
                            nc.vector.tensor_scalar_mul(z[:, :, 4 * c + j, :], src[:, c, :].rearrange("p (b s) -> p b s", s=S),
                                                        const[:, C_HEAD32 + j:C_HEAD32 + j + 1])
                for t in range(NT):
                    dve.wait_ge(v_ps, t + 1)
                    chain.link(nc.vector.tensor_tensor(v[:, t, :], ps[:, 4 + t, :], rows[:, R_B2V, :], ALU.add))
                for two in range(2):
                    nc.vector.tensor_scalar_mul(vz[:, two], v[:], const[:, C_PARITY + two:C_PARITY + two + 1])


EMB_BASE = D - S


def relative_stage(nc, io, keep):
    with ExitStack() as ctx:
        def sb(name, shape, dt=F32):
            return ctx.enter_context(nc.sbuf_tensor("r_" + name, shape, dt))

        def sem(name):
            return ctx.enter_context(nc.semaphore("r_" + name))

        emb = sb("emb", [P, 2, P])
        SLOTS = 8
        stage = sb("stage", [P, SLOTS, 512])
        ps = ctx.enter_context(nc.psum_tensor("r_ps", [P, 8, 512], F32))
        z, skewed, scratch = (keep["qz"], keep["kz"]), (keep["q_rel"], keep["k_rel"]), (io["q_rel"], io["k_rel"])
        emb_in, rel_ps, act_staged, dve_staged, loaded = map(
            sem, ("emb_in", "rel_psum", "act_staged", "dve_staged", "loaded"))
        stored = [sem(f"stored{i}") for i in range(SLOTS)]
        JOBS = 2 * NP * B // 4
        with nc.Block() as block:

            @block.sync
            def _(sp):
                sp.dma_start(emb[:, 0, :], io["emb_rev"]).then_inc(emb_in, 16)
                sp.dma_start(emb[:, 1, :], io["emb_fwd"]).then_inc(emb_in, 16)
                for n in range(JOBS):
                    side, m = divmod(n, JOBS // 2)
                    sp.wait_ge(act_staged if n % 2 == 0 else dve_staged, n // 2 + 1)
                    sp.dma_start(scratch[side][4 * m:4 * m + 4].rearrange("i p j -> p i j"),
                                 stage[:, n % SLOTS].rearrange("p (i j) -> p i j", j=P)).then_inc(stored[n % SLOTS], 16)
                    if m == JOBS // 2 - 1:
                        for slot in range(SLOTS):
                            sp.wait_ge(stored[slot], 16 * ((n + 1) // SLOTS))
                        for half in range(2):
                            src = bass.AP(tensor=scratch[side].tensor, offset=half * S * P + S - 1,
                                          ap=[[P - 1, S], [P * P, NP * B], [1, S]])
                            sp.dma_start(skewed[side][half * S:(half + 1) * S], src).then_inc(loaded, 16)
                sp.wait_ge(loaded, 64)

            @block.tensor
            def _(pe):
                pe.wait_ge(emb_in, 32)
                for n in range(JOBS):
                    side, m = divmod(n, JOBS // 2)
                    if n >= 8:
                        pe.wait_ge(act_staged if n % 2 == 0 else dve_staged, (n - 8) // 2 + 1)
                    for a in range(4):
                        b, p = divmod(4 * m + a, NP)
                        last = nc.tensor.matmul(ps[:, n % 8, a * P:(a + 1) * P],
                                                z[side][:, b, 2 * p:2 * p + 2, :].rearrange("p h s -> p (h s)"), emb[:, side, :],
                                                start=True, stop=True)
                    last.then_inc(rel_ps, 1)

            def staged(eng, copy, parity, done):
                for n in range(parity, JOBS, 2):
                    eng.wait_ge(rel_ps, n + 1)
                    if n >= SLOTS:
                        eng.wait_ge(stored[n % SLOTS], 16 * (n // SLOTS))
                    copy(stage[:, n % SLOTS], ps[:, n % 8]).then_inc(done, 1)

            @block.scalar
            def _(act):
                staged(act, nc.scalar.copy, 0, act_staged)

            @block.vector
            def _(dve):
                staged(dve, nc.vector.tensor_copy, 1, dve_staged)


def attention(nc, ctx, name, keep, dk, scale, rel):
    def sb(n, shape, dt=F32):
        return ctx.enter_context(nc.sbuf_tensor(f"{name}_{n}", shape, dt))

    def sem(n):
        return ctx.enter_context(nc.semaphore(f"{name}_{n}"))

    prob = keep["prob"]
    probT = keep["probT"]
    biggest, total, rtotal = (sb(n, [P, NT, 2, NP]) for n in ("biggest", "total", "rtotal"))
    ps = ctx.enter_context(nc.psum_tensor(name + "_ps", [P, 8, 512], F32))
    chain_done, s_ps, s_read, x_ready, exp_ready = map(sem, ("chain", "scores", "s_read", "shifted", "exp"))
    t_ps, t_read, o_ps, out_ready = map(sem, ("t_psum", "t_read", "o_psum", "out_ready"))
    qz, kT, vz, const, out = keep["qz"], keep["kT"], keep["vz"], keep["const"], keep["out"]
    ident = const[:, C_IDENT:C_IDENT + P]
    in_chunk = P // dk

    def tensor(pe):
        def scores(b):
            if b >= 4:
                pe.wait_ge(s_read, b - 3)
            for p in range(NP):
                for two in range(2):
                    h = 2 * p + two
                    dst = ps[two * S:(two + 1) * S, b % 4, p * S:(p + 1) * S]
                    last = nc.tensor.matmul(dst, qz[:, b, h, :], kT[:, h // in_chunk, b * S:(b + 1) * S],
                                            start=True, stop=not rel)
                    if rel:
                        last = nc.tensor.matmul(dst, keep["k_rel"][:, b * NP + p, :],
                                                ident[:, two * S:(two + 1) * S], start=False, stop=True)
            last.then_inc(s_ps, 1)

        def outputs(t):
            pe.wait_ge(exp_ready, 2 * t + 2)
            for g in range(2):
                n = 2 * t + g
                if n >= 2:
                    pe.wait_ge(t_read, n - 1)
                for a in range(4):
                    last = nc.tensor.transpose(ps[:, 4 + g, a * P:(a + 1) * P],
                                               prob[:, t, 4 * g + a].rearrange("p b s -> p (b s)"), ident)
                last.then_inc(t_ps, 1)
            pe.wait_ge(t_read, 2 * t + 2)
            if t >= 2:
                pe.wait_ge(out_ready, 4 * (t - 1))
            for p in range(NP):
                for two in range(2):
                    h = 2 * p + two
                    last = nc.tensor.matmul(
                        ps[two * S:(two + 1) * S, 6 + t % 2, p * 2 * dk:(p + 1) * 2 * dk],
                        probT[:, t, p, two * S:(two + 1) * S], vz[:, :, t, h * dk:(h + 1) * dk],
                        start=True, stop=True)
            last.then_inc(o_ps, 1)

        for b in range(B):
            scores(b)
            if b >= 3 and b % 2:
                outputs(b // 2 - 1)
        outputs(NT - 1)

    def vector(dve):
        chain = Chain(dve, chain_done)

        def soft(b):
            t, two = divmod(b, 2)
            x = prob[:, t, :, two, :]
            dve.wait_ge(s_ps, b + 1)
            if rel:
                add = keep["q_rel"][:, b * NP:(b + 1) * NP, :]
            else:
                add = const[:, C_CAUSAL:C_CAUSAL + S].unsqueeze(1).broadcast_to([P, NP, S])
            ins = nc.vector.tensor_tensor(x, ps[:, b % 4].rearrange("p (a s) -> p a s", s=S), add, ALU.add)
            ins.then_inc(s_read, 1)
            dve.wait_ge(s_read, b + 1)
            big = biggest[:, t, two, :]
            chain.link(nc.vector.reduce_max(big, x, AX.X))
            nc.vector.tensor_tensor(x, x, big.unsqueeze(2).broadcast_to([P, NP, S]), ALU.subtract).then_inc(x_ready, 1)

        def sums(b):
            t, two = divmod(b, 2)
            dve.wait_ge(exp_ready, b + 1)
            chain.link(nc.vector.reduce_sum(total[:, t, two, :], prob[:, t, :, two, :], AX.X))
            chain.link(nc.vector.reciprocal(rtotal[:, t, two, :], total[:, t, two, :]))

        def outputs(t):
            dve.wait_ge(o_ps, t + 1)
            o = ps[:, 6 + t % 2, 0:NP * 2 * dk].rearrange("p (a b d) -> p a b d", b=2, d=dk)
            dst = out[:, t, :].rearrange("p (a h d) -> p a h d", h=2, d=dk)
            for h in range(2):
                for b in range(2):
                    nc.vector.tensor_tensor(
                        dst[b * S:(b + 1) * S, :, h, :], o[h * S:(h + 1) * S, :, b, :],
                        rtotal[h * S:(h + 1) * S, t, b, :].unsqueeze(2).broadcast_to([S, NP, dk]),
                        ALU.mult).then_inc(out_ready, 1)

        for b in range(B):
            soft(b)
            if b >= 1:
                sums(b - 1)
            if b >= 5 and b % 2:
                outputs(b // 2 - 2)
        sums(B - 1)
        outputs(NT - 2)
        outputs(NT - 1)

    def scalar(act):
        def exps(b):
            t, two = divmod(b, 2)
            act.wait_ge(x_ready, b + 1)
            nc.scalar.activation(prob[:, t, :, two, :], prob[:, t, :, two, :], ACT.Exp,
                                 scale=scale).then_inc(exp_ready, 1)

        def copies(t):
            for g in range(2):
                act.wait_ge(t_ps, 2 * t + g + 1)
                nc.scalar.activation(probT[:, t, 4 * g:4 * g + 4, :],
                                     ps[:, 4 + g, :].rearrange("p (a q) -> p a q", q=P), ACT.Copy).then_inc(t_read, 1)

        for b in range(B):
            exps(b)
            if b >= 3 and b % 2:
                copies(b // 2 - 1)
        copies(NT - 1)

    return tensor, scalar, vector, out_ready


def self_attention(nc, io, keep):
    with ExitStack() as ctx:
        def sb(name, shape, dt=F32):
            return ctx.enter_context(nc.sbuf_tensor("s_" + name, shape, dt))

        def sem(name):
            return ctx.enter_context(nc.semaphore("s_" + name))

        out = sb("out", [P, NT, D])
        outT, hh, wo = sb("outT", [P, NK, T]), sb("hh", [P, NT, D]), sb("wo", [P, NK, D])
        norm = Norm(nc, ctx, "s_norm")
        rows, x1, h, x2, const = keep["rows"], keep["x1"], keep["h"], keep["x2"], keep["const"]
        ident = const[:, C_IDENT:C_IDENT + P]
        with ExitStack() as inner:
            tensor, scalar, vector, _ = attention(nc, inner, "s", dict(keep, out=out), DH, SCALE, True)
            with nc.Block() as block:
                block.tensor(tensor)
                block.scalar(scalar)
                block.vector(vector)

                @block.sync
                def _(sp):
                    with nc.semaphore("s_wo_in") as wo_in:
                        sp.dma_start(wo[:], io["w2o"].rearrange("(k p) n -> p k n", p=P)).then_inc(wo_in, 16)
                        sp.wait_ge(wo_in, 16)
        ps = ctx.enter_context(nc.psum_tensor("s_ps2", [P, 8, 512], F32))
        dve_done, oT_ps, oT_ready, hh_ps = map(sem, ("dve_done", "oT_psum", "oT_ready", "hh_psum"))
        with nc.Block() as block:

            @block.tensor
            def _(pe):
                for k in range(NK):
                    pe_transposes(nc, out, ps[:, k, :], k, ident).then_inc(oT_ps, 1)
                pe.wait_ge(oT_ready, NK)
                for t in range(NT):
                    pe_product(nc, ps[:, 4 + t, :], lambda k: outT[:, k, t * P:(t + 1) * P],
                               lambda k: wo[:, k, :], NK).then_inc(hh_ps, 1)

            @block.scalar
            def _(act):
                for k in range(NK):
                    act.wait_ge(oT_ps, k + 1)
                    nc.scalar.copy(outT[:, k, :], ps[:, k, :]).then_inc(oT_ready, 1)
                norm.scalar(nc, act)

            @block.vector
            def _(dve):
                chain = Chain(dve, dve_done)

                def row(r):
                    return rows[:, r, :].unsqueeze(1).broadcast_to([P, NT, D])

                chain.link(nc.vector.tensor_tensor(hh[:], h[:], row(R_B2O), ALU.add))
                for t in range(NT):
                    dve.wait_ge(hh_ps, t + 1)
                    chain.link(nc.vector.tensor_tensor(hh[:, t, :], hh[:, t, :], ps[:, 4 + t, :], ALU.add))
                norm.vector(nc, dve, chain, hh, 1e-12)
                for t in range(NT):
                    last = nc.vector.tensor_scalar(hh[:, t, :], hh[:, t, :], norm.mom[:, t, 0:1],
                                                   norm.rstd[:, t:t + 1], ALU.subtract, ALU.mult)
                    if t < NT - 1:
                        last.then_inc(dve_done, 1)
                        chain.n += 1
                chain.link(last)
                chain.link(nc.vector.tensor_tensor(hh[:], hh[:], row(R_GAMMA), ALU.mult))
                chain.link(nc.vector.tensor_tensor(hh[:], hh[:], row(R_BETA), ALU.add))
                nc.vector.tensor_tensor(x2[:], x1[:], hh[:], ALU.add)


L = D // 2
DL = L // H
NL = L // P
E = 8
F = 2 * D
NF = F // P


def low_rank_stage(nc, io, keep):
    with ExitStack() as ctx:
        def sb(name, shape, dt=F32):
            return ctx.enter_context(nc.sbuf_tensor("l_" + name, shape, dt))

        def sem(name):
            return ctx.enter_context(nc.semaphore("l_" + name))

        down, wqk, wv = sb("down", [P, NK, L]), sb("wqk", [P, NL, 2 * L]), sb("wv", [P, NL, L])
        g, gT, cT, rot = sb("g", [P, NT, D]), sb("gT", [P, NK, T]), sb("cT", [P, NL, T]), sb("rot", [P, NT, 2 * L])
        prods = [sb(f"prod{i}", [P, NT * 2 * H, DL // 2]) for i in range(4)]
        norm, rms = Norm(nc, ctx, "l_norm"), Norm(nc, ctx, "l_rms")
        ps = ctx.enter_context(nc.psum_tensor("l_ps", [P, 8, 512], F32))
        const, rows, x2, f, kT, qz, vz = (keep[n] for n in ("const", "rows", "x2", "f", "kT", "qz", "vz"))
        ident = const[:, C_IDENT:C_IDENT + P]
        w_in, dve_done, g_ready, gT_ps, gT_ready, c_ps, c_ready, qk_ps, v_ps, v_read = map(
            sem, ("w_in", "dve_done", "g_ready", "gT_psum", "gT_ready", "c_psum", "c_ready", "qk_psum", "v_psum", "v_read"))
        rot_ready, rot_ps = sem("rot_ready"), sem("rot_psum")
        with nc.Block() as block:

            @block.sync
            def _(sp):
                sp.dma_start(down[:], io["w_down"].rearrange("(k p) n -> p k n", p=P)).then_inc(w_in, 16)
                sp.dma_start(wqk[:, :, 0:L], io["w3q"].rearrange("(k p) n -> p k n", p=P)).then_inc(w_in, 16)
                sp.dma_start(wqk[:, :, L:], io["w3k"].rearrange("(k p) n -> p k n", p=P)).then_inc(w_in, 16)
                sp.dma_start(wv[:], io["w3v"].rearrange("(k p) n -> p k n", p=P)).then_inc(w_in, 16)

            @block.tensor
            def _(pe):
                pe.wait_ge(g_ready, NT)
                for k in range(NK):
                    pe_transposes(nc, g, ps[:, k, :], k, ident).then_inc(gT_ps, 1)
                pe.wait_ge(w_in, 64)
                pe.wait_ge(gT_ready, NK)
                for c in range(NL):
                    pe_product(nc, ps[:, 4 + c, :], lambda k: down[:, k, c * P:(c + 1) * P],
                               lambda k: gT[:, k, :], NK).then_inc(c_ps, 1)
                pe.wait_ge(c_ready, NL)
                for t in range(NT):
                    pe_product(nc, ps[:, t, :], lambda k: cT[:, k, t * P:(t + 1) * P],
                               lambda k: wqk[:, k, :], NL).then_inc(qk_ps, 1)
                for t in range(NT):
                    pe_product(nc, ps[:, 6 + t // 2, (t % 2) * L:(t % 2 + 1) * L],
                               lambda k: cT[:, k, t * P:(t + 1) * P], lambda k: wv[:, k, :], NL).then_inc(v_ps, 1)
                pe.wait_ge(rot_ready, 2)
                for c in range(2 * NL):
                    pe_transposes(nc, rot, ps[:, c, :], c, ident).then_inc(rot_ps, 1)

            @block.scalar
            def _(act):
                norm.scalar(nc, act)
                rms.scalar(nc, act)
                for c in range(NL):
                    act.wait_ge(c_ps, c + 1)
                    nc.scalar.copy(cT[:, c, :], ps[:, 4 + c, :]).then_inc(c_ready, 1)
                for two in range(2):
                    act.wait_ge(v_ps, NT)
                    nc.scalar.activation(vz[:, two], ps[:, 6:8, :].rearrange("p a (b n) -> p (a b) n", n=L), ACT.Copy,
                                         scale=const[:, C_PARITY + two:C_PARITY + two + 1]).then_inc(v_read, 1)
                act.wait_ge(rot_ps, 1)
                for j in range(8):
                    nc.scalar.activation(qz[:, :, j, :], ps[:, 0, :].rearrange("p (b s) -> p b s", s=S), ACT.Copy,
                                         scale=const[:, C_HEAD16 + j:C_HEAD16 + j + 1])
                act.wait_ge(rot_ps, 2 * NL)
                nc.scalar.copy(kT[:], ps[:, 2:4, :])

            @block.vector
            def _(dve):
                chain = Chain(dve, dve_done)
                norm.vector(nc, dve, chain, x2, 1e-5)
                for t in range(NT):
                    last = nc.vector.tensor_scalar(f[:, t, :], x2[:, t, :], norm.mom[:, t, 0:1],
                                                   norm.rstd[:, t:t + 1], ALU.subtract, ALU.mult)
                    if t < NT - 1:
                        last.then_inc(dve_done, 1)
                        chain.n += 1
                chain.link(last)
                rms.vector(nc, dve, chain, f, 1e-5, about_zero=True)
                for t in range(NT):
                    nc.vector.scalar_tensor_tensor(out=g[:, t, :], in0=f[:, t, :], scalar=rms.rstd[:, t:t + 1],
                                                   in1=rows[:, R_G1, :], op0=ALU.mult, op1=ALU.mult).then_inc(g_ready, 1)
                for k in range(NK):
                    dve.wait_ge(gT_ps, k + 1)
                    nc.vector.tensor_copy(gT[:, k, :], ps[:, k, :]).then_inc(gT_ready, 1)
                dve.wait_ge(qk_ps, NT)
                pairs = ps[:, 0:NT, :].rearrange("p t n -> p (t n)").rearrange("p (h i two) -> p h i two", i=DL // 2, two=2)
                shape = [P, NT * 2 * H, DL // 2]
                for n, (part, table) in enumerate(((0, C_COS), (1, C_SIN), (0, C_SIN), (1, C_COS))):
                    last = nc.vector.tensor_tensor(prods[n][:], pairs[:, :, :, part],
                                                   const[:, table:table + DL // 2].unsqueeze(1).broadcast_to(shape), ALU.mult)
                    if n < 3:
                        last.then_inc(dve_done, 1)
                        chain.n += 1
                chain.link(last)
                turned = rot[:].rearrange("p t n -> p (t n)").rearrange("p (h i two) -> p h i two", i=DL // 2, two=2)
                nc.vector.tensor_tensor(turned[:, :, :, 0], prods[0][:], prods[1][:], ALU.subtract).then_inc(rot_ready, 1)
                nc.vector.tensor_tensor(turned[:, :, :, 1], prods[2][:], prods[3][:], ALU.add).then_inc(rot_ready, 1)
                dve.wait_ge(rot_ps, 2)
                for j in range(8):
                    nc.vector.tensor_scalar_mul(qz[:, :, 8 + j, :], ps[:, 1, :].rearrange("p (b s) -> p b s", s=S),
                                                const[:, C_HEAD16 + j:C_HEAD16 + j + 1])


def causal_attention(nc, io, keep):
    with ExitStack() as ctx:
        tensor, scalar, vector, _ = attention(nc, ctx, "c", keep, DL, float(DL) ** -0.5, False)
        with nc.Block() as block:
            block.tensor(tensor)
            block.scalar(scalar)
            block.vector(vector)


def router_stage(nc, io, keep):
    with ExitStack() as ctx:
        def sb(name, shape, dt=F32):
            return ctx.enter_context(nc.sbuf_tensor("g_" + name, shape, dt))

        def sem(name):
            return ctx.enter_context(nc.semaphore("g_" + name))

        up, router = sb("up", [P, NL, D]), sb("router", [P, NK, E])
        outT, h3, g, gT = sb("outT", [P, NL, T]), sb("h3", [P, NT, D]), sb("g", [P, NT, D]), sb("gT", [P, NK, T])
        big, total, rtotal = (sb(n, [P, NT]) for n in ("big", "total", "rtotal"))
        pr, hit = sb("pr", [P, NT, E]), sb("hit", [P, 2, NT, E])
        best, weight, which_f = sb("best", [P, NT, 8]), sb("weight", [P, NT, 2]), sb("which_f", [P, NT, 8])
        which = sb("which", [P, NT, 8], U32)
        norm = Norm(nc, ctx, "g_norm")
        ps = ctx.enter_context(nc.psum_tensor("g_ps", [P, 8, 512], F32))
        const, rows, x2, f, out, gates, t_s = (keep[n] for n in ("const", "rows", "x2", "f", "out", "gates", "t_s"))
        ident = const[:, C_IDENT:C_IDENT + P]
        w_in, dve_done, oT_ps, oT_ready, h_ps, g_ready, gT_ps, gT_ready, t_hi, logits = map(
            sem, ("w_in", "dve_done", "oT_psum", "oT_ready", "h_psum", "g_ready", "gT_psum", "gT_ready", "t_hi", "logits"))
        shifted, exp_ready = sem("shifted"), sem("exp_ready")
        with nc.Block() as block:

            @block.sync
            def _(sp):
                sp.dma_start(up[:], io["w_up"].rearrange("(k p) n -> p k n", p=P)).then_inc(w_in, 16)
                sp.dma_start(router[:], io["router"].rearrange("(k p) n -> p k n", p=P)).then_inc(w_in, 16)

            @block.tensor
            def _(pe):
                for k in range(NL):
                    pe_transposes(nc, out, ps[:, k, :], k, ident).then_inc(oT_ps, 1)
                pe.wait_ge(w_in, 32)
                pe.wait_ge(oT_ready, NL)
                for t in range(NT):
                    pe_product(nc, ps[:, 4 + t, :], lambda k: outT[:, k, t * P:(t + 1) * P],
                               lambda k: up[:, k, :], NL).then_inc(h_ps, 1)
                pe.wait_ge(g_ready, NT)
                for k in range(NK):
                    pe_transposes(nc, g, ps[:, k, :], k, ident).then_inc(gT_ps, 1)
                pe.wait_ge(gT_ready, NK)
                for t in range(NT):
                    last = pe_product(nc, ps[:, 4, t * E:(t + 1) * E], lambda k: gT[:, k, t * P:(t + 1) * P],
                                      lambda k: router[:, k, :], NK)
                last.then_inc(logits, 1)

            @block.scalar
            def _(act):
                for k in range(NL):
                    act.wait_ge(oT_ps, k + 1)
                    nc.scalar.copy(outT[:, k, :], ps[:, k, :]).then_inc(oT_ready, 1)
                norm.scalar(nc, act)
                for k in range(NK):
                    act.wait_ge(gT_ready, k + 1)
                    nc.scalar.copy(t_s[:, 0, k, :], gT[:, k, :]).then_inc(t_hi, 1)
                act.wait_ge(shifted, 1)
                nc.scalar.activation(pr[:], pr[:], ACT.Exp).then_inc(exp_ready, 1)

            @block.vector
            def _(dve):
                chain = Chain(dve, dve_done)
                for t in range(NT):
                    dve.wait_ge(h_ps, t + 1)
                    last = nc.vector.tensor_tensor(h3[:, t, :], f[:, t, :], ps[:, 4 + t, :], ALU.add)
                    if t < NT - 1:
                        last.then_inc(dve_done, 1)
                        chain.n += 1
                chain.link(last)
                norm.vector(nc, dve, chain, h3, 1e-5, about_zero=True)
                for t in range(NT):
                    nc.vector.scalar_tensor_tensor(out=g[:, t, :], in0=h3[:, t, :], scalar=norm.rstd[:, t:t + 1],
                                                   in1=rows[:, R_G2, :], op0=ALU.mult, op1=ALU.mult).then_inc(g_ready, 1)
                for k in range(NK):
                    dve.wait_ge(gT_ps, k + 1)
                    nc.vector.tensor_copy(gT[:, k, :], ps[:, k, :]).then_inc(gT_ready, 1)
                nc.vector.tensor_tensor(x2[:], x2[:], h3[:], ALU.add)
                for k in range(NK):
                    dve.wait_ge(t_hi, k + 1)
                    nc.vector.tensor_tensor(t_s[:, 1, k, :], gT[:, k, :], t_s[:, 0, k, :].bitcast(F32), ALU.subtract)
                dve.wait_ge(logits, 1)
                lg = ps[:, 4, 0:NT * E].rearrange("p (t e) -> p t e", e=E)
                chain.link(nc.vector.reduce_max(big[:], lg, AX.X))
                nc.vector.tensor_tensor(pr[:], lg, big[:].unsqueeze(2).broadcast_to([P, NT, E]), ALU.subtract).then_inc(shifted, 1)
                dve.wait_ge(exp_ready, 1)
                chain.link(nc.vector.reduce_sum(total[:], pr[:], AX.X))
                chain.link(nc.vector.reciprocal(rtotal[:], total[:]))
                chain.link(nc.vector.tensor_tensor(pr[:], pr[:], rtotal[:].unsqueeze(2).broadcast_to([P, NT, E]), ALU.mult))
                for t in range(NT):
                    chain.link(nc.vector.max(best[:, t, :], pr[:, t, :]))
                    chain.link(nc.vector.max_index(which[:, t, :], best[:, t, :], pr[:, t, :]))
                chain.link(nc.vector.tensor_copy(which_f[:], which[:]))
                chain.link(nc.vector.tensor_tensor(total[:], best[:, :, 0], best[:, :, 1], ALU.add))
                chain.link(nc.vector.reciprocal(rtotal[:], total[:]))
                chain.link(nc.vector.tensor_tensor(weight[:], best[:, :, 0:2], rtotal[:].unsqueeze(2).broadcast_to([P, NT, 2]),
                                                   ALU.mult))
                for t in range(NT):
                    for n in range(2):
                        chain.link(nc.vector.tensor_scalar(hit[:, n, t, :], const[:, C_IOTA:C_IOTA + E],
                                                           which_f[:, t, n:n + 1], weight[:, t, n:n + 1],
                                                           ALU.is_equal, ALU.mult))
                nc.vector.tensor_tensor(gates[:], hit[:, 0], hit[:, 1], ALU.add)


PIECE = 1024
N13, N2 = 2 * NK, NF // 2
SLOTS_W = 6


def expert_steps(more):
    out = []
    for fc in range(NF):
        out.append(("H", fc))
        if fc < N2:
            out.append(("W2", fc))
    for t in range(NT):
        out.append(("Y", t))
        if more:
            out += [("W13", 2 * t), ("W13", 2 * t + 1)]
    return out


def experts(nc, io, keep):
    with ExitStack() as ctx:
        def sb(name, shape, dt=F32):
            return ctx.enter_context(nc.sbuf_tensor("e_" + name, shape, dt))

        def sem(name):
            return ctx.enter_context(nc.semaphore("e_" + name))

        raw = sb("raw", [P, SLOTS_W, PIECE])
        w13 = sb("w13", [P, 2, N13, PIECE], F32R)
        w2 = sb("w2", [P, 2, NF, D], F32R)
        hid = sb("hid", [P, 2, NF, T], F32R)
        gated = sb("gated", [P, 2, T])
        full = sb("full", [P, 2, T])
        ps_h = ctx.enter_context(nc.psum_tensor("e_ps_h", [P, 4, 512], F32))
        ps_y = ctx.enter_context(nc.psum_tensor("e_ps_y", [P, NT, 512], F32))
        y, gates, t_s = keep["x2"], keep["gates"], keep["t_s"]
        staged = [sem(f"staged{i}") for i in range(SLOTS_W)]
        w_hi, w_lo, h_ps, silu_ready, full_ready, hid_hi, hid_lo, y_ps, y_read, stored = map(
            sem, ("w_hi", "w_lo", "h_psum", "silu_ready", "full_ready", "hid_hi", "hid_lo", "y_psum", "y_read", "stored"))
        PIECES = N13 + N2

        def source(e, i):
            if i < NK:
                return io["w1"][e, i * P:(i + 1) * P, :]
            if i < N13:
                return io["w3"][e, (i - NK) * P:(i - NK + 1) * P, :]
            i -= N13
            return io["w2"][e, 2 * i * P:2 * (i + 1) * P, :].rearrange("(two p) n -> p two n", p=P)

        def halves(i, half):
            if i < N13:
                return w13[:, half, i, :]
            return w2[:, half, 2 * (i - N13):2 * (i - N13) + 2, :].rearrange("p a n -> p (a n)")

        def loop(eng, first, body):
            first()
            with eng.Fori(0, E - 1) as e:
                body(e, True)
            body(E - 1, False)

        with nc.Block() as block:

            @block.sync
            def _(sp):
                def load(e, i, wait=True):
                    slot = i % SLOTS_W
                    if wait:
                        sp.wait_ge(w_lo, PIECES * e + i - SLOTS_W + 1)
                    dst = raw[:, slot] if i < N13 else raw[:, slot].rearrange("p (a n) -> p a n", a=2)
                    sp.dma_start(dst, source(e, i)).then_inc(staged[slot], 16)

                for i in range(PIECES):
                    load(0, i, wait=i >= SLOTS_W)
                with sp.Fori(1, E) as e:
                    for i in range(PIECES):
                        load(e, i)
                sp.wait_ge(y_read, NT * E)
                sp.dma_start(io["out"].rearrange("(t two) s d -> (two s) t d", two=2), y[:]).then_inc(stored, 16)
                sp.wait_ge(stored, 16)

            def piece(eng, e, i):
                eng.wait_ge(staged[i % SLOTS_W], 32 * e + (16 if i < SLOTS_W else 32))

            @block.scalar
            def _(act):
                def high(e, i):
                    piece(act, e, i)
                    nc.scalar.copy(halves(i, 0), raw[:, i % SLOTS_W]).then_inc(w_hi, 1)

                def first():
                    for i in range(N13):
                        high(0, i)

                def body(e, more):
                    for s in expert_steps(more):
                        if s[0] == "H":
                            fc = s[1]
                            act.wait_ge(h_ps, 2 * (NF * e + fc) + 1)
                            nc.scalar.activation(gated[:, fc % 2, :], ps_h[:, 2 * (fc % 2), :], ACT.Silu).then_inc(silu_ready, 1)
                            act.wait_ge(full_ready, NF * e + fc + 1)
                            nc.scalar.copy(hid[:, 0, fc, :], full[:, fc % 2, :]).then_inc(hid_hi, 1)
                        elif s[0] == "W2":
                            high(e, N13 + s[1])
                        elif s[0] == "W13":
                            if s[1] == 0:
                                act.wait_ge(h_ps, 2 * NF * (e + 1))
                            high(e + 1, s[1])

                loop(act, first, body)

            @block.vector
            def _(dve):
                def low(e, i):
                    dve.wait_ge(w_hi, PIECES * e + i + 1)
                    nc.vector.tensor_tensor(halves(i, 1), raw[:, i % SLOTS_W], halves(i, 0).bitcast(F32),
                                            ALU.subtract).then_inc(w_lo, 1)

                def first():
                    for i in range(N13):
                        low(0, i)

                def body(e, more):
                    for s in expert_steps(more):
                        if s[0] == "H":
                            fc = s[1]
                            dve.wait_ge(h_ps, 2 * (NF * e + fc) + 2)
                            dve.wait_ge(silu_ready, NF * e + fc + 1)
                            nc.vector.tensor_tensor(full[:, fc % 2, :], gated[:, fc % 2, :], ps_h[:, 2 * (fc % 2) + 1, :],
                                                    ALU.mult).then_inc(full_ready, 1)
                            dve.wait_ge(hid_hi, NF * e + fc + 1)
                            nc.vector.tensor_tensor(hid[:, 1, fc, :], full[:, fc % 2, :], hid[:, 0, fc, :].bitcast(F32),
                                                    ALU.subtract).then_inc(hid_lo, 1)
                        elif s[0] == "W2":
                            low(e, N13 + s[1])
                        elif s[0] == "W13":
                            low(e + 1, s[1])
                        else:
                            t = s[1]
                            dve.wait_ge(y_ps, NT * e + t + 1)
                            nc.vector.scalar_tensor_tensor(out=y[:, t, :], in0=ps_y[:, t, :],
                                                           scalar=gates[:, t, bass.ds(e, 1)], in1=y[:, t, :],
                                                           op0=ALU.mult, op1=ALU.add).then_inc(y_read, 1)
                            dve.wait_ge(y_read, NT * e + t + 1)

                loop(dve, first, body)

            @block.tensor
            def _(pe):
                def three(out, a, b, start, stop):
                    for n, (i, j) in enumerate(((1, 0), (0, 1), (0, 0))):
                        last = nc.tensor.matmul(out, a(i), b(j), start=(start and n == 0), stop=(stop and n == 2))
                    return last

                def body(e, more):
                    for s in expert_steps(more):
                        if s[0] == "H":
                            fc = s[1]
                            if fc == 0:
                                pe.wait_ge(w_lo, PIECES * e + N13)
                            if fc >= 2:
                                pe.wait_ge(full_ready, NF * e + fc - 1)
                            for side in range(2):
                                for k in range(NK):
                                    last = three(ps_h[:, 2 * (fc % 2) + side, :],
                                                 lambda i: w13[:, i, side * NK + k, fc * P:(fc + 1) * P],
                                                 lambda i: t_s[:, i, k, :], k == 0, k == NK - 1)
                                last.then_inc(h_ps, 1)
                        elif s[0] == "Y":
                            t = s[1]
                            if t == 0:
                                pe.wait_ge(w_lo, PIECES * (e + 1))
                            for fc in range(NF):
                                if t == 0:
                                    pe.wait_ge(hid_lo, NF * e + fc + 1)
                                last = three(ps_y[:, t, :], lambda i: hid[:, i, fc, t * P:(t + 1) * P],
                                             lambda i: w2[:, i, fc, :], fc == 0, fc == NF - 1)
                            last.then_inc(y_ps, 1)

                loop(pe, lambda: None, body)


INPUTS = ("x", "ctxT", "mask", "wqT", "wkT", "wvT", "woT", "bias_col", "bias_row", "const",
          "w2q", "w2k", "w2v", "w2o", "emb_fwd", "emb_rev",
          "w_down", "w3q", "w3k", "w3v", "w_up", "router", "w1", "w2", "w3")


def build(nc, io):
    with ExitStack() as ctx:
        def sb(name, shape, dt=F32):
            return ctx.enter_context(nc.sbuf_tensor(name, shape, dt))

        keep = {"const": sb("const", [P, C_ALL]), "bias": sb("bias", [P, B_ALL])}
        with ExitStack() as first:
            keep["wk"] = first.enter_context(nc.sbuf_tensor("wk_s", [P, 2, NK, D], F32R))
            keep["wv"] = first.enter_context(nc.sbuf_tensor("wv_s", [P, 2, NK, D], F32R))
            query_stage(nc, io, keep)
            cross_attention(nc, io, keep)
        keep["rows"] = sb("rows", [P, R_ALL, D])
        keep["x2"] = sb("x2", [P, NT, D])
        with ExitStack() as second:
            for n, shape in (("x1", [P, NT, D]), ("h", [P, NT, D]), ("kT", [P, NK, T]), ("qz", [P, B, H, S]),
                             ("vz", [P, 2, NT, D]), ("kz", [P, B, H, S])):
                keep[n] = second.enter_context(nc.sbuf_tensor(n, shape, F32))
            project_stage(nc, io, keep)
            for n in ("q_rel", "k_rel"):
                keep[n] = second.enter_context(nc.sbuf_tensor(n, [P, B * NP, S], F32))
            relative_stage(nc, io, keep)
            keep["prob"] = keep["kz"][:, 0:B // 2].rearrange("p t h s -> p (t h s)").rearrange("p (t a two s) -> p t a two s", a=NP, two=2, s=S)
            keep["probT"] = keep["kz"][:, B // 2:].rearrange("p t h s -> p (t h s)").rearrange(
                "p (t a q) -> p t a q", a=NP, q=P)
            self_attention(nc, io, keep)
        keep["t_s"] = sb("t_s", [P, 2, NK, T], F32R)
        keep["gates"] = sb("gates", [P, NT, E])
        with ExitStack() as fourth:
            for n, shape in (("f", [P, NT, D]), ("kT", [P, NL, T]), ("qz", [P, B, H, S]), ("vz", [P, 2, NT, L]),
                             ("out", [P, NT, L]), ("prob", [P, NT, NP, 2, S]), ("probT", [P, NT, NP, P])):
                keep[n] = fourth.enter_context(nc.sbuf_tensor("c_" + n, shape, F32))
            low_rank_stage(nc, io, keep)
            causal_attention(nc, io, keep)
            router_stage(nc, io, keep)
        experts(nc, io, keep)


def kernel(**inputs):
    import concourse.bacc as bacc
    from concourse.bass_utils import run_bass_kernel_spmd as run

    a = {k: np.asarray(v) for k, v in inputs.items()}

    def columns(name):
        return a[name].reshape(-1, P).T

    emb = a["L0_attn_dist_emb"]
    laid_out = {
        "x": a["x"].reshape(T, D),
        "ctxT": np.pad(a["ctx_1024"].transpose(0, 2, 1), ((0, 0), (0, 0), (0, KPAD - KEYS))),
        "mask": np.pad(a["mask_Bx1xSxS2_ik1"].reshape(B, S, KEYS), ((0, 0), (0, 0), (0, KPAD - KEYS))),
        "wqT": a["L0_xattn_WQ_w"].T, "wkT": a["L0_xattn_WK_w"].T, "wvT": a["L0_xattn_WV_w"].T,
        "woT": a["L0_xattn_WO_w"].T,
        "bias_col": np.concatenate([columns(n) for n in ("L0_xattn_WQ_b", "L0_xattn_WK_b", "L0_xattn_WV_b",
                                                        "L0_attn_bq", "L0_attn_bk")], axis=1),
        "bias_row": np.stack([a[n] for n in ("L0_xattn_WO_b", "L0_attn_bv", "L0_attn_bo", "L0_attn_ln_gamma",
                                            "L0_attn_ln_beta", "L0_ffn_g1", "L0_ffn_g2")]),
        "w2q": a["L0_attn_Wq"], "w2k": a["L0_attn_Wk"], "w2v": a["L0_attn_Wv"], "w2o": a["L0_attn_Wo"],
        "emb_fwd": np.tile(emb[EMB_BASE:EMB_BASE + P].T, (4, 1)),
        "emb_rev": np.tile(emb[EMB_BASE - 1:EMB_BASE - 1 + P][::-1].T, (4, 1)),
        "w_down": a["L0_ffn_w_down"], "w3q": a["L0_ffn_wq"], "w3k": a["L0_ffn_wk"], "w3v": a["L0_ffn_wv"],
        "w_up": a["L0_ffn_w_up"], "router": a["L0_ffn_router_w"],
        "w1": a["L0_ffn_w1"], "w2": a["L0_ffn_w2"], "w3": a["L0_ffn_w3"],
        "const": constants(),
    }
    nc = bacc.Bacc("TRN2", target_bir_lowering=False, num_devices=1)
    io, arrays = {}, {}
    for name, value in laid_out.items():
        value = np.ascontiguousarray(value)
        arrays["in_" + name] = value
        io[name] = nc.dram_tensor("in_" + name, value.shape, mybir.dt.from_np(value.dtype), kind="ExternalInput").ap()
    io["qT"] = nc.dram_tensor("scratch_qT", (P, NK, T), F32, kind="Internal").ap()
    io["attn"] = nc.dram_tensor("scratch_attn", (B, S, D), F32, kind="Internal").ap()
    for n in ("q_rel", "k_rel"):
        io[n] = nc.dram_tensor("scratch_" + n, (B * NP, P, P), F32, kind="Internal").ap()
    io["out"] = nc.dram_tensor("out", (B, S, D), F32, kind="ExternalOutput").ap()
    build(nc, io)
    result = run(nc, [arrays], core_ids=[0])
    return result.results[0]["out"]
```

```python
from contextlib import ExitStack

import numpy as np

import concourse.bass as bass
from concourse import mybir

F32 = mybir.dt.float32
F32R = mybir.dt.float32r
F16 = mybir.dt.float16
BF16 = mybir.dt.bfloat16
I32 = mybir.dt.int32
U32 = mybir.dt.uint32
ALU = mybir.AluOpType
ACT = mybir.ActivationFunctionType
AX = mybir.AxisListType

P = 128
B, S, D = 8, 64, 512
T = B * S
NT = T // P
NK = D // P
KEYS = 1601
H = 16
NP = H // 2
DH = D // H
KC = 402
NC = 4
KPAD = NC * KC
NKT = -(-KEYS // P)
TAIL = KEYS - (NKT - 1) * P
SCALE = float(DH) ** -0.5
MASKED = 1e-9 / SCALE
LOWEST = -3.0e38
V_SCALE = 16.0
P_SCALE = 32768.0

C_IDENT = 0
C_HEAD32 = C_IDENT + P
C_HEAD16 = C_HEAD32 + 4
C_PARITY = C_HEAD16 + 8
C_COS = C_PARITY + 2
C_SIN = C_COS + 8
C_CAUSAL = C_SIN + 8
C_IOTA = C_CAUSAL + S
C_ALL = C_IOTA + 8


def constants():
    c = np.zeros((P, C_ALL), np.float32)
    p = np.arange(P)
    c[:, C_IDENT:C_IDENT + P] = np.eye(P)
    c[:, C_HEAD32:C_HEAD32 + 4] = p[:, None] // 32 == np.arange(4)
    c[:, C_HEAD16:C_HEAD16 + 8] = p[:, None] // 16 == np.arange(8)
    c[:, C_PARITY:C_PARITY + 2] = p[:, None] // S == np.arange(2)
    freq = (1.0 / np.float32(10000.0) ** (np.arange(0, 16, 2, dtype=np.float32) / 16)).astype(np.float32)
    ang = (p % S).astype(np.float32)[:, None] * freq
    c[:, C_COS:C_COS + 8] = np.cos(ang)
    c[:, C_SIN:C_SIN + 8] = np.sin(ang)
    c[:, C_CAUSAL:C_CAUSAL + S] = np.where(np.arange(S) <= (p % S)[:, None], 0.0, -1.0e30)
    c[:, C_IOTA:C_IOTA + 8] = np.arange(8)
    return c


class Chain:

    def __init__(self, eng, sem):
        self.eng, self.sem, self.n = eng, sem, 0

    def link(self, ins):
        self.n += 1
        ins.then_inc(self.sem, 1)
        self.eng.wait_ge(self.sem, self.n)


def dve_moments(nc, chain, x, stats, moments):
    for t in range(NT):
        last = nc.vector.bn_stats(stats[:, t, :], x[:, t, :])
        if t < NT - 1:
            last.then_inc(chain.sem, 1)
            chain.n += 1
    chain.link(last)
    for t in range(NT):
        last = nc.vector.bn_aggr(moments[:, t, :], stats[:, t, :])
        if t < NT - 1:
            last.then_inc(chain.sem, 1)
            chain.n += 1
    chain.link(last)


def query_stage(nc, io, keep):
    with ExitStack() as ctx:
        def sb(name, shape, dt=F32):
            return ctx.enter_context(nc.sbuf_tensor("q_" + name, shape, dt))

        def sem(name):
            return ctx.enter_context(nc.semaphore("q_" + name))

        x = sb("x", [P, NT, D])
        xn = sb("xn", [P, NT, D])
        xnT = sb("xnT", [P, NK, T])
        qT = sb("qT", [P, NK, T])
        wq = sb("wq", [P, NK, D])
        wk = sb("wk", [P, NK, D])
        wv = sb("wv", [P, NK, D])
        stats = sb("stats", [P, NT, 6])
        mom = sb("mom", [P, NT, 2])
        std = sb("std", [P, NT])
        rstd = sb("rstd", [P, NT])
        ps = ctx.enter_context(nc.psum_tensor("q_ps", [P, 8, 512], F32))
        const, bias = keep["const"], keep["bias"]
        x_in, wq_in, wk_in, wv_in, const_in = map(sem, ("x_in", "wq_in", "wk_in", "wv_in", "const_in"))
        dve_done, var_ready, std_ready, xn_ready = map(sem, ("dve_done", "var_ready", "std_ready", "xn_ready"))
        xnT_ps, xnT_ready, q_ps, q_ready, q_out = map(sem, ("xnT_ps", "xnT_ready", "q_psum", "q_ready", "q_out"))
        w_hi = sem("w_hi")
        with nc.Block() as block:

            @block.sync
            def _(sp):
                sp.dma_start(x[:], io["x"].rearrange("(t p) d -> p t d", p=P)).then_inc(x_in, 16)
                sp.dma_start(const[:], io["const"]).then_inc(const_in, 16)
                sp.dma_start(bias[:], io["bias_col"]).then_inc(const_in, 16)
                sp.dma_start(wq[:], io["wqT"].rearrange("(k p) n -> p k n", p=P)).then_inc(wq_in, 16)
                sp.dma_start(wk[:], io["wkT"].rearrange("(k p) n -> p k n", p=P)).then_inc(wk_in, 16)
                sp.dma_start(wv[:], io["wvT"].rearrange("(k p) n -> p k n", p=P)).then_inc(wv_in, 16)
                for c in range(NK):
                    sp.wait_ge(q_ready, c + 1)
                    sp.dma_start(io["qT"][:, c, :], qT[:, c, :]).then_inc(q_out, 16)
                sp.wait_ge(q_out, 16 * NK)

            @block.vector
            def _(dve):
                chain = Chain(dve, dve_done)
                dve.wait_ge(x_in, 16)
                dve_moments(nc, chain, x, stats, mom)
                nc.vector.tensor_scalar_add(std[:], mom[:, :, 1], 1e-5).then_inc(var_ready, 1)
                dve.wait_ge(std_ready, 1)
                chain.link(nc.vector.reciprocal(rstd[:], std[:]))
                for t in range(NT):
                    nc.vector.tensor_scalar(xn[:, t, :], x[:, t, :], mom[:, t, 0:1], rstd[:, t:t + 1],
                                            ALU.subtract, ALU.mult).then_inc(xn_ready, 1)
                for k in range(NK):
                    dve.wait_ge(xnT_ps, k + 1)
                    nc.vector.tensor_copy(xnT[:, k, :], ps[:, k, :]).then_inc(xnT_ready, 1)
                for n, (w, hl) in enumerate(((wk, keep["wk"]), (wv, keep["wv"]))):
                    dve.wait_ge(w_hi, n + 1)
                    chain.link(nc.vector.tensor_tensor(hl[:, 1], w[:], hl[:, 0].bitcast(F32), ALU.subtract))

            @block.scalar
            def _(act):
                act.wait_ge(var_ready, 1)
                nc.scalar.activation(std[:], std[:], ACT.Sqrt).then_inc(std_ready, 1)
                act.wait_ge(wk_in, 16)
                nc.scalar.activation(keep["wk"][:, 0], wk[:], ACT.Copy).then_inc(w_hi, 1)
                act.wait_ge(wv_in, 16)
                nc.scalar.activation(keep["wv"][:, 0], wv[:], ACT.Copy).then_inc(w_hi, 1)
                act.wait_ge(const_in, 32)
                for c in range(NK):
                    act.wait_ge(q_ps, c + 1)
                    nc.scalar.activation(qT[:, c, :], ps[:, 4 + c, :], ACT.Identity,
                                         bias=bias[:, BQ + c:BQ + c + 1]).then_inc(q_ready, 1)

            @block.tensor
            def _(pe):
                pe.wait_ge(const_in, 32)
                pe.wait_ge(xn_ready, NT)
                for k in range(NK):
                    for t in range(NT):
                        last = nc.tensor.transpose(ps[:, k, t * P:(t + 1) * P], xn[:, t, k * P:(k + 1) * P],
                                                   const[:, C_IDENT:C_IDENT + P])
                    last.then_inc(xnT_ps, 1)
                pe.wait_ge(wq_in, 16)
                pe.wait_ge(xnT_ready, NK)
                for c in range(NK):
                    for k in range(NK):
                        last = nc.tensor.matmul(ps[:, 4 + c, :], wq[:, k, c * P:(c + 1) * P], xnT[:, k, :],
                                                start=(k == 0), stop=(k == NK - 1))
                    last.then_inc(q_ps, 1)


BQ, BK, BV, B2Q, B2K = 0, 4, 8, 12, 16
B_ALL = 20


NG = -(-NKT // 4)
EARLY = 4
KEYS_AHEAD = [("K", 0, j) for j in range(NC)] + [("K", 1, j) for j in range(NC - 1)]
FIRST_STEPS = (KEYS_AHEAD[:NC] + [("V", 0), ("S", 0), ("V", 1), ("M", 0), ("V", 2), ("E", 0), ("V", 3)]
               + KEYS_AHEAD[NC:])


def pair_steps(p, between, after):
    a = p - 1
    mark, at = ("", p) if p < NP else ("'", 0)
    before = [("PV", a - 1, g) for g in range(1, NG)] + [("O", a - 1)] if a else []
    ahead = {5: [("C", 2)], 6: [("C", 3)], 7: [("Q",)]}.get(p, [])
    middle = [("PT", a, 1), ("PV", a, 0), ("PT", a, 2), ("PT", a, 3)]
    if ahead:
        rest = ahead + between + middle[:1] + [("M" + mark, at)] + middle[1:] + [("E" + mark, at)]
    else:
        rest = [("M" + mark, at)] + between + middle[:1] + [("E" + mark, at)] + middle[1:]
    return [("S" + mark, at)] + before + [("PT", a, 0)] + rest + after


def batch_steps(more):
    out = []
    for p in range(1, NP + 1):
        c = (p + 1) // 2
        between = [("K", c % NK, NC - 1), ("K", (c + 1) % NK, 0)] if p % 2 else [("K", (c + 1) % NK, 1), ("K", (c + 1) % NK, 2)]
        after = {3: [("C", 0)], 4: [("C", 1)], 7: [("A",)]}.get(p, [])
        if p == 1:
            between = [("V", 4), ("V", 5)] + between + [("V", 6), ("V", 7)]
            after = [("V", kt) for kt in range(8, NKT)]
        out += pair_steps(p, between, after)
    p = NP - 1
    out += [("PV", p, 1), ("V'", 0), ("PV", p, 2), ("V'", 1), ("PV", p, 3), ("O", p), ("V'", 2), ("V'", 3)]
    ahead = ("C", "Q", "A", "S'", "M'", "E'", "V'")
    return [s for s in out if more or not (s[0] in ahead or s in KEYS_AHEAD)]


def jobs(steps):
    return [s for s in steps if s[0] in ("V", "V'", "K", "PT")]


RING = 3
FIRST_JOBS = len(jobs(FIRST_STEPS))
JOB_INDEX = {more: {s: n for n, s in enumerate(jobs(batch_steps(more)))} for more in (True, False)}
NJ = len(JOB_INDEX[True])
SKIPS = [JOB_INDEX[True][("V", kt)] for kt in (EARLY + 3, EARLY + 6)][:-NJ % RING]


def job_bank(n):
    return (n + sum(n >= m for m in SKIPS)) % RING


def bank_user(n):
    before = (n - d for d in range(1, NJ))
    return next(m for m in before if job_bank(m % NJ) == job_bank(n))


def cross_attention(nc, io, keep):
    with ExitStack() as ctx:
        def sb(name, shape, dt=F32):
            return ctx.enter_context(nc.sbuf_tensor("x_" + name, shape, dt))

        def sem(name):
            return ctx.enter_context(nc.semaphore("x_" + name))

        SLOTS = 3
        ctx_raw = sb("ctx_raw", [P, SLOTS, NK, KC])
        ctx_s = sb("ctx_s", [P, 2, NK, KPAD], F32R)
        kT = sb("kT", [P, 2, 2, KPAD], F32R)
        v = sb("v", [P, 2, NKT, D], F16)
        prob = sb("prob", [P, 2, KPAD])
        probT = sb("probT", [P, 2, NKT, P], F16)
        q_raw = sb("q_raw", [P, NK, S])
        q_s = sb("q_s", [P, 2, H, S], F32R)
        mask_raw = sb("mask_raw", [P, KEYS], I32)
        mask01 = sb("mask01", [P, KPAD], BF16)
        mask_add = sb("mask_add", [P, KPAD])
        out_b = sb("out_b", [S, D])
        biggest = sb("biggest", [P, 2])
        negmax = sb("negmax", [P, 2])
        total = sb("total", [P, 2])
        rtotal = sb("rtotal", [P, 2])
        ps_s = ctx.enter_context(nc.psum_tensor("x_ps_s", [P, NC, 512], F32))
        ring = ctx.enter_context(nc.psum_tensor("x_ring", [P, RING, 512], F32))
        ps_o = ctx.enter_context(nc.psum_tensor("x_ps_o", [P, 512], F32))
        ctx_in = [sem(f"ctx_in{i}") for i in range(SLOTS)]
        q_in, mask_in, out_stored, out_free = map(sem, ("q_in", "mask_in", "out_stored", "out_free"))
        mask_ready, q_hi, q_ready, ctx_hi = map(sem, ("mask_ready", "q_hi", "q_ready", "ctx_hi"))
        ctx_ready = [sem(f"ctx_ready{j}") for j in range(NC)]
        scores, scores_read, max_done, max_ready, exp_done = map(
            sem, ("scores", "scores_read", "max_done", "max_ready", "exp_done"))
        job_done, job_hi, job_lo = map(sem, ("job_done", "job_hi", "job_lo"))
        o_done, o_read, rtotal_ready, total_scaled, pads = map(
            sem, ("o_done", "o_read", "rtotal_ready", "total_scaled", "pads"))
        const, bias = keep["const"], keep["bias"]
        wk, wv = keep["wk"], keep["wv"]
        ident = const[:, C_IDENT:C_IDENT + P]
        ctxT = io["ctxT"].rearrange("b (k p) s -> b p k s", p=P)

        def jobs_before(b, step, more=True):
            return FIRST_JOBS + b * NJ + JOB_INDEX[more][step]

        def piece(b, j):
            return b * NC + j

        def tile_keys(kt):
            return P if kt < NKT - 1 else TAIL

        def group(g):
            return range(4 * g, min(4 * g + 4, NKT))

        with nc.Block() as block:

            def first_steps(job, steps):
                n = 0
                for s in FIRST_STEPS:
                    if s[0] in steps:
                        steps[s[0]](0, s[1])
                    elif s[0] in ("K", "V"):
                        job(n)[s[0]](ring[:, (n - FIRST_JOBS) % RING], *s[1:])
                        n += 1

            def batches(eng, first, body):
                first()
                with eng.Fori(0, B - 1) as b:
                    body(b, True)
                body(B - 1, False)

            @block.sync
            def _(sp):
                def context(b, j, slot):
                    sp.dma_start(ctx_raw[:, slot], ctxT[b, :, :, j * KC:(j + 1) * KC]).then_inc(ctx_in[slot], 16)

                def small(b):
                    sp.dma_start(q_raw[:], io["qT"][:, :, bass.ds(b * S, S)]).then_inc(q_in, 16)

                def mask(b):
                    for half in range(2):
                        sp.dma_start(mask_raw[half * S:(half + 1) * S, :], io["mask"][b, :, :]).then_inc(mask_in, 16)

                small(0)
                mask(0)
                sp.sem_inc(out_free, 1)
                for j in range(NC):
                    if j >= SLOTS:
                        sp.wait_ge(ctx_ready[j - SLOTS], 1)
                    context(0, j, j % SLOTS)
                with sp.Fori(0, B - 1) as b:
                    for j in range(SLOTS):
                        sp.wait_ge(ctx_ready[j if j else NC - 1], b + 1)
                        context(b + 1, j, j)
                    sp.wait_ge(q_ready, b + 1)
                    small(b + 1)
                    sp.wait_ge(mask_ready, 2 * b + 2)
                    mask(b + 1)
                    sp.wait_ge(ctx_ready[0], b + 2)
                    context(b + 1, NC - 1, 0)
                    sp.wait_ge(o_read, 2 * NP * b + 2 * NP)
                    sp.dma_start(io["attn"][b, :, :], out_b[:]).then_inc(out_stored, 16)
                    sp.wait_ge(out_stored, 16 * b + 16)
                    sp.sem_inc(out_free, 1)
                sp.wait_ge(o_read, 2 * NP * B)
                sp.dma_start(io["attn"][B - 1, :, :], out_b[:]).then_inc(out_stored, 16)
                sp.wait_ge(out_stored, 16 * B)

            def slot_of(j):
                return j % SLOTS

            def ctx_landed(eng, b, j):
                if slot_of(j) == 0:
                    eng.wait_ge(ctx_in[0], b * 32 + (16 if j == 0 else 32))
                else:
                    eng.wait_ge(ctx_in[slot_of(j)], b * 16 + 16)

            POOL_PIECES = (0, 1)

            def context_low(eng, ins, b, j):
                eng.wait_ge(ctx_hi, piece(b, j) + 1)
                cols = slice(j * KC, (j + 1) * KC)
                ins.tensor_tensor(ctx_s[:, 1, :, cols], ctx_raw[:, slot_of(j)], ctx_s[:, 0, :, cols].bitcast(F32),
                                  ALU.subtract).then_inc(ctx_ready[j], 1)

            @block.gpsimd
            def _(pool):
                for j in POOL_PIECES:
                    context_low(pool, nc.gpsimd, 0, j)
                with pool.Fori(1, B) as b:
                    for j in POOL_PIECES:
                        context_low(pool, nc.gpsimd, b, j)

            @block.scalar
            def _(act):
                def queries(b):
                    act.wait_ge(q_in, 16 * b + 16)
                    for h in range(4):
                        nc.scalar.activation(q_s[:, 0, h::4, :], q_raw[:], ACT.Copy,
                                             scale=const[:, C_HEAD32 + h:C_HEAD32 + h + 1]).then_inc(q_hi, 1)

                def context(b, j):
                    ctx_landed(act, b, j)
                    nc.scalar.activation(ctx_s[:, 0, :, j * KC:(j + 1) * KC], ctx_raw[:, slot_of(j)],
                                         ACT.Copy).then_inc(ctx_hi, 1)

                def keys(bank, c, j):
                    nc.scalar.activation(kT[:, c % 2, 0, j * KC:(j + 1) * KC], bank[:, 0:KC], ACT.Identity,
                                         bias=bias[:, BK + c:BK + c + 1]).then_inc(job_hi, 1)

                def values(bank, kt):
                    n = tile_keys(kt)
                    nc.scalar.activation(v[0:n, 0, kt, :], bank[0:n, :], ACT.Copy, scale=V_SCALE).then_inc(job_hi, 1)

                def exponentials(b, p):
                    act.wait_ge(max_ready, NP * b + p + 1)
                    nc.scalar.activation(prob[:, p % 2, :], prob[:, p % 2, :], ACT.Exp,
                                         bias=negmax[:, p % 2:p % 2 + 1], scale=SCALE,
                                         accum_out=total[:, p % 2:p % 2 + 1]).then_inc(exp_done, 1)

                def first():
                    queries(0)
                    for j in range(NC):
                        context(0, j)

                    def job(n):
                        act.wait_ge(job_done, n + 1)
                        return {"K": keys, "V": values}

                    first_steps(job, {"E": exponentials})

                def body(b, more):
                    for s in batch_steps(more):
                        if s in JOB_INDEX[more]:
                            act.wait_ge(job_done, jobs_before(b, s, more) + 1)
                            bank = ring[:, job_bank(JOB_INDEX[more][s])]
                        if s[0] == "K":
                            keys(bank, s[1], s[2])
                        elif s[0] in ("V", "V'"):
                            values(bank, s[1])
                        elif s[0] == "PT":
                            _, p, g = s
                            n = tile_keys(group(g)[0]) if len(group(g)) == 1 else P
                            w = P * len(group(g))
                            nc.scalar.activation(probT[0:n, 0, 4 * g:4 * g + len(group(g)), :],
                                                 bank[0:n, 0:w].rearrange("p (a c) -> p a c", c=P), ACT.Copy,
                                                 scale=P_SCALE).then_inc(job_hi, 1)
                        elif s[0] == "C":
                            act.wait_ge(job_done, jobs_before(b, ("K", NK - 1, s[1])) + 1)
                            context(b + 1, s[1])
                        elif s[0] == "Q":
                            act.wait_ge(scores, NP * b + NP)
                            queries(b + 1)
                        elif s[0] == "E":
                            if s[1] >= 2:
                                act.wait_ge(rtotal_ready, NP * b + s[1] - 1)
                            exponentials(b, s[1])
                        elif s[0] == "E'":
                            act.wait_ge(rtotal_ready, NP * b + NP - 1)
                            exponentials(b + 1, 0)
                        elif s[0] == "O":
                            p = s[1]
                            act.wait_ge(o_done, NP * b + p + 1)
                            act.wait_ge(rtotal_ready, NP * b + p + 1)
                            if p == 0:
                                act.wait_ge(out_free, b + 1)
                            for h in range(2):
                                nc.scalar.activation(
                                    out_b[:, (2 * p + h) * DH:(2 * p + h + 1) * DH],
                                    ps_o[h * S:(h + 1) * S, (p % 2) * 64 + h * DH:(p % 2) * 64 + (h + 1) * DH],
                                    ACT.Copy, scale=rtotal[h * S:(h + 1) * S, p % 2:p % 2 + 1]).then_inc(o_read, 1)

                batches(act, first, body)

            @block.vector
            def _(dve):
                def low(out, psum, hi, scale=None):
                    if scale is None:
                        return nc.vector.tensor_tensor(out, psum, hi, ALU.subtract)
                    op = ALU.add if not isinstance(scale, float) else ALU.mult
                    return nc.vector.scalar_tensor_tensor(out=out, in0=psum, scalar=scale, in1=hi, op0=op,
                                                          op1=ALU.subtract)

                def queries(b):
                    for h in range(4):
                        dve.wait_ge(q_hi, 4 * b + h + 1)
                        last = nc.vector.scalar_tensor_tensor(
                            out=q_s[:, 1, h::4, :], in0=q_raw[:], scalar=const[:, C_HEAD32 + h:C_HEAD32 + h + 1],
                            in1=q_s[:, 0, h::4, :].bitcast(F32), op0=ALU.mult, op1=ALU.subtract)
                    last.then_inc(q_ready, 1)

                def masks(b):
                    dve.wait_ge(mask_in, 32 * b + 32)
                    nc.vector.tensor_scalar(mask01[:, 0:KEYS], mask_raw[:], 0, None, ALU.not_equal).then_inc(mask_ready, 1)
                    nc.vector.tensor_scalar(mask_add[:, 0:KEYS], mask_raw[:], 0, MASKED, ALU.is_equal,
                                            ALU.mult).then_inc(mask_ready, 1)

                def keys(bank, c, j):
                    cols = slice(j * KC, (j + 1) * KC)
                    low(kT[:, c % 2, 1, cols], bank[:, 0:KC], kT[:, c % 2, 0, cols].bitcast(F32),
                        bias[:, BK + c:BK + c + 1]).then_inc(job_lo, 1)

                def values(bank, kt):
                    n = tile_keys(kt)
                    low(v[0:n, 1, kt, :], bank[0:n, :], v[0:n, 0, kt, :], V_SCALE).then_inc(job_lo, 1)

                def masked_scores(b, p):
                    if p == 0:
                        dve.wait_ge(mask_ready, 2 * b + 2)
                    dve.wait_ge(scores, NP * b + p + 1)
                    nc.vector.tensor_tensor(prob[:, p % 2, :].rearrange("p (c n) -> p c n", n=KC),
                                            ps_s[:, :, 0:KC], mask01[:].rearrange("p (c n) -> p c n", n=KC),
                                            ALU.mult).then_inc(scores_read, 1)

                def maxima(b, p):
                    k = p % 2
                    dve.wait_ge(scores_read, NP * b + p + 1)
                    nc.vector.memset(negmax[:, k:k + 1], 0.0).then_inc(max_done, 1)
                    nc.vector.tensor_tensor_reduce(
                        out=prob[:, k, :], in0=prob[:, k, :], in1=mask_add[:], scale=1.0, scalar=LOWEST,
                        op0=ALU.add, op1=ALU.max, accum_out=biggest[:, k:k + 1]).then_inc(max_done, 1)
                    dve.wait_ge(max_done, 2 * (NP * b + p + 1))
                    nc.vector.tensor_scalar_mul(negmax[:, k:k + 1], biggest[:, k:k + 1], -SCALE).then_inc(max_ready, 1)

                def first():
                    nc.vector.memset(mask01[:, KEYS:], 0.0).then_inc(pads, 1)
                    nc.vector.memset(mask_add[:, KEYS:], LOWEST).then_inc(pads, 1)
                    queries(0)
                    for j in (2, 3):
                        context_low(dve, nc.vector, 0, j)
                    masks(0)
                    dve.wait_ge(pads, 2)

                    def job(n):
                        dve.wait_ge(job_hi, n + 1)
                        return {"K": keys, "V": values}

                    first_steps(job, {"S": masked_scores, "M": maxima})

                def body(b, more):
                    for s in batch_steps(more):
                        if s in JOB_INDEX[more]:
                            dve.wait_ge(job_hi, jobs_before(b, s, more) + 1)
                            bank = ring[:, job_bank(JOB_INDEX[more][s])]
                        if s[0] == "K":
                            keys(bank, s[1], s[2])
                        elif s[0] in ("V", "V'"):
                            values(bank, s[1])
                        elif s[0] == "PT":
                            _, p, g = s
                            n = tile_keys(group(g)[0]) if len(group(g)) == 1 else P
                            cols = slice(4 * g, 4 * g + len(group(g)))
                            low(probT[0:n, 1, cols, :],
                                bank[0:n, 0:P * len(group(g))].rearrange("p (a c) -> p a c", c=P),
                                probT[0:n, 0, cols, :], P_SCALE).then_inc(job_lo, 1)
                            if g == 0:
                                dve.wait_ge(exp_done, NP * b + p + 1)
                                k = p % 2
                                if p >= 2:
                                    dve.wait_ge(o_read, 2 * (NP * b + p - 1))
                                nc.vector.tensor_scalar_mul(rtotal[:, k:k + 1], total[:, k:k + 1],
                                                            V_SCALE * P_SCALE).then_inc(total_scaled, 1)
                                dve.wait_ge(total_scaled, NP * b + p + 1)
                                nc.vector.reciprocal(rtotal[:, k:k + 1], rtotal[:, k:k + 1]).then_inc(rtotal_ready, 1)
                        elif s[0] == "C":
                            if s[1] not in POOL_PIECES:
                                context_low(dve, nc.vector, b + 1, s[1])
                        elif s[0] == "Q":
                            queries(b + 1)
                        elif s[0] == "A":
                            masks(b + 1)
                        elif s[0] == "S":
                            masked_scores(b, s[1])
                        elif s[0] == "S'":
                            masked_scores(b + 1, 0)
                        elif s[0] == "M":
                            if s[1] >= 2:
                                dve.wait_ge(exp_done, NP * b + s[1] - 1)
                            maxima(b, s[1])
                        elif s[0] == "M'":
                            dve.wait_ge(exp_done, NP * b + NP - 1)
                            maxima(b + 1, 0)

                batches(dve, first, body)

            @block.tensor
            def _(pe):
                def three(out, a, b, start, stop):
                    for n, (i, j) in enumerate(((1, 0), (0, 1), (0, 0))):
                        last = nc.tensor.matmul(out, a(i), b(j), start=(start and n == 0), stop=(stop and n == 2))
                    return last

                def keys(bank, c, j):
                    for k in range(NK):
                        last = three(bank[:, 0:KC], lambda i: wk[:, i, k, c * P:(c + 1) * P],
                                     lambda i: ctx_s[:, i, k, j * KC:(j + 1) * KC], k == 0, k == NK - 1)
                    last.then_inc(job_done, 1)

                def values(bank, kt):
                    n = tile_keys(kt)
                    for k in range(NK):
                        last = three(bank[0:n, :], lambda i: ctx_s[:, i, k, kt * P:kt * P + n],
                                     lambda i: wv[:, i, k, :], k == 0, k == NK - 1)
                    last.then_inc(job_done, 1)

                def pair_scores(p):
                    for j in range(NC):
                        last = three(ps_s[:, j, 0:KC], lambda i: q_s[:, i, 2 * p:2 * p + 2, :].rearrange("p h s -> p (h s)"),
                                     lambda i: kT[:, p // 2 % 2, i, j * KC:(j + 1) * KC], True, True)
                    last.then_inc(scores, 1)

                def first():
                    def job(n):
                        if n < NC:
                            pe.wait_ge(ctx_ready[n], 1)
                        if n >= RING:
                            pe.wait_ge(job_lo, n - RING + 1)
                        return {"K": keys, "V": values}

                    def first_scores(_, p):
                        pe.wait_ge(q_ready, 1)
                        pe.wait_ge(job_lo, NC)
                        pair_scores(p)

                    first_steps(job, {"S": first_scores})

                def body(b, more):
                    for s in batch_steps(more):
                        if s in JOB_INDEX[more]:
                            n = JOB_INDEX[more][s]
                            pe.wait_ge(job_lo, FIRST_JOBS + b * NJ + bank_user(n) + 1)
                            bank = ring[:, job_bank(n)]
                        if s[0] == "K":
                            if s[1] == 0:
                                pe.wait_ge(ctx_ready[s[2]], b + 2)
                            keys(bank, s[1], s[2])
                        elif s[0] in ("V", "V'"):
                            values(bank, s[1])
                        elif s[0] == "S":
                            p = s[1]
                            if p > 1:
                                pe.wait_ge(job_lo, jobs_before(b, ("K", p // 2, NC - 1), more) + 1)
                            pe.wait_ge(scores_read, NP * b + p)
                            pair_scores(p)
                        elif s[0] == "S'":
                            pe.wait_ge(q_ready, b + 2)
                            pe.wait_ge(job_lo, jobs_before(b, ("K", 0, NC - 1)) + 1)
                            pe.wait_ge(scores_read, NP * b + NP)
                            pair_scores(0)
                        elif s[0] == "PT":
                            _, p, g = s
                            pe.wait_ge(exp_done, NP * b + p + 1)
                            for a, kt in enumerate(group(g)):
                                n = tile_keys(kt)
                                last = nc.tensor.transpose(bank[0:n, a * P:(a + 1) * P],
                                                           prob[:, p % 2, kt * P:kt * P + n], ident)
                            last.then_inc(job_done, 1)
                        elif s[0] == "PV":
                            _, p, g = s
                            if p == 0 and g:
                                pe.wait_ge(job_lo, jobs_before(b, ("V", group(g)[-1]), more) + 1)
                            else:
                                pe.wait_ge(job_lo, jobs_before(b, ("PT", p, g), more) + 1)
                            if g == 0 and p:
                                pe.wait_ge(o_read, 2 * (NP * b + p))
                            for kt in group(g):
                                n = tile_keys(kt)
                                last = three(ps_o[:, (p % 2) * 64:(p % 2) * 64 + 64],
                                             lambda i: probT[0:n, i, kt, :],
                                             lambda i: v[0:n, i, kt, p * 64:(p + 1) * 64],
                                             kt == 0, kt == NKT - 1)
                            if g == NG - 1:
                                last.then_inc(o_done, 1)

                batches(pe, first, body)




class Norm:

    def __init__(self, nc, ctx, name):
        def sb(tile, shape):
            return ctx.enter_context(nc.sbuf_tensor(f"{name}_{tile}", shape, F32))

        self.stats, self.mom = sb("stats", [P, NT, 6]), sb("mom", [P, NT, 2])
        self.std, self.root, self.rstd, self.square = (sb(t, [P, NT]) for t in ("std", "root", "rstd", "square"))
        self.var_ready = ctx.enter_context(nc.semaphore(name + "_var_ready"))
        self.root_ready = ctx.enter_context(nc.semaphore(name + "_root_ready"))

    def vector(self, nc, dve, chain, x, eps, about_zero=False):
        dve_moments(nc, chain, x, self.stats, self.mom)
        if about_zero:
            chain.link(nc.vector.tensor_tensor(self.square[:], self.mom[:, :, 0], self.mom[:, :, 0], ALU.mult))
            nc.vector.scalar_tensor_tensor(out=self.std[:], in0=self.square[:], scalar=eps, in1=self.mom[:, :, 1],
                                           op0=ALU.add, op1=ALU.add).then_inc(self.var_ready, 1)
        else:
            nc.vector.tensor_scalar_add(self.std[:], self.mom[:, :, 1], eps).then_inc(self.var_ready, 1)
        dve.wait_ge(self.root_ready, 1)
        chain.link(nc.vector.reciprocal(self.rstd[:], self.root[:]))

    def scalar(self, nc, act):
        act.wait_ge(self.var_ready, 1)
        nc.scalar.activation(self.root[:], self.std[:], ACT.Sqrt).then_inc(self.root_ready, 1)


def pe_transposes(nc, src, out, k, ident):
    for t in range(NT):
        last = nc.tensor.transpose(out[:, t * P:(t + 1) * P], src[:, t, k * P:(k + 1) * P], ident)
    return last


def pe_product(nc, out, lhsT, rhs, chunks):
    for k in range(chunks):
        last = nc.tensor.matmul(out, lhsT(k), rhs(k), start=(k == 0), stop=(k == chunks - 1))
    return last


R_BO, R_B2V, R_B2O, R_GAMMA, R_BETA, R_G1, R_G2 = range(7)
R_ALL = 7


EMB_BASE = D - S


def project_stage(nc, io, keep):
    with ExitStack() as ctx:
        def sb(name, shape, dt=F32):
            return ctx.enter_context(nc.sbuf_tensor("p_" + name, shape, dt))

        def sem(name):
            return ctx.enter_context(nc.semaphore("p_" + name))

        x, attn = sb("x", [P, NT, D]), sb("attn", [P, NT, D])
        attnT, hT, w2v = sb("attnT", [P, NK, T]), sb("hT", [P, NK, T]), sb("w2v", [P, NK, D])
        wo, w2k = (keep["k_rel"][:, n * B * NP // 2:(n + 1) * B * NP // 2, :].rearrange(
            "p i s -> p (i s)").rearrange("p (k n) -> p k n", n=D) for n in range(2))
        w2q, qT = (keep["q_rel"][:, n * B * NP // 2:(n + 1) * B * NP // 2, :].rearrange(
            "p i s -> p (i s)").rearrange("p (k n) -> p k n", n=D) for n in range(2))
        emb = sb("emb", [P, 2, P])
        SLOTS = 8

        def stage(slot):
            return (x, attnT)[slot // 4][:, slot % 4, :]

        v = attn
        norm = Norm(nc, ctx, "p_norm")
        ps = ctx.enter_context(nc.psum_tensor("p_ps", [P, 8, 512], F32))
        const, bias, rows = keep["const"], keep["bias"], keep["rows"]
        x1, h, kT, qz, kz, vz = (keep[n] for n in ("x1", "h", "kT", "qz", "kz", "vz"))
        ident = const[:, C_IDENT:C_IDENT + P]
        attn_in, x_in, bo_in, rows_in, wo_in, weights_in = map(
            sem, ("attn_in", "x_in", "bo_in", "rows_in", "wo_in", "weights_in"))
        dve_done, aT_ps, aT_ready, x1_ps, h_ready = map(sem, ("dve_done", "aT_psum", "aT_ready", "x1_psum", "h_ready"))
        hT_ps, hT_ready, k_ps, k_ready, q_ps, q_ready, v_ps = map(
            sem, ("hT_psum", "hT_ready", "k_psum", "k_ready", "q_psum", "q_ready", "v_psum"))
        emb_in, rel_ps, act_staged, dve_staged, z_ready = map(sem, ("emb_in", "rel_psum", "act_staged", "dve_staged", "z_ready"))
        stored = [sem(f"stored{i}") for i in range(SLOTS)]
        sides = ((kz, 1, keep["k_rel"], io["k_rel"], keep["k_rel_in"]), (qz, 0, keep["q_rel"], io["q_rel"], keep["q_rel_in"]))
        JOBS = 2 * NP * B // 4
        with nc.Block() as block:

            def load_turned(eng, side):
                _, _, turned, scratch, turned_in = sides[side]
                for slot in range(SLOTS):
                    eng.wait_ge(stored[slot], 16 * (side + 1) * (JOBS // 2 // SLOTS))
                for half in range(2):
                    src = bass.AP(tensor=scratch.tensor, offset=half * S * P + S - 1,
                                  ap=[[P - 1, S], [P * P, NP * B], [1, S]])
                    eng.dma_start(turned[half * S:(half + 1) * S], src).then_inc(turned_in, 16)

            @block.sync
            def _(sp):
                sp.dma_start(attn[:], io["attn"].rearrange("(t two) s d -> (two s) t d", two=2)).then_inc(attn_in, 16)
                sp.dma_start(wo[:], io["woT"].rearrange("(k p) n -> p k n", p=P)).then_inc(wo_in, 16)
                sp.dma_start(x[:], io["x"].rearrange("(t p) d -> p t d", p=P)).then_inc(x_in, 16)
                for w, name in ((w2k, "w2k"), (w2q, "w2q"), (w2v, "w2v")):
                    sp.dma_start(w[:], io[name].rearrange("(k p) n -> p k n", p=P)).then_inc(weights_in, 16)
                sp.dma_start(emb[:, 0, :], io["emb_rev"]).then_inc(emb_in, 16)
                sp.dma_start(emb[:, 1, :], io["emb_fwd"]).then_inc(emb_in, 16)
                for n in range(JOBS):
                    side, m = divmod(n, JOBS // 2)
                    scratch = sides[side][3]
                    sp.wait_ge(act_staged if n % 2 == 0 else dve_staged, n // 2 + 1)
                    sp.dma_start(scratch[4 * m:4 * m + 4].rearrange("i p j -> p i j"),
                                 stage(n % SLOTS).rearrange("p (i j) -> p i j", j=P)).then_inc(stored[n % SLOTS], 16)
                load_turned(sp, 1)

            @block.gpsimd
            def _(pool):
                pool.dma_start(rows[:, R_BO], io["bias_row"][R_BO].partition_broadcast(P)).then_inc(bo_in, 16)
                pool.dma_start(rows[:, R_BO + 1:], io["bias_row"][R_BO + 1:].partition_broadcast(P)).then_inc(rows_in, 16)
                load_turned(pool, 0)

            @block.tensor
            def _(pe):
                pe.wait_ge(attn_in, 16)
                for k in range(NK):
                    pe_transposes(nc, attn, ps[:, k, :], k, ident).then_inc(aT_ps, 1)
                pe.wait_ge(wo_in, 16)
                pe.wait_ge(aT_ready, NK)
                for t in range(NT):
                    pe_product(nc, ps[:, 4 + t, :], lambda k: attnT[:, k, t * P:(t + 1) * P],
                               lambda k: wo[:, k, :], NK).then_inc(x1_ps, 1)
                pe.wait_ge(h_ready, NT)
                for k in range(NK):
                    pe_transposes(nc, h, ps[:, k, :], k, ident).then_inc(hT_ps, 1)
                pe.wait_ge(weights_in, 48)
                pe.wait_ge(hT_ready, NK)
                for c in range(NK):
                    pe_product(nc, ps[:, 4 + c, :], lambda k: w2k[:, k, c * P:(c + 1) * P],
                               lambda k: hT[:, k, :], NK).then_inc(k_ps, 1)
                for c in range(NK):
                    pe_product(nc, ps[:, c, :], lambda k: w2q[:, k, c * P:(c + 1) * P],
                               lambda k: hT[:, k, :], NK).then_inc(q_ps, 1)
                pe.wait_ge(emb_in, 32)
                pe.wait_ge(q_ready, NK)
                for n in range(JOBS):
                    side, m = divmod(n, JOBS // 2)
                    z, table = sides[side][:2]
                    if m == 0:
                        pe.wait_ge(z_ready, side + 1)
                    if n >= 8:
                        pe.wait_ge(act_staged if n % 2 == 0 else dve_staged, (n - 8) // 2 + 1)
                    for a in range(4):
                        b, p = divmod(4 * m + a, NP)
                        last = nc.tensor.matmul(ps[:, n % 8, a * P:(a + 1) * P],
                                                z[:, b, 2 * p:2 * p + 2, :].rearrange("p h s -> p (h s)"), emb[:, table, :],
                                                start=True, stop=True)
                    last.then_inc(rel_ps, 1)
                for t in range(NT):
                    pe.wait_ge(act_staged if t % 2 == 0 else dve_staged, (JOBS - 8 + t) // 2 + 1)
                    pe_product(nc, ps[:, t, :], lambda k: hT[:, k, t * P:(t + 1) * P],
                               lambda k: w2v[:, k, :], NK).then_inc(v_ps, 1)

            def staged(eng, copy, parity, done):
                for n in range(parity, JOBS, 2):
                    eng.wait_ge(rel_ps, n + 1)
                    if n >= SLOTS:
                        eng.wait_ge(stored[n % SLOTS], 16 * (n // SLOTS))
                    copy(stage(n % SLOTS), ps[:, n % 8]).then_inc(done, 1)

            @block.scalar
            def _(act):
                for k in range(NK):
                    act.wait_ge(aT_ps, k + 1)
                    nc.scalar.activation(attnT[:, k, :], ps[:, k, :], ACT.Identity,
                                         bias=bias[:, BV + k:BV + k + 1]).then_inc(aT_ready, 1)
                norm.scalar(nc, act)
                for c in range(NK):
                    act.wait_ge(k_ps, c + 1)
                    nc.scalar.activation(kT[:, c, :], ps[:, 4 + c, :], ACT.Identity,
                                         bias=bias[:, B2K + c:B2K + c + 1]).then_inc(k_ready, 1)
                for c in range(NK):
                    act.wait_ge(q_ps, c + 1)
                    nc.scalar.activation(qT[:, c, :], ps[:, c, :], ACT.Identity,
                                         bias=bias[:, B2Q + c:B2Q + c + 1]).then_inc(q_ready, 1)
                staged(act, nc.scalar.copy, 0, act_staged)

            @block.vector
            def _(dve):
                chain = Chain(dve, dve_done)
                dve.wait_ge(x_in, 16)
                dve.wait_ge(bo_in, 16)
                chain.link(nc.vector.tensor_tensor(
                    x1[:], x[:], rows[:, R_BO, :].unsqueeze(1).broadcast_to([P, NT, D]), ALU.add))
                for t in range(NT):
                    dve.wait_ge(x1_ps, t + 1)
                    chain.link(nc.vector.tensor_tensor(x1[:, t, :], x1[:, t, :], ps[:, 4 + t, :], ALU.add))
                norm.vector(nc, dve, chain, x1, 1e-5)
                for t in range(NT):
                    nc.vector.tensor_scalar(h[:, t, :], x1[:, t, :], norm.mom[:, t, 0:1], norm.rstd[:, t:t + 1],
                                            ALU.subtract, ALU.mult).then_inc(h_ready, 1)
                for k in range(NK):
                    dve.wait_ge(hT_ps, k + 1)
                    nc.vector.tensor_copy(hT[:, k, :], ps[:, k, :]).then_inc(hT_ready, 1)
                for z, src, ready in ((kz, kT, k_ready), (qz, qT, q_ready)):
                    for c in range(NK):
                        dve.wait_ge(ready, c + 1)
                        for j in range(4):
                            last = nc.vector.tensor_scalar_mul(
                                z[:, :, 4 * c + j, :], src[:, c, :].rearrange("p (b s) -> p b s", s=S),
                                const[:, C_HEAD32 + j:C_HEAD32 + j + 1])
                    last.then_inc(z_ready, 1)
                staged(dve, nc.vector.tensor_copy, 1, dve_staged)
                dve.wait_ge(rows_in, 16)
                for t in range(NT):
                    dve.wait_ge(v_ps, t + 1)
                    chain.link(nc.vector.tensor_tensor(v[:, t, :], ps[:, t, :], rows[:, R_B2V, :], ALU.add))
                for two in range(2):
                    nc.vector.tensor_scalar_mul(vz[:, two], v[:], const[:, C_PARITY + two:C_PARITY + two + 1])


def attention(nc, ctx, name, keep, dk, scale, rel):
    def sb(n, shape, dt=F32):
        return ctx.enter_context(nc.sbuf_tensor(f"{name}_{n}", shape, dt))

    def sem(n):
        return ctx.enter_context(nc.semaphore(f"{name}_{n}"))

    prob = keep["prob"]
    probT = keep["probT"]
    biggest, total, rtotal = (sb(n, [P, NT, 2, NP]) for n in ("biggest", "total", "rtotal"))
    ps = ctx.enter_context(nc.psum_tensor(name + "_ps", [P, 8, 512], F32))
    chain_done, s_ps, s_read, x_ready, exp_ready = map(sem, ("chain", "scores", "s_read", "shifted", "exp"))
    t_ps, t_read, o_ps, out_ready = map(sem, ("t_psum", "t_read", "o_psum", "out_ready"))
    qz, kT, vz, const, out = keep["qz"], keep["kT"], keep["vz"], keep["const"], keep["out"]
    ident = const[:, C_IDENT:C_IDENT + P]
    in_chunk = P // dk

    def tensor(pe):
        def scores(b):
            if b >= 4:
                pe.wait_ge(s_read, b - 3)
            for p in range(NP):
                for two in range(2):
                    h = 2 * p + two
                    dst = ps[two * S:(two + 1) * S, b % 4, p * S:(p + 1) * S]
                    last = nc.tensor.matmul(dst, qz[:, b, h, :], kT[:, h // in_chunk, b * S:(b + 1) * S],
                                            start=True, stop=not rel)
                    if rel:
                        if b == 0 and h == 0:
                            pe.wait_ge(keep["k_rel_in"], 32)
                        last = nc.tensor.matmul(dst, keep["k_rel"][:, b * NP + p, :],
                                                ident[:, two * S:(two + 1) * S], start=False, stop=True)
            last.then_inc(s_ps, 1)

        def outputs(t):
            pe.wait_ge(exp_ready, 2 * t + 2)
            for g in range(2):
                n = 2 * t + g
                if n >= 2:
                    pe.wait_ge(t_read, n - 1)
                for a in range(4):
                    last = nc.tensor.transpose(ps[:, 4 + g, a * P:(a + 1) * P],
                                               prob[:, t, 4 * g + a].rearrange("p b s -> p (b s)"), ident)
                last.then_inc(t_ps, 1)
            pe.wait_ge(t_read, 2 * t + 2)
            if t >= 2:
                pe.wait_ge(out_ready, 4 * (t - 1))
            for p in range(NP):
                for two in range(2):
                    h = 2 * p + two
                    last = nc.tensor.matmul(
                        ps[two * S:(two + 1) * S, 6 + t % 2, p * 2 * dk:(p + 1) * 2 * dk],
                        probT[:, t, p, two * S:(two + 1) * S], vz[:, :, t, h * dk:(h + 1) * dk],
                        start=True, stop=True)
            last.then_inc(o_ps, 1)

        for b in range(B):
            scores(b)
            if b >= 3 and b % 2:
                outputs(b // 2 - 1)
        outputs(NT - 1)

    def vector(dve):
        chain = Chain(dve, chain_done)

        def soft(b):
            t, two = divmod(b, 2)
            x = prob[:, t, :, two, :]
            dve.wait_ge(s_ps, b + 1)
            if rel:
                if b == 0:
                    dve.wait_ge(keep["q_rel_in"], 32)
                add = keep["q_rel"][:, b * NP:(b + 1) * NP, :]
            else:
                add = const[:, C_CAUSAL:C_CAUSAL + S].unsqueeze(1).broadcast_to([P, NP, S])
            ins = nc.vector.tensor_tensor(x, ps[:, b % 4].rearrange("p (a s) -> p a s", s=S), add, ALU.add)
            ins.then_inc(s_read, 1)
            dve.wait_ge(s_read, b + 1)
            big = biggest[:, t, two, :]
            chain.link(nc.vector.reduce_max(big, x, AX.X))
            nc.vector.tensor_tensor(x, x, big.unsqueeze(2).broadcast_to([P, NP, S]), ALU.subtract).then_inc(x_ready, 1)

        def sums(b):
            t, two = divmod(b, 2)
            dve.wait_ge(exp_ready, b + 1)
            chain.link(nc.vector.reduce_sum(total[:, t, two, :], prob[:, t, :, two, :], AX.X))
            chain.link(nc.vector.reciprocal(rtotal[:, t, two, :], total[:, t, two, :]))

        def outputs(t):
            dve.wait_ge(o_ps, t + 1)
            o = ps[:, 6 + t % 2, 0:NP * 2 * dk].rearrange("p (a b d) -> p a b d", b=2, d=dk)
            dst = out[:, t, :].rearrange("p (a h d) -> p a h d", h=2, d=dk)
            for h in range(2):
                for b in range(2):
                    nc.vector.tensor_tensor(
                        dst[b * S:(b + 1) * S, :, h, :], o[h * S:(h + 1) * S, :, b, :],
                        rtotal[h * S:(h + 1) * S, t, b, :].unsqueeze(2).broadcast_to([S, NP, dk]),
                        ALU.mult).then_inc(out_ready, 1)

        for b in range(B):
            soft(b)
            if b >= 1:
                sums(b - 1)
            if b >= 5 and b % 2:
                outputs(b // 2 - 2)
        sums(B - 1)
        outputs(NT - 2)
        outputs(NT - 1)

    def scalar(act):
        def exps(b):
            t, two = divmod(b, 2)
            act.wait_ge(x_ready, b + 1)
            nc.scalar.activation(prob[:, t, :, two, :], prob[:, t, :, two, :], ACT.Exp,
                                 scale=scale).then_inc(exp_ready, 1)

        def copies(t):
            for g in range(2):
                act.wait_ge(t_ps, 2 * t + g + 1)
                nc.scalar.activation(probT[:, t, 4 * g:4 * g + 4, :],
                                     ps[:, 4 + g, :].rearrange("p (a q) -> p a q", q=P), ACT.Copy).then_inc(t_read, 1)

        for b in range(B):
            exps(b)
            if b >= 3 and b % 2:
                copies(b // 2 - 1)
        copies(NT - 1)

    return tensor, scalar, vector, out_ready


def self_attention(nc, io, keep):
    with ExitStack() as ctx:
        def sb(name, shape, dt=F32):
            return ctx.enter_context(nc.sbuf_tensor("s_" + name, shape, dt))

        def sem(name):
            return ctx.enter_context(nc.semaphore("s_" + name))

        out = sb("out", [P, NT, D])
        outT, hh, wo = sb("outT", [P, NK, T]), sb("hh", [P, NT, D]), sb("wo", [P, NK, D])
        norm = Norm(nc, ctx, "s_norm")
        rows, x1, h, x2, const = keep["rows"], keep["x1"], keep["h"], keep["x2"], keep["const"]
        ident = const[:, C_IDENT:C_IDENT + P]
        with ExitStack() as inner:
            tensor, scalar, vector, _ = attention(nc, inner, "s", dict(keep, out=out), DH, SCALE, True)
            with nc.Block() as block:
                block.tensor(tensor)
                block.scalar(scalar)
                block.vector(vector)

                @block.sync
                def _(sp):
                    with nc.semaphore("s_wo_in") as wo_in:
                        sp.dma_start(wo[:], io["w2o"].rearrange("(k p) n -> p k n", p=P)).then_inc(wo_in, 16)
                        sp.wait_ge(wo_in, 16)
        ps = ctx.enter_context(nc.psum_tensor("s_ps2", [P, 8, 512], F32))
        dve_done, oT_ps, oT_ready, hh_ps = map(sem, ("dve_done", "oT_psum", "oT_ready", "hh_psum"))
        with nc.Block() as block:

            @block.tensor
            def _(pe):
                for k in range(NK):
                    pe_transposes(nc, out, ps[:, k, :], k, ident).then_inc(oT_ps, 1)
                pe.wait_ge(oT_ready, NK)
                for t in range(NT):
                    pe_product(nc, ps[:, 4 + t, :], lambda k: outT[:, k, t * P:(t + 1) * P],
                               lambda k: wo[:, k, :], NK).then_inc(hh_ps, 1)

            @block.scalar
            def _(act):
                for k in range(NK):
                    act.wait_ge(oT_ps, k + 1)
                    nc.scalar.copy(outT[:, k, :], ps[:, k, :]).then_inc(oT_ready, 1)
                norm.scalar(nc, act)

            @block.vector
            def _(dve):
                chain = Chain(dve, dve_done)

                def row(r):
                    return rows[:, r, :].unsqueeze(1).broadcast_to([P, NT, D])

                chain.link(nc.vector.tensor_tensor(hh[:], h[:], row(R_B2O), ALU.add))
                for t in range(NT):
                    dve.wait_ge(hh_ps, t + 1)
                    chain.link(nc.vector.tensor_tensor(hh[:, t, :], hh[:, t, :], ps[:, 4 + t, :], ALU.add))
                norm.vector(nc, dve, chain, hh, 1e-12)
                for t in range(NT):
                    last = nc.vector.tensor_scalar(hh[:, t, :], hh[:, t, :], norm.mom[:, t, 0:1],
                                                   norm.rstd[:, t:t + 1], ALU.subtract, ALU.mult)
                    if t < NT - 1:
                        last.then_inc(dve_done, 1)
                        chain.n += 1
                chain.link(last)
                chain.link(nc.vector.tensor_tensor(hh[:], hh[:], row(R_GAMMA), ALU.mult))
                chain.link(nc.vector.tensor_tensor(hh[:], hh[:], row(R_BETA), ALU.add))
                nc.vector.tensor_tensor(x2[:], x1[:], hh[:], ALU.add)


L = D // 2
DL = L // H
NL = L // P
E = 8
F = 2 * D
NF = F // P


def low_rank_stage(nc, io, keep):
    with ExitStack() as ctx:
        def sb(name, shape, dt=F32):
            return ctx.enter_context(nc.sbuf_tensor("l_" + name, shape, dt))

        def sem(name):
            return ctx.enter_context(nc.semaphore("l_" + name))

        down, wqk, wv = sb("down", [P, NK, L]), sb("wqk", [P, NL, 2 * L]), sb("wv", [P, NL, L])
        g, gT, cT, rot = sb("g", [P, NT, D]), sb("gT", [P, NK, T]), sb("cT", [P, NL, T]), sb("rot", [P, NT, 2 * L])
        prods = [sb(f"prod{i}", [P, NT * 2 * H, DL // 2]) for i in range(4)]
        norm, rms = Norm(nc, ctx, "l_norm"), Norm(nc, ctx, "l_rms")
        ps = ctx.enter_context(nc.psum_tensor("l_ps", [P, 8, 512], F32))
        const, rows, x2, f, kT, qz, vz = (keep[n] for n in ("const", "rows", "x2", "f", "kT", "qz", "vz"))
        ident = const[:, C_IDENT:C_IDENT + P]
        w_in, dve_done, g_ready, gT_ps, gT_ready, c_ps, c_ready, qk_ps, v_ps, v_read = map(
            sem, ("w_in", "dve_done", "g_ready", "gT_psum", "gT_ready", "c_psum", "c_ready", "qk_psum", "v_psum", "v_read"))
        rot_ready, rot_ps = sem("rot_ready"), sem("rot_psum")
        with nc.Block() as block:

            @block.sync
            def _(sp):
                sp.dma_start(down[:], io["w_down"].rearrange("(k p) n -> p k n", p=P)).then_inc(w_in, 16)
                sp.dma_start(wqk[:, :, 0:L], io["w3q"].rearrange("(k p) n -> p k n", p=P)).then_inc(w_in, 16)
                sp.dma_start(wqk[:, :, L:], io["w3k"].rearrange("(k p) n -> p k n", p=P)).then_inc(w_in, 16)
                sp.dma_start(wv[:], io["w3v"].rearrange("(k p) n -> p k n", p=P)).then_inc(w_in, 16)

            @block.tensor
            def _(pe):
                pe.wait_ge(g_ready, NT)
                for k in range(NK):
                    pe_transposes(nc, g, ps[:, k, :], k, ident).then_inc(gT_ps, 1)
                pe.wait_ge(w_in, 64)
                pe.wait_ge(gT_ready, NK)
                for c in range(NL):
                    pe_product(nc, ps[:, 4 + c, :], lambda k: down[:, k, c * P:(c + 1) * P],
                               lambda k: gT[:, k, :], NK).then_inc(c_ps, 1)
                pe.wait_ge(c_ready, NL)
                for t in range(NT):
                    pe_product(nc, ps[:, t, :], lambda k: cT[:, k, t * P:(t + 1) * P],
                               lambda k: wqk[:, k, :], NL).then_inc(qk_ps, 1)
                for t in range(NT):
                    pe_product(nc, ps[:, 6 + t // 2, (t % 2) * L:(t % 2 + 1) * L],
                               lambda k: cT[:, k, t * P:(t + 1) * P], lambda k: wv[:, k, :], NL).then_inc(v_ps, 1)
                pe.wait_ge(rot_ready, 2)
                for c in range(2 * NL):
                    pe_transposes(nc, rot, ps[:, c, :], c, ident).then_inc(rot_ps, 1)

            @block.scalar
            def _(act):
                norm.scalar(nc, act)
                rms.scalar(nc, act)
                for c in range(NL):
                    act.wait_ge(c_ps, c + 1)
                    nc.scalar.copy(cT[:, c, :], ps[:, 4 + c, :]).then_inc(c_ready, 1)
                for two in range(2):
                    act.wait_ge(v_ps, NT)
                    nc.scalar.activation(vz[:, two], ps[:, 6:8, :].rearrange("p a (b n) -> p (a b) n", n=L), ACT.Copy,
                                         scale=const[:, C_PARITY + two:C_PARITY + two + 1]).then_inc(v_read, 1)
                act.wait_ge(rot_ps, 1)
                for j in range(8):
                    nc.scalar.activation(qz[:, :, j, :], ps[:, 0, :].rearrange("p (b s) -> p b s", s=S), ACT.Copy,
                                         scale=const[:, C_HEAD16 + j:C_HEAD16 + j + 1])
                act.wait_ge(rot_ps, 2 * NL)
                nc.scalar.copy(kT[:], ps[:, 2:4, :])

            @block.vector
            def _(dve):
                chain = Chain(dve, dve_done)
                norm.vector(nc, dve, chain, x2, 1e-5)
                for t in range(NT):
                    last = nc.vector.tensor_scalar(f[:, t, :], x2[:, t, :], norm.mom[:, t, 0:1],
                                                   norm.rstd[:, t:t + 1], ALU.subtract, ALU.mult)
                    if t < NT - 1:
                        last.then_inc(dve_done, 1)
                        chain.n += 1
                chain.link(last)
                rms.vector(nc, dve, chain, f, 1e-5, about_zero=True)
                for t in range(NT):
                    nc.vector.scalar_tensor_tensor(out=g[:, t, :], in0=f[:, t, :], scalar=rms.rstd[:, t:t + 1],
                                                   in1=rows[:, R_G1, :], op0=ALU.mult, op1=ALU.mult).then_inc(g_ready, 1)
                for k in range(NK):
                    dve.wait_ge(gT_ps, k + 1)
                    nc.vector.tensor_copy(gT[:, k, :], ps[:, k, :]).then_inc(gT_ready, 1)
                dve.wait_ge(qk_ps, NT)
                pairs = ps[:, 0:NT, :].rearrange("p t n -> p (t n)").rearrange("p (h i two) -> p h i two", i=DL // 2, two=2)
                shape = [P, NT * 2 * H, DL // 2]
                for n, (part, table) in enumerate(((0, C_COS), (1, C_SIN), (0, C_SIN), (1, C_COS))):
                    last = nc.vector.tensor_tensor(prods[n][:], pairs[:, :, :, part],
                                                   const[:, table:table + DL // 2].unsqueeze(1).broadcast_to(shape), ALU.mult)
                    if n < 3:
                        last.then_inc(dve_done, 1)
                        chain.n += 1
                chain.link(last)
                turned = rot[:].rearrange("p t n -> p (t n)").rearrange("p (h i two) -> p h i two", i=DL // 2, two=2)
                nc.vector.tensor_tensor(turned[:, :, :, 0], prods[0][:], prods[1][:], ALU.subtract).then_inc(rot_ready, 1)
                nc.vector.tensor_tensor(turned[:, :, :, 1], prods[2][:], prods[3][:], ALU.add).then_inc(rot_ready, 1)
                dve.wait_ge(rot_ps, 2)
                for j in range(8):
                    nc.vector.tensor_scalar_mul(qz[:, :, 8 + j, :], ps[:, 1, :].rearrange("p (b s) -> p b s", s=S),
                                                const[:, C_HEAD16 + j:C_HEAD16 + j + 1])


def causal_attention(nc, io, keep):
    with ExitStack() as ctx:
        tensor, scalar, vector, _ = attention(nc, ctx, "c", keep, DL, float(DL) ** -0.5, False)
        with nc.Block() as block:
            block.tensor(tensor)
            block.scalar(scalar)
            block.vector(vector)


def router_stage(nc, io, keep):
    with ExitStack() as ctx:
        def sb(name, shape, dt=F32):
            return ctx.enter_context(nc.sbuf_tensor("g_" + name, shape, dt))

        def sem(name):
            return ctx.enter_context(nc.semaphore("g_" + name))

        up, router = sb("up", [P, NL, D]), sb("router", [P, NK, E])
        outT, h3, g, gT = sb("outT", [P, NL, T]), sb("h3", [P, NT, D]), sb("g", [P, NT, D]), sb("gT", [P, NK, T])
        big, total, rtotal = (sb(n, [P, NT]) for n in ("big", "total", "rtotal"))
        pr, hit = sb("pr", [P, NT, E]), sb("hit", [P, 2, NT, E])
        best, weight, which_f = sb("best", [P, NT, 8]), sb("weight", [P, NT, 2]), sb("which_f", [P, NT, 8])
        which = sb("which", [P, NT, 8], U32)
        norm = Norm(nc, ctx, "g_norm")
        ps = ctx.enter_context(nc.psum_tensor("g_ps", [P, 8, 512], F32))
        const, rows, x2, f, out, gates, t_s = (keep[n] for n in ("const", "rows", "x2", "f", "out", "gates", "t_s"))
        ident = const[:, C_IDENT:C_IDENT + P]
        w_in, dve_done, oT_ps, oT_ready, h_ps, g_ready, gT_ps, gT_ready, t_hi, logits = map(
            sem, ("w_in", "dve_done", "oT_psum", "oT_ready", "h_psum", "g_ready", "gT_psum", "gT_ready", "t_hi", "logits"))
        shifted, exp_ready = sem("shifted"), sem("exp_ready")
        with nc.Block() as block:

            @block.sync
            def _(sp):
                sp.dma_start(up[:], io["w_up"].rearrange("(k p) n -> p k n", p=P)).then_inc(w_in, 16)
                sp.dma_start(router[:], io["router"].rearrange("(k p) n -> p k n", p=P)).then_inc(w_in, 16)

            @block.tensor
            def _(pe):
                for k in range(NL):
                    pe_transposes(nc, out, ps[:, k, :], k, ident).then_inc(oT_ps, 1)
                pe.wait_ge(w_in, 32)
                pe.wait_ge(oT_ready, NL)
                for t in range(NT):
                    pe_product(nc, ps[:, 4 + t, :], lambda k: outT[:, k, t * P:(t + 1) * P],
                               lambda k: up[:, k, :], NL).then_inc(h_ps, 1)
                pe.wait_ge(g_ready, NT)
                for k in range(NK):
                    pe_transposes(nc, g, ps[:, k, :], k, ident).then_inc(gT_ps, 1)
                pe.wait_ge(gT_ready, NK)
                for t in range(NT):
                    last = pe_product(nc, ps[:, 4, t * E:(t + 1) * E], lambda k: gT[:, k, t * P:(t + 1) * P],
                                      lambda k: router[:, k, :], NK)
                last.then_inc(logits, 1)

            @block.scalar
            def _(act):
                for k in range(NL):
                    act.wait_ge(oT_ps, k + 1)
                    nc.scalar.copy(outT[:, k, :], ps[:, k, :]).then_inc(oT_ready, 1)
                norm.scalar(nc, act)
                for k in range(NK):
                    act.wait_ge(gT_ready, k + 1)
                    nc.scalar.copy(t_s[:, 0, k, :], gT[:, k, :]).then_inc(t_hi, 1)
                act.wait_ge(shifted, 1)
                nc.scalar.activation(pr[:], pr[:], ACT.Exp).then_inc(exp_ready, 1)

            @block.vector
            def _(dve):
                chain = Chain(dve, dve_done)
                for t in range(NT):
                    dve.wait_ge(h_ps, t + 1)
                    last = nc.vector.tensor_tensor(h3[:, t, :], f[:, t, :], ps[:, 4 + t, :], ALU.add)
                    if t < NT - 1:
                        last.then_inc(dve_done, 1)
                        chain.n += 1
                chain.link(last)
                norm.vector(nc, dve, chain, h3, 1e-5, about_zero=True)
                for t in range(NT):
                    nc.vector.scalar_tensor_tensor(out=g[:, t, :], in0=h3[:, t, :], scalar=norm.rstd[:, t:t + 1],
                                                   in1=rows[:, R_G2, :], op0=ALU.mult, op1=ALU.mult).then_inc(g_ready, 1)
                for k in range(NK):
                    dve.wait_ge(gT_ps, k + 1)
                    nc.vector.tensor_copy(gT[:, k, :], ps[:, k, :]).then_inc(gT_ready, 1)
                nc.vector.tensor_tensor(x2[:], x2[:], h3[:], ALU.add)
                for k in range(NK):
                    dve.wait_ge(t_hi, k + 1)
                    nc.vector.tensor_tensor(t_s[:, 1, k, :], gT[:, k, :], t_s[:, 0, k, :].bitcast(F32), ALU.subtract)
                dve.wait_ge(logits, 1)
                lg = ps[:, 4, 0:NT * E].rearrange("p (t e) -> p t e", e=E)
                chain.link(nc.vector.reduce_max(big[:], lg, AX.X))
                nc.vector.tensor_tensor(pr[:], lg, big[:].unsqueeze(2).broadcast_to([P, NT, E]), ALU.subtract).then_inc(shifted, 1)
                dve.wait_ge(exp_ready, 1)
                chain.link(nc.vector.reduce_sum(total[:], pr[:], AX.X))
                chain.link(nc.vector.reciprocal(rtotal[:], total[:]))
                chain.link(nc.vector.tensor_tensor(pr[:], pr[:], rtotal[:].unsqueeze(2).broadcast_to([P, NT, E]), ALU.mult))
                for t in range(NT):
                    chain.link(nc.vector.max(best[:, t, :], pr[:, t, :]))
                    chain.link(nc.vector.max_index(which[:, t, :], best[:, t, :], pr[:, t, :]))
                chain.link(nc.vector.tensor_copy(which_f[:], which[:]))
                chain.link(nc.vector.tensor_tensor(total[:], best[:, :, 0], best[:, :, 1], ALU.add))
                chain.link(nc.vector.reciprocal(rtotal[:], total[:]))
                chain.link(nc.vector.tensor_tensor(weight[:], best[:, :, 0:2], rtotal[:].unsqueeze(2).broadcast_to([P, NT, 2]),
                                                   ALU.mult))
                for t in range(NT):
                    for n in range(2):
                        chain.link(nc.vector.tensor_scalar(hit[:, n, t, :], const[:, C_IOTA:C_IOTA + E],
                                                           which_f[:, t, n:n + 1], weight[:, t, n:n + 1],
                                                           ALU.is_equal, ALU.mult))
                nc.vector.tensor_tensor(gates[:], hit[:, 0], hit[:, 1], ALU.add)


PIECE = 1024
N13, N2 = 2 * NK, NF // 2
SLOTS_W = 6


def expert_steps(more):
    out = []
    for fc in range(NF):
        out.append(("H", fc))
        if fc < N2:
            out.append(("W2", fc))
    pieces = [("W13", i) for i in range(N13)] if more else []
    return out + pieces[:2] + [("Y", 0)] + pieces[2:5] + [("Y", 1)] + pieces[5:] + [("Y", 2), ("Y", 3)]


def experts(nc, io, keep):
    with ExitStack() as ctx:
        def sb(name, shape, dt=F32):
            return ctx.enter_context(nc.sbuf_tensor("e_" + name, shape, dt))

        def sem(name):
            return ctx.enter_context(nc.semaphore("e_" + name))

        raw = sb("raw", [P, SLOTS_W, PIECE])
        w13 = sb("w13", [P, 2, N13, PIECE], F32R)
        w2 = sb("w2", [P, 2, NF, D], F32R)
        hid = sb("hid", [P, 2, NF, T], F32R)
        gated = sb("gated", [P, 2, T])
        full = sb("full", [P, 2, T])
        ps_h = ctx.enter_context(nc.psum_tensor("e_ps_h", [P, 4, 512], F32))
        ps_y = ctx.enter_context(nc.psum_tensor("e_ps_y", [P, NT, 512], F32))
        y, gates, t_s = keep["x2"], keep["gates"], keep["t_s"]
        staged = [sem(f"staged{i}") for i in range(SLOTS_W)]
        w_hi, w_lo, h_ps, silu_ready, full_ready, hid_hi, hid_lo, y_ps, y_read, stored = map(
            sem, ("w_hi", "w_lo", "h_psum", "silu_ready", "full_ready", "hid_hi", "hid_lo", "y_psum", "y_read", "stored"))
        PIECES = N13 + N2

        def source(e, i):
            if i < NK:
                return io["w1"][e, i * P:(i + 1) * P, :]
            if i < N13:
                return io["w3"][e, (i - NK) * P:(i - NK + 1) * P, :]
            i -= N13
            return io["w2"][e, 2 * i * P:2 * (i + 1) * P, :].rearrange("(two p) n -> p two n", p=P)

        def halves(i, half):
            if i < N13:
                return w13[:, half, i, :]
            return w2[:, half, 2 * (i - N13):2 * (i - N13) + 2, :].rearrange("p a n -> p (a n)")

        def loop(eng, first, body):
            first()
            with eng.Fori(0, E - 1) as e:
                body(e, True)
            body(E - 1, False)

        with nc.Block() as block:

            @block.sync
            def _(sp):
                def load(e, i, wait=True):
                    slot = i % SLOTS_W
                    if wait:
                        sp.wait_ge(w_lo, PIECES * e + i - SLOTS_W + 1)
                    dst = raw[:, slot] if i < N13 else raw[:, slot].rearrange("p (a n) -> p a n", a=2)
                    sp.dma_start(dst, source(e, i)).then_inc(staged[slot], 16)

                for i in range(PIECES):
                    load(0, i, wait=i >= SLOTS_W)
                with sp.Fori(1, E) as e:
                    for i in range(PIECES):
                        load(e, i)
                sp.wait_ge(y_read, NT * E)
                sp.dma_start(io["out"].rearrange("(t two) s d -> (two s) t d", two=2), y[:]).then_inc(stored, 16)
                sp.wait_ge(stored, 16)

            def piece(eng, e, i):
                eng.wait_ge(staged[i % SLOTS_W], 32 * e + (16 if i < SLOTS_W else 32))

            @block.scalar
            def _(act):
                def high(e, i):
                    piece(act, e, i)
                    nc.scalar.copy(halves(i, 0), raw[:, i % SLOTS_W]).then_inc(w_hi, 1)

                def first():
                    for i in range(N13):
                        high(0, i)

                def body(e, more):
                    for s in expert_steps(more):
                        if s[0] == "H":
                            fc = s[1]
                            act.wait_ge(h_ps, 2 * (NF * e + fc) + 1)
                            nc.scalar.activation(gated[:, fc % 2, :], ps_h[:, 2 * (fc % 2), :], ACT.Silu).then_inc(silu_ready, 1)
                            act.wait_ge(full_ready, NF * e + fc + 1)
                            nc.scalar.copy(hid[:, 0, fc, :], full[:, fc % 2, :]).then_inc(hid_hi, 1)
                        elif s[0] == "W2":
                            high(e, N13 + s[1])
                        elif s[0] == "W13":
                            if s[1] == 0:
                                act.wait_ge(h_ps, 2 * NF * (e + 1))
                            high(e + 1, s[1])

                loop(act, first, body)

            @block.vector
            def _(dve):
                def low(e, i):
                    dve.wait_ge(w_hi, PIECES * e + i + 1)
                    nc.vector.tensor_tensor(halves(i, 1), raw[:, i % SLOTS_W], halves(i, 0).bitcast(F32),
                                            ALU.subtract).then_inc(w_lo, 1)

                def first():
                    for i in range(N13):
                        low(0, i)

                def body(e, more):
                    for s in expert_steps(more):
                        if s[0] == "H":
                            fc = s[1]
                            dve.wait_ge(h_ps, 2 * (NF * e + fc) + 2)
                            dve.wait_ge(silu_ready, NF * e + fc + 1)
                            nc.vector.tensor_tensor(full[:, fc % 2, :], gated[:, fc % 2, :], ps_h[:, 2 * (fc % 2) + 1, :],
                                                    ALU.mult).then_inc(full_ready, 1)
                            dve.wait_ge(hid_hi, NF * e + fc + 1)
                            nc.vector.tensor_tensor(hid[:, 1, fc, :], full[:, fc % 2, :], hid[:, 0, fc, :].bitcast(F32),
                                                    ALU.subtract).then_inc(hid_lo, 1)
                        elif s[0] == "W2":
                            low(e, N13 + s[1])
                        elif s[0] == "W13":
                            low(e + 1, s[1])
                        else:
                            t = s[1]
                            dve.wait_ge(y_ps, NT * e + t + 1)
                            nc.vector.scalar_tensor_tensor(out=y[:, t, :], in0=ps_y[:, t, :],
                                                           scalar=gates[:, t, bass.ds(e, 1)], in1=y[:, t, :],
                                                           op0=ALU.mult, op1=ALU.add).then_inc(y_read, 1)
                            dve.wait_ge(y_read, NT * e + t + 1)

                loop(dve, first, body)

            @block.tensor
            def _(pe):
                def three(out, a, b, start, stop):
                    for n, (i, j) in enumerate(((1, 0), (0, 1), (0, 0))):
                        last = nc.tensor.matmul(out, a(i), b(j), start=(start and n == 0), stop=(stop and n == 2))
                    return last

                def body(e, more):
                    for s in expert_steps(more):
                        if s[0] == "H":
                            fc = s[1]
                            if fc == 0:
                                pe.wait_ge(w_lo, PIECES * e + N13)
                            if fc >= 2:
                                pe.wait_ge(full_ready, NF * e + fc - 1)
                            for side in range(2):
                                for k in range(NK):
                                    last = three(ps_h[:, 2 * (fc % 2) + side, :],
                                                 lambda i: w13[:, i, side * NK + k, fc * P:(fc + 1) * P],
                                                 lambda i: t_s[:, i, k, :], k == 0, k == NK - 1)
                                last.then_inc(h_ps, 1)
                        elif s[0] == "Y":
                            t = s[1]
                            if t == 0:
                                pe.wait_ge(w_lo, PIECES * (e + 1))
                            for fc in range(NF):
                                if t == 0:
                                    pe.wait_ge(hid_lo, NF * e + fc + 1)
                                last = three(ps_y[:, t, :], lambda i: hid[:, i, fc, t * P:(t + 1) * P],
                                             lambda i: w2[:, i, fc, :], fc == 0, fc == NF - 1)
                            last.then_inc(y_ps, 1)

                loop(pe, lambda: None, body)


INPUTS = ("x", "ctxT", "mask", "wqT", "wkT", "wvT", "woT", "bias_col", "bias_row", "const",
          "w2q", "w2k", "w2v", "w2o", "emb_fwd", "emb_rev",
          "w_down", "w3q", "w3k", "w3v", "w_up", "router", "w1", "w2", "w3")


def build(nc, io):
    with ExitStack() as ctx:
        def sb(name, shape, dt=F32):
            return ctx.enter_context(nc.sbuf_tensor(name, shape, dt))

        keep = {"const": sb("const", [P, C_ALL]), "bias": sb("bias", [P, B_ALL])}
        with ExitStack() as first:
            keep["wk"] = first.enter_context(nc.sbuf_tensor("wk_s", [P, 2, NK, D], F32R))
            keep["wv"] = first.enter_context(nc.sbuf_tensor("wv_s", [P, 2, NK, D], F32R))
            query_stage(nc, io, keep)
            cross_attention(nc, io, keep)
        keep["rows"] = sb("rows", [P, R_ALL, D])
        keep["x2"] = sb("x2", [P, NT, D])
        with ExitStack() as second:
            for n, shape in (("x1", [P, NT, D]), ("h", [P, NT, D]), ("kT", [P, NK, T]), ("qz", [P, B, H, S]),
                             ("vz", [P, 2, NT, D]), ("kz", [P, B, H, S])):
                keep[n] = second.enter_context(nc.sbuf_tensor(n, shape, F32))
            for n in ("q_rel", "k_rel"):
                keep[n] = second.enter_context(nc.sbuf_tensor(n, [P, B * NP, S], F32))
                keep[n + "_in"] = second.enter_context(nc.semaphore(n + "_in"))
            project_stage(nc, io, keep)
            keep["prob"] = keep["kz"][:, 0:B // 2].rearrange("p t h s -> p (t h s)").rearrange("p (t a two s) -> p t a two s", a=NP, two=2, s=S)
            keep["probT"] = keep["kz"][:, B // 2:].rearrange("p t h s -> p (t h s)").rearrange(
                "p (t a q) -> p t a q", a=NP, q=P)
            self_attention(nc, io, keep)
        keep["t_s"] = sb("t_s", [P, 2, NK, T], F32R)
        keep["gates"] = sb("gates", [P, NT, E])
        with ExitStack() as fourth:
            for n, shape in (("f", [P, NT, D]), ("kT", [P, NL, T]), ("qz", [P, B, H, S]), ("vz", [P, 2, NT, L]),
                             ("out", [P, NT, L]), ("prob", [P, NT, NP, 2, S]), ("probT", [P, NT, NP, P])):
                keep[n] = fourth.enter_context(nc.sbuf_tensor("c_" + n, shape, F32))
            low_rank_stage(nc, io, keep)
            causal_attention(nc, io, keep)
            router_stage(nc, io, keep)
        experts(nc, io, keep)


def kernel(**inputs):
    import concourse.bacc as bacc
    from concourse.bass_utils import run_bass_kernel_spmd as run

    a = {k: np.asarray(v) for k, v in inputs.items()}

    def columns(name):
        return a[name].reshape(-1, P).T

    emb = a["L0_attn_dist_emb"]
    laid_out = {
        "x": a["x"].reshape(T, D),
        "ctxT": np.pad(a["ctx_1024"].transpose(0, 2, 1), ((0, 0), (0, 0), (0, KPAD - KEYS))),
        "mask": a["mask_Bx1xSxS2_ik1"].reshape(B, S, KEYS),
        "wqT": a["L0_xattn_WQ_w"].T, "wkT": a["L0_xattn_WK_w"].T, "wvT": a["L0_xattn_WV_w"].T,
        "woT": a["L0_xattn_WO_w"].T,
        "bias_col": np.concatenate([columns(n) for n in ("L0_xattn_WQ_b", "L0_xattn_WK_b", "L0_xattn_WV_b",
                                                        "L0_attn_bq", "L0_attn_bk")], axis=1),
        "bias_row": np.stack([a[n] for n in ("L0_xattn_WO_b", "L0_attn_bv", "L0_attn_bo", "L0_attn_ln_gamma",
                                            "L0_attn_ln_beta", "L0_ffn_g1", "L0_ffn_g2")]),
        "w2q": a["L0_attn_Wq"], "w2k": a["L0_attn_Wk"], "w2v": a["L0_attn_Wv"], "w2o": a["L0_attn_Wo"],
        "emb_fwd": np.tile(emb[EMB_BASE:EMB_BASE + P].T, (4, 1)),
        "emb_rev": np.tile(emb[EMB_BASE - 1:EMB_BASE - 1 + P][::-1].T, (4, 1)),
        "w_down": a["L0_ffn_w_down"], "w3q": a["L0_ffn_wq"], "w3k": a["L0_ffn_wk"], "w3v": a["L0_ffn_wv"],
        "w_up": a["L0_ffn_w_up"], "router": a["L0_ffn_router_w"],
        "w1": a["L0_ffn_w1"], "w2": a["L0_ffn_w2"], "w3": a["L0_ffn_w3"],
        "const": constants(),
    }
    nc = bacc.Bacc("TRN2", target_bir_lowering=False, num_devices=1)
    io, arrays = {}, {}
    for name, value in laid_out.items():
        value = np.ascontiguousarray(value)
        arrays["in_" + name] = value
        io[name] = nc.dram_tensor("in_" + name, value.shape, mybir.dt.from_np(value.dtype), kind="ExternalInput").ap()
    io["qT"] = nc.dram_tensor("scratch_qT", (P, NK, T), F32, kind="Internal").ap()
    io["attn"] = nc.dram_tensor("scratch_attn", (B, S, D), F32, kind="Internal").ap()
    for n in ("q_rel", "k_rel"):
        io[n] = nc.dram_tensor("scratch_" + n, (B * NP, P, P), F32, kind="Internal").ap()
    io["out"] = nc.dram_tensor("out", (B, S, D), F32, kind="ExternalOutput").ap()
    build(nc, io)
    result = run(nc, [arrays], core_ids=[0])
    return result.results[0]["out"]
```

```python
from contextlib import ExitStack

import numpy as np

import concourse.bass as bass
from concourse import mybir

F32 = mybir.dt.float32
F32R = mybir.dt.float32r
F16 = mybir.dt.float16
BF16 = mybir.dt.bfloat16
I32 = mybir.dt.int32
U32 = mybir.dt.uint32
ALU = mybir.AluOpType
ACT = mybir.ActivationFunctionType
AX = mybir.AxisListType

P = 128
B, S, D = 8, 64, 512
T = B * S
NT = T // P
NK = D // P
KEYS = 1601
H = 16
NP = H // 2
DH = D // H
KC = 402
NC = 4
KPAD = NC * KC
NKT = -(-KEYS // P)
TAIL = KEYS - (NKT - 1) * P
SCALE = float(DH) ** -0.5
MASKED = 1e-9 / SCALE
LOWEST = -3.0e38
V_SCALE = 16.0
P_SCALE = 32768.0

C_IDENT = 0
C_HEAD32 = C_IDENT + P
C_HEAD16 = C_HEAD32 + 4
C_PARITY = C_HEAD16 + 8
C_COS = C_PARITY + 2
C_SIN = C_COS + 8
C_CAUSAL = C_SIN + 8
C_IOTA = C_CAUSAL + S
C_ALL = C_IOTA + 8


def constants():
    c = np.zeros((P, C_ALL), np.float32)
    p = np.arange(P)
    c[:, C_IDENT:C_IDENT + P] = np.eye(P)
    c[:, C_HEAD32:C_HEAD32 + 4] = p[:, None] // 32 == np.arange(4)
    c[:, C_HEAD16:C_HEAD16 + 8] = p[:, None] // 16 == np.arange(8)
    c[:, C_PARITY:C_PARITY + 2] = p[:, None] // S == np.arange(2)
    freq = (1.0 / np.float32(10000.0) ** (np.arange(0, 16, 2, dtype=np.float32) / 16)).astype(np.float32)
    ang = (p % S).astype(np.float32)[:, None] * freq
    c[:, C_COS:C_COS + 8] = np.cos(ang)
    c[:, C_SIN:C_SIN + 8] = np.sin(ang)
    c[:, C_CAUSAL:C_CAUSAL + S] = np.where(np.arange(S) <= (p % S)[:, None], 0.0, -1.0e30)
    c[:, C_IOTA:C_IOTA + 8] = np.arange(8)
    return c


class Chain:

    def __init__(self, eng, sem):
        self.eng, self.sem, self.n = eng, sem, 0

    def step(self, ins):
        self.n += 1
        ins.then_inc(self.sem, 1)

    def wait(self):
        self.eng.wait_ge(self.sem, self.n)

    def link(self, ins):
        self.step(ins)
        self.wait()


CTX_SLOTS = 3


def load_context(sp, io, keep, b, j, slot):
    ctxT = io["ctxT"].rearrange("b (k p) s -> b p k s", p=P)
    sp.dma_start(keep["ctx_raw"][:, slot], ctxT[b, :, :, j * KC:(j + 1) * KC]).then_inc(keep["ctx_in"][slot], 16)


def context_high(nc, act, keep, b, j):
    slot = j % CTX_SLOTS
    act.wait_ge(keep["ctx_in"][slot], b * 16 + 16 if slot else b * 32 + (16 if j == 0 else 32))
    nc.scalar.activation(keep["ctx_s"][:, 0, :, j * KC:(j + 1) * KC], keep["ctx_raw"][:, slot],
                         ACT.Copy).then_inc(keep["ctx_hi"], 1)


def context_low(eng, ins, keep, b, j):
    eng.wait_ge(keep["ctx_hi"], b * NC + j + 1)
    ctx_s, cols = keep["ctx_s"], slice(j * KC, (j + 1) * KC)
    ins.tensor_tensor(ctx_s[:, 1, :, cols], keep["ctx_raw"][:, j % CTX_SLOTS], ctx_s[:, 0, :, cols].bitcast(F32),
                      ALU.subtract).then_inc(keep["ctx_ready"][j], 1)


def query_stage(nc, io, keep):
    with ExitStack() as ctx:
        def sb(name, shape, dt=F32):
            return ctx.enter_context(nc.sbuf_tensor("q_" + name, shape, dt))

        def sem(name):
            return ctx.enter_context(nc.semaphore("q_" + name))

        x = sb("x", [P, NT, D])
        xn = sb("xn", [P, NT, D])
        xnT = sb("xnT", [P, NK, T])
        qT = keep["qT"]
        wq = sb("wq", [P, NK, D])
        wk = sb("wk", [P, NK, D])
        wv = sb("wv", [P, NK, D])
        stats = sb("stats", [P, NT, 6])
        mom = sb("mom", [P, NT, 2])
        std = sb("std", [P, NT])
        rstd = sb("rstd", [P, NT])
        ps = ctx.enter_context(nc.psum_tensor("q_ps", [P, 8, 512], F32))
        const, bias = keep["const"], keep["bias"]
        x_in, wq_in, wk_in, wv_in, const_in = map(sem, ("x_in", "wq_in", "wk_in", "wv_in", "const_in"))
        dve_done, var_ready, std_ready, xn_ready = map(sem, ("dve_done", "var_ready", "std_ready", "xn_ready"))
        xnT_ps, xnT_ready, q_ps, q_ready = map(sem, ("xnT_ps", "xnT_ready", "q_psum", "q_ready"))
        w_hi = sem("w_hi")
        with nc.Block() as block:

            @block.sync
            def _(sp):
                sp.dma_start(x[:], io["x"].rearrange("(t p) d -> p t d", p=P)).then_inc(x_in, 16)
                sp.dma_start(const[:], io["const"]).then_inc(const_in, 16)
                sp.dma_start(bias[:], io["bias_col"]).then_inc(const_in, 16)
                sp.dma_start(wq[:], io["wqT"].rearrange("(k p) n -> p k n", p=P)).then_inc(wq_in, 16)
                sp.dma_start(wk[:], io["wkT"].rearrange("(k p) n -> p k n", p=P)).then_inc(wk_in, 16)
                sp.dma_start(wv[:], io["wvT"].rearrange("(k p) n -> p k n", p=P)).then_inc(wv_in, 16)
                for j in range(CTX_SLOTS):
                    load_context(sp, io, keep, 0, j, j)
                for c in range(NK):
                    sp.wait_ge(q_ready, c + 1)
                    sp.dma_start(io["qT"][:, c, :], qT[:, c, :]).then_inc(keep["q_out"], 16)

            @block.vector
            def _(dve):
                chain = Chain(dve, dve_done)
                dve.wait_ge(x_in, 16)
                for t in range(NT):
                    chain.step(nc.vector.bn_stats(stats[:, t, :], x[:, t, :]))
                chain.wait()
                for t in range(NT):
                    chain.step(nc.vector.bn_aggr(mom[:, t, :], stats[:, t, :]))
                chain.wait()
                nc.vector.tensor_scalar_add(std[:], mom[:, :, 1], 1e-5).then_inc(var_ready, 1)
                dve.wait_ge(std_ready, 1)
                chain.link(nc.vector.reciprocal(rstd[:], std[:]))
                for t in range(NT):
                    nc.vector.tensor_scalar(xn[:, t, :], x[:, t, :], mom[:, t, 0:1], rstd[:, t:t + 1],
                                            ALU.subtract, ALU.mult).then_inc(xn_ready, 1)
                for k in range(NK):
                    dve.wait_ge(xnT_ps, k + 1)
                    nc.vector.tensor_copy(xnT[:, k, :], ps[:, k, :]).then_inc(xnT_ready, 1)
                for n, (w, hl) in enumerate(((wk, keep["wk"]), (wv, keep["wv"]))):
                    dve.wait_ge(w_hi, n + 1)
                    chain.link(nc.vector.tensor_tensor(hl[:, 1], w[:], hl[:, 0].bitcast(F32), ALU.subtract))
                for j in range(CTX_SLOTS):
                    context_low(dve, nc.vector, keep, 0, j)

            @block.scalar
            def _(act):
                act.wait_ge(var_ready, 1)
                nc.scalar.activation(std[:], std[:], ACT.Sqrt).then_inc(std_ready, 1)
                act.wait_ge(wk_in, 16)
                nc.scalar.activation(keep["wk"][:, 0], wk[:], ACT.Copy).then_inc(w_hi, 1)
                act.wait_ge(wv_in, 16)
                nc.scalar.activation(keep["wv"][:, 0], wv[:], ACT.Copy).then_inc(w_hi, 1)
                act.wait_ge(const_in, 32)
                for c in range(NK):
                    if c < CTX_SLOTS:
                        context_high(nc, act, keep, 0, c)
                    act.wait_ge(q_ps, c + 1)
                    nc.scalar.activation(qT[:, c, :], ps[:, 4 + c, :], ACT.Identity,
                                         bias=bias[:, BQ + c:BQ + c + 1]).then_inc(q_ready, 1)

            @block.tensor
            def _(pe):
                pe.wait_ge(const_in, 32)
                pe.wait_ge(xn_ready, NT)
                for k in range(NK):
                    for t in range(NT):
                        last = nc.tensor.transpose(ps[:, k, t * P:(t + 1) * P], xn[:, t, k * P:(k + 1) * P],
                                                   const[:, C_IDENT:C_IDENT + P])
                    last.then_inc(xnT_ps, 1)
                pe.wait_ge(wq_in, 16)
                pe.wait_ge(xnT_ready, NK)
                for c in range(NK):
                    for k in range(NK):
                        last = nc.tensor.matmul(ps[:, 4 + c, :], wq[:, k, c * P:(c + 1) * P], xnT[:, k, :],
                                                start=(k == 0), stop=(k == NK - 1))
                    last.then_inc(q_ps, 1)


BQ, BK, BV, B2Q, B2K = 0, 4, 8, 12, 16
B_ALL = 20


NG = -(-NKT // 4)
EARLY = 4
KEYS_AHEAD = [("K", 0, j) for j in range(NC)] + [("K", 1, j) for j in range(NC - 1)]
FIRST_STEPS = (KEYS_AHEAD[:NC] + [("V", 0), ("S", 0), ("V", 1), ("M", 0), ("V", 2), ("E", 0), ("V", 3)]
               + KEYS_AHEAD[NC:])


def pair_steps(p, between, after):
    a = p - 1
    mark, at = ("", p) if p < NP else ("'", 0)
    before = [("PV", a - 1, g) for g in range(1, NG)] + [("O", a - 1)] if a else []
    ahead = {5: [("C", 2)], 6: [("C", 3)], 7: [("Q",)]}.get(p, [])
    middle = [("PT", a, 1), ("PV", a, 0), ("PT", a, 2), ("PT", a, 3)]
    if p == NP:
        rest = between + middle + [("M" + mark, at), ("E" + mark, at)]
    elif ahead:
        rest = ahead + between + middle[:1] + [("M" + mark, at)] + middle[1:] + [("E" + mark, at)]
    else:
        rest = [("M" + mark, at)] + between + middle[:1] + [("E" + mark, at)] + middle[1:]
    return [("S" + mark, at)] + before + [("PT", a, 0)] + rest + after


def batch_steps(more):
    out = []
    for p in range(1, NP + 1):
        c = (p + 1) // 2
        between = [("K", c % NK, NC - 1), ("K", (c + 1) % NK, 0)] if p % 2 else [("K", (c + 1) % NK, 1), ("K", (c + 1) % NK, 2)]
        after = {3: [("C", 0)], 4: [("C", 1)], 7: [("A",)]}.get(p, [])
        if p == 1:
            between = [("V", 4), ("V", 5)] + between + [("V", 6), ("V", 7)]
            after = [("V", kt) for kt in range(8, NKT)]
        out += pair_steps(p, between, after)
    p = NP - 1
    out += [("PV", p, 1), ("V'", 0), ("PV", p, 2), ("V'", 1), ("PV", p, 3), ("O", p), ("V'", 2), ("V'", 3)]
    ahead = ("C", "Q", "A", "S'", "M'", "E'", "V'")
    return [s for s in out if more or not (s[0] in ahead or s in KEYS_AHEAD)]


def jobs(steps):
    return [s for s in steps if s[0] in ("V", "V'", "K", "PT")]


RING = 3
FIRST_JOBS = len(jobs(FIRST_STEPS))
JOB_INDEX = {more: {s: n for n, s in enumerate(jobs(batch_steps(more)))} for more in (True, False)}
NJ = len(JOB_INDEX[True])
SKIPS = [JOB_INDEX[True][("V", kt)] for kt in (EARLY + 3, EARLY + 6)][:-NJ % RING]


def job_bank(n):
    return (n + sum(n >= m for m in SKIPS)) % RING


def bank_user(n):
    before = (n - d for d in range(1, NJ))
    return next(m for m in before if job_bank(m % NJ) == job_bank(n))


def cross_attention(nc, io, keep):
    with ExitStack() as ctx:
        def sb(name, shape, dt=F32):
            return ctx.enter_context(nc.sbuf_tensor("x_" + name, shape, dt))

        def sem(name):
            return ctx.enter_context(nc.semaphore("x_" + name))

        SLOTS, ctx_s, ctx_ready = CTX_SLOTS, keep["ctx_s"], keep["ctx_ready"]
        kT = sb("kT", [P, 2, 2, KPAD], F32R)
        v = sb("v", [P, 2, NKT, D], F16)
        prob = sb("prob", [P, 2, KPAD])
        probT = sb("probT", [P, 2, NKT, P], F16)
        q_raw = sb("q_raw", [P, NK, S])
        q_s = sb("q_s", [P, 2, H, S], F32R)
        mask_raw = sb("mask_raw", [P, KEYS], I32)
        mask01 = sb("mask01", [P, KPAD], BF16)
        mask_add = sb("mask_add", [P, KPAD])
        out_b = sb("out_b", [S, D])
        biggest = sb("biggest", [P, 2])
        negmax = sb("negmax", [P, 2])
        total = sb("total", [P, 2])
        rtotal = sb("rtotal", [P, 2])
        ps_s = ctx.enter_context(nc.psum_tensor("x_ps_s", [P, NC, 512], F32))
        ring = ctx.enter_context(nc.psum_tensor("x_ring", [P, RING, 512], F32))
        ps_o = ctx.enter_context(nc.psum_tensor("x_ps_o", [P, 512], F32))
        q_in, mask_in, out_stored, out_free = map(sem, ("q_in", "mask_in", "out_stored", "out_free"))
        mask_ready, q_hi, q_ready = map(sem, ("mask_ready", "q_hi", "q_ready"))
        scores, scores_read, max_done, max_ready, exp_done = map(
            sem, ("scores", "scores_read", "max_done", "max_ready", "exp_done"))
        job_done, job_hi, job_lo = map(sem, ("job_done", "job_hi", "job_lo"))
        o_done, o_read, rtotal_ready, total_scaled, pads = map(
            sem, ("o_done", "o_read", "rtotal_ready", "total_scaled", "pads"))
        const, bias = keep["const"], keep["bias"]
        wk, wv = keep["wk"], keep["wv"]
        ident = const[:, C_IDENT:C_IDENT + P]

        def jobs_before(b, step, more=True):
            return FIRST_JOBS + b * NJ + JOB_INDEX[more][step]

        def tile_keys(kt):
            return P if kt < NKT - 1 else TAIL

        def group(g):
            return range(4 * g, min(4 * g + 4, NKT))

        with nc.Block() as block:

            def first_steps(job, steps):
                n = 0
                for s in FIRST_STEPS:
                    if s[0] in steps:
                        steps[s[0]](0, s[1])
                    elif s[0] in ("K", "V"):
                        job(n)[s[0]](ring[:, (n - FIRST_JOBS) % RING], *s[1:])
                        n += 1

            def batches(eng, first, body):
                first()
                with eng.Fori(0, B - 1) as b:
                    body(b, True)
                body(B - 1, False)

            @block.sync
            def _(sp):
                def context(b, j, slot):
                    load_context(sp, io, keep, b, j, slot)

                def small(b):
                    sp.dma_start(q_raw[:], io["qT"][:, :, bass.ds(b * S, S)]).then_inc(q_in, 16)

                def mask(b):
                    for half in range(2):
                        sp.dma_start(mask_raw[half * S:(half + 1) * S, :], io["mask"][b, :, :]).then_inc(mask_in, 16)

                for j in range(SLOTS, NC):
                    sp.wait_ge(ctx_ready[j - SLOTS], 1)
                    context(0, j, j % SLOTS)
                sp.wait_ge(keep["q_out"], 16 * NK)
                small(0)
                mask(0)
                sp.sem_inc(out_free, 1)
                with sp.Fori(0, B - 1) as b:
                    for j in range(SLOTS):
                        sp.wait_ge(ctx_ready[j if j else NC - 1], b + 1)
                        context(b + 1, j, j)
                    sp.wait_ge(q_ready, b + 1)
                    small(b + 1)
                    sp.wait_ge(mask_ready, 2 * b + 2)
                    mask(b + 1)
                    sp.wait_ge(ctx_ready[0], b + 2)
                    context(b + 1, NC - 1, 0)
                    sp.wait_ge(o_read, 2 * NP * b + 2 * NP)
                    sp.dma_start(io["attn"][b, :, :], out_b[:]).then_inc(out_stored, 16)
                    sp.wait_ge(out_stored, 16 * b + 16)
                    sp.sem_inc(out_free, 1)
                sp.wait_ge(o_read, 2 * NP * B)
                sp.dma_start(io["attn"][B - 1, :, :], out_b[:]).then_inc(out_stored, 16)
                sp.wait_ge(out_stored, 16 * B)

            POOL_PIECES = (0, 1)

            @block.gpsimd
            def _(pool):
                with pool.Fori(1, B) as b:
                    for j in POOL_PIECES:
                        context_low(pool, nc.gpsimd, keep, b, j)

            @block.scalar
            def _(act):
                def queries(b):
                    act.wait_ge(q_in, 16 * b + 16)
                    for h in range(4):
                        nc.scalar.activation(q_s[:, 0, h::4, :], q_raw[:], ACT.Copy,
                                             scale=const[:, C_HEAD32 + h:C_HEAD32 + h + 1]).then_inc(q_hi, 1)

                def keys(bank, c, j):
                    nc.scalar.activation(kT[:, c % 2, 0, j * KC:(j + 1) * KC], bank[:, 0:KC], ACT.Identity,
                                         bias=bias[:, BK + c:BK + c + 1]).then_inc(job_hi, 1)

                def values(bank, kt):
                    n = tile_keys(kt)
                    nc.scalar.activation(v[0:n, 0, kt, :], bank[0:n, :], ACT.Copy, scale=V_SCALE).then_inc(job_hi, 1)

                def exponentials(b, p):
                    act.wait_ge(max_ready, NP * b + p + 1)
                    nc.scalar.activation(prob[:, p % 2, :], prob[:, p % 2, :], ACT.Exp,
                                         bias=negmax[:, p % 2:p % 2 + 1], scale=SCALE,
                                         accum_out=total[:, p % 2:p % 2 + 1]).then_inc(exp_done, 1)

                def first():
                    def job(n):
                        if n == 1:
                            for j in range(SLOTS, NC):
                                context_high(nc, act, keep, 0, j)
                        if n == 2:
                            queries(0)
                        act.wait_ge(job_done, n + 1)
                        return {"K": keys, "V": values}

                    first_steps(job, {"E": exponentials})

                def body(b, more):
                    for s in batch_steps(more):
                        if s in JOB_INDEX[more]:
                            act.wait_ge(job_done, jobs_before(b, s, more) + 1)
                            bank = ring[:, job_bank(JOB_INDEX[more][s])]
                        if s[0] == "K":
                            keys(bank, s[1], s[2])
                        elif s[0] in ("V", "V'"):
                            values(bank, s[1])
                        elif s[0] == "PT":
                            _, p, g = s
                            n = tile_keys(group(g)[0]) if len(group(g)) == 1 else P
                            w = P * len(group(g))
                            nc.scalar.activation(probT[0:n, 0, 4 * g:4 * g + len(group(g)), :],
                                                 bank[0:n, 0:w].rearrange("p (a c) -> p a c", c=P), ACT.Copy,
                                                 scale=P_SCALE).then_inc(job_hi, 1)
                        elif s[0] == "C":
                            act.wait_ge(job_done, jobs_before(b, ("K", NK - 1, s[1])) + 1)
                            context_high(nc, act, keep, b + 1, s[1])
                        elif s[0] == "Q":
                            act.wait_ge(scores, NP * b + NP)
                            queries(b + 1)
                        elif s[0] == "E":
                            if s[1] >= 2:
                                act.wait_ge(rtotal_ready, NP * b + s[1] - 1)
                            exponentials(b, s[1])
                        elif s[0] == "E'":
                            act.wait_ge(rtotal_ready, NP * b + NP - 1)
                            exponentials(b + 1, 0)
                        elif s[0] == "O":
                            p = s[1]
                            act.wait_ge(o_done, NP * b + p + 1)
                            act.wait_ge(rtotal_ready, NP * b + p + 1)
                            if p == 0:
                                act.wait_ge(out_free, b + 1)
                            for h in range(2):
                                nc.scalar.activation(
                                    out_b[:, (2 * p + h) * DH:(2 * p + h + 1) * DH],
                                    ps_o[h * S:(h + 1) * S, (p % 2) * 64 + h * DH:(p % 2) * 64 + (h + 1) * DH],
                                    ACT.Copy, scale=rtotal[h * S:(h + 1) * S, p % 2:p % 2 + 1]).then_inc(o_read, 1)

                batches(act, first, body)

            @block.vector
            def _(dve):
                def low(out, psum, hi, scale=None):
                    if scale is None:
                        return nc.vector.tensor_tensor(out, psum, hi, ALU.subtract)
                    op = ALU.add if not isinstance(scale, float) else ALU.mult
                    return nc.vector.scalar_tensor_tensor(out=out, in0=psum, scalar=scale, in1=hi, op0=op,
                                                          op1=ALU.subtract)

                def queries(b):
                    for h in range(4):
                        dve.wait_ge(q_hi, 4 * b + h + 1)
                        last = nc.vector.scalar_tensor_tensor(
                            out=q_s[:, 1, h::4, :], in0=q_raw[:], scalar=const[:, C_HEAD32 + h:C_HEAD32 + h + 1],
                            in1=q_s[:, 0, h::4, :].bitcast(F32), op0=ALU.mult, op1=ALU.subtract)
                    last.then_inc(q_ready, 1)

                def masks(b):
                    dve.wait_ge(mask_in, 32 * b + 32)
                    nc.vector.tensor_scalar(mask01[:, 0:KEYS], mask_raw[:], 0, None, ALU.not_equal).then_inc(mask_ready, 1)
                    nc.vector.tensor_scalar(mask_add[:, 0:KEYS], mask_raw[:], 0, MASKED, ALU.is_equal,
                                            ALU.mult).then_inc(mask_ready, 1)

                def keys(bank, c, j):
                    cols = slice(j * KC, (j + 1) * KC)
                    low(kT[:, c % 2, 1, cols], bank[:, 0:KC], kT[:, c % 2, 0, cols].bitcast(F32),
                        bias[:, BK + c:BK + c + 1]).then_inc(job_lo, 1)

                def values(bank, kt):
                    n = tile_keys(kt)
                    low(v[0:n, 1, kt, :], bank[0:n, :], v[0:n, 0, kt, :], V_SCALE).then_inc(job_lo, 1)

                def masked_scores(b, p):
                    if p == 0:
                        dve.wait_ge(mask_ready, 2 * b + 2)
                    dve.wait_ge(scores, NP * b + p + 1)
                    nc.vector.tensor_tensor(prob[:, p % 2, :].rearrange("p (c n) -> p c n", n=KC),
                                            ps_s[:, :, 0:KC], mask01[:].rearrange("p (c n) -> p c n", n=KC),
                                            ALU.mult).then_inc(scores_read, 1)

                def maxima(b, p):
                    k = p % 2
                    dve.wait_ge(scores_read, NP * b + p + 1)
                    nc.vector.memset(negmax[:, k:k + 1], 0.0).then_inc(max_done, 1)
                    nc.vector.tensor_tensor_reduce(
                        out=prob[:, k, :], in0=prob[:, k, :], in1=mask_add[:], scale=1.0, scalar=LOWEST,
                        op0=ALU.add, op1=ALU.max, accum_out=biggest[:, k:k + 1]).then_inc(max_done, 1)
                    dve.wait_ge(max_done, 2 * (NP * b + p + 1))
                    nc.vector.tensor_scalar_mul(negmax[:, k:k + 1], biggest[:, k:k + 1], -SCALE).then_inc(max_ready, 1)

                def first():
                    nc.vector.memset(mask01[:, KEYS:], 0.0).then_inc(pads, 1)
                    nc.vector.memset(mask_add[:, KEYS:], LOWEST).then_inc(pads, 1)
                    dve.wait_ge(pads, 2)

                    def job(n):
                        if n == 1:
                            for j in range(SLOTS, NC):
                                context_low(dve, nc.vector, keep, 0, j)
                        if n == 2:
                            queries(0)
                            masks(0)
                        dve.wait_ge(job_hi, n + 1)
                        return {"K": keys, "V": values}

                    first_steps(job, {"S": masked_scores, "M": maxima})

                def body(b, more):
                    for s in batch_steps(more):
                        if s in JOB_INDEX[more]:
                            dve.wait_ge(job_hi, jobs_before(b, s, more) + 1)
                            bank = ring[:, job_bank(JOB_INDEX[more][s])]
                        if s[0] == "K":
                            keys(bank, s[1], s[2])
                        elif s[0] in ("V", "V'"):
                            values(bank, s[1])
                        elif s[0] == "PT":
                            _, p, g = s
                            n = tile_keys(group(g)[0]) if len(group(g)) == 1 else P
                            cols = slice(4 * g, 4 * g + len(group(g)))
                            low(probT[0:n, 1, cols, :],
                                bank[0:n, 0:P * len(group(g))].rearrange("p (a c) -> p a c", c=P),
                                probT[0:n, 0, cols, :], P_SCALE).then_inc(job_lo, 1)
                            if g == 0:
                                dve.wait_ge(exp_done, NP * b + p + 1)
                                k = p % 2
                                if p >= 2:
                                    dve.wait_ge(o_read, 2 * (NP * b + p - 1))
                                nc.vector.tensor_scalar_mul(rtotal[:, k:k + 1], total[:, k:k + 1],
                                                            V_SCALE * P_SCALE).then_inc(total_scaled, 1)
                                dve.wait_ge(total_scaled, NP * b + p + 1)
                                nc.vector.reciprocal(rtotal[:, k:k + 1], rtotal[:, k:k + 1]).then_inc(rtotal_ready, 1)
                        elif s[0] == "C":
                            if s[1] not in POOL_PIECES:
                                context_low(dve, nc.vector, keep, b + 1, s[1])
                        elif s[0] == "Q":
                            queries(b + 1)
                        elif s[0] == "A":
                            masks(b + 1)
                        elif s[0] == "S":
                            masked_scores(b, s[1])
                        elif s[0] == "S'":
                            masked_scores(b + 1, 0)
                        elif s[0] == "M":
                            if s[1] >= 2:
                                dve.wait_ge(exp_done, NP * b + s[1] - 1)
                            maxima(b, s[1])
                        elif s[0] == "M'":
                            dve.wait_ge(exp_done, NP * b + NP - 1)
                            maxima(b + 1, 0)

                batches(dve, first, body)

            @block.tensor
            def _(pe):
                def three(out, a, b, start, stop):
                    for n, (i, j) in enumerate(((1, 0), (0, 1), (0, 0))):
                        last = nc.tensor.matmul(out, a(i), b(j), start=(start and n == 0), stop=(stop and n == 2))
                    return last

                def keys(bank, c, j):
                    for k in range(NK):
                        last = three(bank[:, 0:KC], lambda i: wk[:, i, k, c * P:(c + 1) * P],
                                     lambda i: ctx_s[:, i, k, j * KC:(j + 1) * KC], k == 0, k == NK - 1)
                    last.then_inc(job_done, 1)

                def values(bank, kt):
                    n = tile_keys(kt)
                    for k in range(NK):
                        last = three(bank[0:n, :], lambda i: ctx_s[:, i, k, kt * P:kt * P + n],
                                     lambda i: wv[:, i, k, :], k == 0, k == NK - 1)
                    last.then_inc(job_done, 1)

                def pair_scores(p):
                    for j in range(NC):
                        last = three(ps_s[:, j, 0:KC], lambda i: q_s[:, i, 2 * p:2 * p + 2, :].rearrange("p h s -> p (h s)"),
                                     lambda i: kT[:, p // 2 % 2, i, j * KC:(j + 1) * KC], True, True)
                    last.then_inc(scores, 1)

                def first():
                    def job(n):
                        if n < NC:
                            pe.wait_ge(ctx_ready[n], 1)
                        if n >= RING:
                            pe.wait_ge(job_lo, n - RING + 1)
                        return {"K": keys, "V": values}

                    def first_scores(_, p):
                        pe.wait_ge(q_ready, 1)
                        pe.wait_ge(job_lo, NC)
                        pair_scores(p)

                    first_steps(job, {"S": first_scores})

                def body(b, more):
                    for s in batch_steps(more):
                        if s in JOB_INDEX[more]:
                            n = JOB_INDEX[more][s]
                            pe.wait_ge(job_lo, FIRST_JOBS + b * NJ + bank_user(n) + 1)
                            bank = ring[:, job_bank(n)]
                        if s[0] == "K":
                            if s[1] == 0:
                                pe.wait_ge(ctx_ready[s[2]], b + 2)
                            keys(bank, s[1], s[2])
                        elif s[0] in ("V", "V'"):
                            values(bank, s[1])
                        elif s[0] == "S":
                            p = s[1]
                            if p > 1:
                                pe.wait_ge(job_lo, jobs_before(b, ("K", p // 2, NC - 1), more) + 1)
                            pe.wait_ge(scores_read, NP * b + p)
                            pair_scores(p)
                        elif s[0] == "S'":
                            pe.wait_ge(q_ready, b + 2)
                            pe.wait_ge(job_lo, jobs_before(b, ("K", 0, NC - 1)) + 1)
                            pe.wait_ge(scores_read, NP * b + NP)
                            pair_scores(0)
                        elif s[0] == "PT":
                            _, p, g = s
                            pe.wait_ge(exp_done, NP * b + p + 1)
                            for a, kt in enumerate(group(g)):
                                n = tile_keys(kt)
                                last = nc.tensor.transpose(bank[0:n, a * P:(a + 1) * P],
                                                           prob[:, p % 2, kt * P:kt * P + n], ident)
                            last.then_inc(job_done, 1)
                        elif s[0] == "PV":
                            _, p, g = s
                            if p == 0 and g:
                                pe.wait_ge(job_lo, jobs_before(b, ("V", group(g)[-1]), more) + 1)
                            else:
                                pe.wait_ge(job_lo, jobs_before(b, ("PT", p, g), more) + 1)
                            if g == 0 and p:
                                pe.wait_ge(o_read, 2 * (NP * b + p))
                            for kt in group(g):
                                n = tile_keys(kt)
                                last = three(ps_o[:, (p % 2) * 64:(p % 2) * 64 + 64],
                                             lambda i: probT[0:n, i, kt, :],
                                             lambda i: v[0:n, i, kt, p * 64:(p + 1) * 64],
                                             kt == 0, kt == NKT - 1)
                            if g == NG - 1:
                                last.then_inc(o_done, 1)

                batches(pe, first, body)




class Norm:

    def __init__(self, nc, ctx, name):
        def sb(tile, shape):
            return ctx.enter_context(nc.sbuf_tensor(f"{name}_{tile}", shape, F32))

        self.stats, self.mom = sb("stats", [P, NT, 6]), sb("mom", [P, NT, 2])
        self.std, self.root, self.rstd, self.square = (sb(t, [P, NT]) for t in ("std", "root", "rstd", "square"))
        self.var_ready = ctx.enter_context(nc.semaphore(name + "_var_ready"))
        self.root_ready = ctx.enter_context(nc.semaphore(name + "_root_ready"))

    def tile_stats(self, nc, chain, x, t):
        chain.step(nc.vector.bn_stats(self.stats[:, t, :], x[:, t, :]))

    def vector(self, nc, dve, chain, x, eps, about_zero=False, stats=True):
        if stats:
            for t in range(NT):
                self.tile_stats(nc, chain, x, t)
        chain.wait()
        for t in range(NT):
            chain.step(nc.vector.bn_aggr(self.mom[:, t, :], self.stats[:, t, :]))
        chain.wait()
        if about_zero:
            chain.link(nc.vector.tensor_tensor(self.square[:], self.mom[:, :, 0], self.mom[:, :, 0], ALU.mult))
            nc.vector.scalar_tensor_tensor(out=self.std[:], in0=self.square[:], scalar=eps, in1=self.mom[:, :, 1],
                                           op0=ALU.add, op1=ALU.add).then_inc(self.var_ready, 1)
        else:
            nc.vector.tensor_scalar_add(self.std[:], self.mom[:, :, 1], eps).then_inc(self.var_ready, 1)
        dve.wait_ge(self.root_ready, 1)
        chain.link(nc.vector.reciprocal(self.rstd[:], self.root[:]))

    def scalar(self, nc, act):
        act.wait_ge(self.var_ready, 1)
        nc.scalar.activation(self.root[:], self.std[:], ACT.Sqrt).then_inc(self.root_ready, 1)


def pe_transposes(nc, src, out, k, ident):
    for t in range(NT):
        last = nc.tensor.transpose(out[:, t * P:(t + 1) * P], src[:, t, k * P:(k + 1) * P], ident)
    return last


def pe_product(nc, out, lhsT, rhs, chunks):
    for k in range(chunks):
        last = nc.tensor.matmul(out, lhsT(k), rhs(k), start=(k == 0), stop=(k == chunks - 1))
    return last


R_BO, R_B2V, R_B2O, R_GAMMA, R_BETA, R_G1, R_G2 = range(7)
R_ALL = 7


EMB_BASE = D - S
TURNED = 2


def project_stage(nc, io, keep):
    with ExitStack() as ctx:
        def sb(name, shape, dt=F32):
            return ctx.enter_context(nc.sbuf_tensor("p_" + name, shape, dt))

        def sem(name):
            return ctx.enter_context(nc.semaphore("p_" + name))

        x, attn = sb("x", [P, NT, D]), sb("attn", [P, NT, D])
        attnT, hT, w2v = sb("attnT", [P, NK, T]), sb("hT", [P, NK, T]), sb("w2v", [P, NK, D])
        wo, w2k = (keep["k_rel"][:, n * B * NP // 2:(n + 1) * B * NP // 2, :].rearrange(
            "p i s -> p (i s)").rearrange("p (k n) -> p k n", n=D) for n in range(2))
        w2q = keep["q_rel"][:, 0:B * NP // 2, :].rearrange("p i s -> p (i s)").rearrange("p (k n) -> p k n", n=D)
        qT_s = keep["q_rel"][:, B * NP // 2:, :].bitcast(F16).rearrange("p i s -> p (i s)").rearrange(
            "p (i k n) -> p i k n", i=2, n=T)
        emb, emb_s = sb("emb", [P, 2, P]), sb("emb_s", [P, 2, 2, P], F16)
        SLOTS = 8

        def stage(slot):
            return (x, attnT)[slot // 4][:, slot % 4, :]

        v = attn
        norm = Norm(nc, ctx, "p_norm")
        ps = ctx.enter_context(nc.psum_tensor("p_ps", [P, 8, 512], F32))
        const, bias, rows = keep["const"], keep["bias"], keep["rows"]
        x1, h, kT_s, qz, vz = (keep[n] for n in ("x1", "h", "kT_s", "qz", "vz"))
        kz = keep["kz"][:].bitcast(F16).rearrange("p b h s -> p (b h s)").rearrange(
            "p (i b h s) -> p i b h s", i=2, b=B, h=H)
        ident = const[:, C_IDENT:C_IDENT + P]
        attn_in, x_in, rows_in, wo_in, weights_in = map(sem, ("attn_in", "x_in", "rows_in", "wo_in", "weights_in"))
        dve_done, aT_ps, aT_ready, x1_ps, h_ready = map(sem, ("dve_done", "aT_psum", "aT_ready", "x1_psum", "h_ready"))
        hT_ps, hT_ready, k_ps, q_ps, v_ps, hi_ready = map(
            sem, ("hT_psum", "hT_ready", "k_psum", "q_psum", "v_psum", "hi_ready"))
        emb_in, rel_ps, act_staged, dve_staged, z_hi, z_lo, emb_hi, emb_lo, lo_done = map(
            sem, ("emb_in", "rel_psum", "act_staged", "dve_staged", "z_hi", "z_lo", "emb_hi", "emb_lo", "lo_done"))
        stored = [sem(f"stored{i}") for i in range(SLOTS)]
        sides = ((kz, 1, keep["k_rel"], io["k_rel"], keep["k_rel_in"]), (qz, 0, keep["q_rel"], io["q_rel"], keep["q_rel_in"]))
        JOBS = 2 * NP * B // 4
        with nc.Block() as block:

            def load_turned(eng, side):
                _, _, turned, scratch, turned_in = sides[side]
                for slot in range(SLOTS):
                    eng.wait_ge(stored[slot], 16 * (side + 1) * (JOBS // 2 // SLOTS))
                groups = len(turned_in)
                n = NP * B // groups
                for g in range(groups):
                    for half in range(2):
                        src = bass.AP(tensor=scratch.tensor, offset=g * n * P * P + half * S * P + S - 1,
                                      ap=[[P - 1, S], [P * P, n], [1, S]])
                        eng.dma_start(turned[half * S:(half + 1) * S, g * n:(g + 1) * n], src).then_inc(turned_in[g], 16)

            @block.sync
            def _(sp):
                sp.dma_start(attn[:], io["attn"].rearrange("(t two) s d -> (two s) t d", two=2)).then_inc(attn_in, 16)
                sp.dma_start(wo[:], io["woT"].rearrange("(k p) n -> p k n", p=P)).then_inc(wo_in, 16)
                sp.dma_start(x[:], io["x"].rearrange("(t p) d -> p t d", p=P)).then_inc(x_in, 16)
                sp.dma_start(rows[:, R_BO], io["bias_row"][R_BO].partition_broadcast(P)).then_inc(x_in, 16)
                for w, name in ((w2k, "w2k"), (w2q, "w2q"), (w2v, "w2v")):
                    sp.dma_start(w[:], io[name].rearrange("(k p) n -> p k n", p=P)).then_inc(weights_in, 16)
                sp.dma_start(emb[:, 0, :], io["emb_rev"]).then_inc(emb_in, 16)
                sp.dma_start(emb[:, 1, :], io["emb_fwd"]).then_inc(emb_in, 16)
                for n in range(JOBS):
                    side, m = divmod(n, JOBS // 2)
                    scratch = sides[side][3]
                    sp.wait_ge(act_staged if n % 2 == 0 else dve_staged, n // 2 + 1)
                    sp.dma_start(scratch[4 * m:4 * m + 4].rearrange("i p j -> p i j"),
                                 stage(n % SLOTS).rearrange("p (i j) -> p i j", j=P)).then_inc(stored[n % SLOTS], 16)
                load_turned(sp, 1)

            @block.gpsimd
            def _(pool):
                pool.dma_start(rows[:, R_BO + 1:], io["bias_row"][R_BO + 1:].partition_broadcast(P)).then_inc(rows_in, 16)
                load_turned(pool, 0)

            @block.tensor
            def _(pe):
                pe.wait_ge(attn_in, 16)
                for k in range(NK):
                    pe_transposes(nc, attn, ps[:, k, :], k, ident).then_inc(aT_ps, 1)
                pe.wait_ge(wo_in, 16)
                pe.wait_ge(aT_ready, NK)
                for t in range(NT):
                    pe_product(nc, ps[:, 4 + t, :], lambda k: attnT[:, k, t * P:(t + 1) * P],
                               lambda k: wo[:, k, :], NK).then_inc(x1_ps, 1)
                pe.wait_ge(h_ready, NT)
                for k in range(NK):
                    pe_transposes(nc, h, ps[:, k, :], k, ident).then_inc(hT_ps, 1)
                pe.wait_ge(weights_in, 48)
                pe.wait_ge(hT_ready, NK)
                for c in range(NK):
                    pe_product(nc, ps[:, 4 + c, :], lambda k: w2k[:, k, c * P:(c + 1) * P],
                               lambda k: hT[:, k, :], NK).then_inc(k_ps, 1)
                for c in range(NK):
                    pe_product(nc, ps[:, c, :], lambda k: w2q[:, k, c * P:(c + 1) * P],
                               lambda k: hT[:, k, :], NK).then_inc(q_ps, 1)
                pe.wait_ge(emb_lo, 1)
                for n in range(JOBS):
                    side, m = divmod(n, JOBS // 2)
                    z, table = sides[side][:2]
                    if m == 0:
                        pe.wait_ge(z_hi, side + 1)
                        pe.wait_ge(z_lo, side + 1)
                    if n < NK:
                        pe.wait_ge(lo_done, NK + n + 1)
                    if n >= 8:
                        pe.wait_ge(act_staged if n % 2 == 0 else dve_staged, (n - 8) // 2 + 1)
                    for a in range(4):
                        b, p = divmod(4 * m + a, NP)
                        for k, (i, j) in enumerate(((1, 0), (0, 1), (0, 0))):
                            last = nc.tensor.matmul(ps[:, n % 8, a * P:(a + 1) * P],
                                                    z[:, i, b, 2 * p:2 * p + 2, :].rearrange("p h s -> p (h s)"),
                                                    emb_s[:, j, table, :], start=(k == 0), stop=(k == 2))
                    last.then_inc(rel_ps, 1)
                for t in range(NT):
                    pe.wait_ge(act_staged if t % 2 == 0 else dve_staged, (JOBS - 8 + t) // 2 + 1)
                    pe_product(nc, ps[:, t, :], lambda k: hT[:, k, t * P:(t + 1) * P],
                               lambda k: w2v[:, k, :], NK).then_inc(v_ps, 1)

            def staged(eng, copy, parity, done):
                for n in range(parity, JOBS, 2):
                    eng.wait_ge(rel_ps, n + 1)
                    if n >= SLOTS:
                        eng.wait_ge(stored[n % SLOTS], 16 * (n // SLOTS))
                    copy(stage(n % SLOTS), ps[:, n % 8]).then_inc(done, 1)

            @block.scalar
            def _(act):
                for k in range(NK):
                    act.wait_ge(aT_ps, k + 1)
                    nc.scalar.activation(attnT[:, k, :], ps[:, k, :], ACT.Identity,
                                         bias=bias[:, BV + k:BV + k + 1]).then_inc(aT_ready, 1)
                norm.scalar(nc, act)
                act.wait_ge(emb_in, 32)
                nc.scalar.copy(emb_s[:, 0], emb[:]).then_inc(emb_hi, 1)
                for n, (halves, z, psum, bank, bias_at) in enumerate(((kT_s, kz, k_ps, 4, B2K), (qT_s, qz, q_ps, 0, B2Q))):
                    for c in range(NK):
                        act.wait_ge(psum, c + 1)
                        nc.scalar.activation(halves[:, 0, c, :], ps[:, bank + c, :], ACT.Identity,
                                             bias=bias[:, bias_at + c:bias_at + c + 1]).then_inc(hi_ready, 1)
                        act.wait_ge(hi_ready, NK * n + c + 1)
                        for j in range(4):
                            last = nc.scalar.activation(
                                z[:, 0, :, 4 * c + j, :], halves[:, 0, c, :].rearrange("p (b s) -> p b s", s=S), ACT.Copy,
                                scale=const[:, C_HEAD32 + j:C_HEAD32 + j + 1])
                    last.then_inc(z_hi, 1)
                staged(act, nc.scalar.copy, 0, act_staged)

            @block.vector
            def _(dve):
                chain = Chain(dve, dve_done)
                dve.wait_ge(x_in, 32)
                chain.link(nc.vector.tensor_tensor(
                    x1[:], x[:], rows[:, R_BO, :].unsqueeze(1).broadcast_to([P, NT, D]), ALU.add))
                for t in range(NT):
                    dve.wait_ge(x1_ps, t + 1)
                    chain.link(nc.vector.tensor_tensor(x1[:, t, :], x1[:, t, :], ps[:, 4 + t, :], ALU.add))
                    norm.tile_stats(nc, chain, x1, t)
                norm.vector(nc, dve, chain, x1, 1e-5, stats=False)
                for t in range(NT):
                    nc.vector.tensor_scalar(h[:, t, :], x1[:, t, :], norm.mom[:, t, 0:1], norm.rstd[:, t:t + 1],
                                            ALU.subtract, ALU.mult).then_inc(h_ready, 1)
                for k in range(NK):
                    dve.wait_ge(hT_ps, k + 1)
                    nc.vector.tensor_copy(hT[:, k, :], ps[:, k, :]).then_inc(hT_ready, 1)
                dve.wait_ge(emb_hi, 1)
                nc.vector.tensor_tensor(emb_s[:, 1], emb[:], emb_s[:, 0], ALU.subtract).then_inc(emb_lo, 1)
                for n, (halves, z, bank, bias_at) in enumerate(((kT_s, kz, 4, B2K), (qT_s, qz, 0, B2Q))):
                    for c in range(NK):
                        dve.wait_ge(hi_ready, NK * n + c + 1)
                        nc.vector.scalar_tensor_tensor(
                            out=halves[:, 1, c, :], in0=ps[:, bank + c, :], scalar=bias[:, bias_at + c:bias_at + c + 1],
                            in1=halves[:, 0, c, :], op0=ALU.add, op1=ALU.subtract).then_inc(lo_done, 1)
                        dve.wait_ge(lo_done, NK * n + c + 1)
                        for j in range(4):
                            last = nc.vector.tensor_scalar_mul(
                                z[:, 1, :, 4 * c + j, :], halves[:, 1, c, :].rearrange("p (b s) -> p b s", s=S),
                                const[:, C_HEAD32 + j:C_HEAD32 + j + 1])
                    last.then_inc(z_lo, 1)
                staged(dve, nc.vector.tensor_copy, 1, dve_staged)
                dve.wait_ge(rows_in, 16)
                for t in range(NT):
                    dve.wait_ge(v_ps, t + 1)
                    chain.link(nc.vector.tensor_tensor(v[:, t, :], ps[:, t, :], rows[:, R_B2V, :], ALU.add))
                for two in range(2):
                    nc.vector.tensor_scalar_mul(vz[:, two], v[:], const[:, C_PARITY + two:C_PARITY + two + 1])


def attention(nc, ctx, name, keep, dk, scale, rel, project=None):
    def sb(n, shape, dt=F32):
        return ctx.enter_context(nc.sbuf_tensor(f"{name}_{n}", shape, dt))

    def sem(n):
        return ctx.enter_context(nc.semaphore(f"{name}_{n}"))

    prob = keep["prob"]
    probT = keep["probT"]
    biggest, total, rtotal = (sb(n, [P, NT, 2, NP]) for n in ("biggest", "total", "rtotal"))
    ps = ctx.enter_context(nc.psum_tensor(name + "_ps", [P, 8, 512], F32))
    chain_done, s_ps, s_read, x_ready, exp_ready = map(sem, ("chain", "scores", "s_read", "shifted", "exp"))
    t_ps, t_read, o_ps, out_ready, max_ready = map(sem, ("t_psum", "t_read", "o_psum", "out_ready", "max_ready"))
    qz, kT_s, vz, const, out = keep["qz"], keep["kT_s"], keep["vz"], keep["const"], keep["out"]
    ident = const[:, C_IDENT:C_IDENT + P]
    in_chunk = P // dk
    if project:
        weights, weights_in, outT, use, then = project
        oT_ps, oT_ready, proj_ps, proj_read = map(sem, ("oT_psum", "oT_ready", "proj_psum", "proj_read"))
        chunks = H * dk // P

    def tensor(pe):
        def scores(b):
            if b >= 4:
                pe.wait_ge(s_read, b - 3)
            for p in range(NP):
                for n, (i, j) in enumerate(((1, 0), (0, 1), (0, 0))):
                    last = nc.tensor.matmul(ps[:, b % 4, p * S:(p + 1) * S],
                                            qz[:, i, b, 2 * p:2 * p + 2, :].rearrange("p h s -> p (h s)"),
                                            kT_s[:, j, 2 * p // in_chunk, b * S:(b + 1) * S],
                                            start=(n == 0), stop=(n == 2 and not rel))
                if rel:
                    if b == 0 and p == 0:
                        pe.wait_ge(keep["k_rel_in"][0], 32)
                    for two in range(2):
                        last = nc.tensor.matmul(ps[two * S:(two + 1) * S, b % 4, p * S:(p + 1) * S],
                                                keep["k_rel"][:, b * NP + p, :],
                                                ident[:, two * S:(two + 1) * S], start=False, stop=True)
            last.then_inc(s_ps, 1)

        def transposes(t):
            pe.wait_ge(exp_ready, 2 * t + 2)
            for g in range(2):
                n = 2 * t + g
                if n >= 2:
                    pe.wait_ge(t_read, n - 1)
                for a in range(4):
                    last = nc.tensor.transpose(ps[:, 4 + g, a * P:(a + 1) * P],
                                               prob[:, t, 4 * g + a].rearrange("p b s -> p (b s)"), ident)
                last.then_inc(t_ps, 1)

        def outputs(t):
            pe.wait_ge(t_read, 2 * t + 2)
            if t >= 2:
                pe.wait_ge(out_ready, 4 * (t - 1))
            for p in range(NP):
                for two in range(2):
                    h = 2 * p + two
                    last = nc.tensor.matmul(
                        ps[two * S:(two + 1) * S, 6 + t % 2, p * 2 * dk:(p + 1) * 2 * dk],
                        probT[:, t, p, two * S:(two + 1) * S], vz[:, :, t, h * dk:(h + 1) * dk],
                        start=True, stop=True)
            last.then_inc(o_ps, 1)

        def turn(t):
            pe.wait_ge(out_ready, 4 * (t + 1))
            pe.wait_ge(s_read, B - 3 + 2 * (t % 2))
            if t >= 2:
                pe.wait_ge(oT_ready, t - 1)
            for k in range(chunks):
                last = nc.tensor.transpose(ps[:, 2 * (t % 2), k * P:(k + 1) * P], out[:, t, k * P:(k + 1) * P], ident)
            last.then_inc(oT_ps, 1)

        def product(t):
            if t == 0:
                pe.wait_ge(weights_in, 16)
            pe.wait_ge(oT_ready, t + 1)
            pe.wait_ge(s_read, B - 2 + 2 * (t % 2))
            if t >= 2:
                pe.wait_ge(proj_read, t - 1)
            pe_product(nc, ps[:, 2 * (t % 2) + 1, :], lambda k: outT[:, k, t * P:(t + 1) * P],
                       lambda k: weights[:, k, :], chunks).then_inc(proj_ps, 1)

        for b in range(B):
            scores(b)
            if b >= 5 and b % 2:
                transposes(b // 2 - 2)
                outputs(b // 2 - 2)
        for t in range(NT):
            if project:
                turn(t)
            if t < 2:
                transposes(t + 2)
            if project:
                product(t)
            if t < 2:
                outputs(t + 2)

    def vector(dve):
        chain = Chain(dve, chain_done)

        def soft(b):
            t, two = divmod(b, 2)
            x = prob[:, t, :, two, :]
            dve.wait_ge(s_ps, b + 1)
            if rel:
                if b % (B // TURNED) == 0:
                    dve.wait_ge(keep["q_rel_in"][b // (B // TURNED)], 32)
                add = keep["q_rel"][:, b * NP:(b + 1) * NP, :]
            else:
                add = const[:, C_CAUSAL:C_CAUSAL + S].unsqueeze(1).broadcast_to([P, NP, S])
            ins = nc.vector.tensor_tensor(x, ps[:, b % 4].rearrange("p (a s) -> p a s", s=S), add, ALU.add)
            ins.then_inc(s_read, 1)
            dve.wait_ge(s_read, b + 1)
            big = biggest[:, t, two, :]
            nc.vector.reduce_max(big, x, AX.X).then_inc(max_ready, 1)

        def sums(b):
            t, two = divmod(b, 2)
            dve.wait_ge(exp_ready, b + 1)
            chain.link(nc.vector.reduce_sum(total[:, t, two, :], prob[:, t, :, two, :], AX.X))
            chain.link(nc.vector.reciprocal(rtotal[:, t, two, :], total[:, t, two, :]))

        def outputs(t):
            dve.wait_ge(o_ps, t + 1)
            o = ps[:, 6 + t % 2, 0:NP * 2 * dk].rearrange("p (a b d) -> p a b d", b=2, d=dk)
            dst = out[:, t, :].rearrange("p (a h d) -> p a h d", h=2, d=dk)
            for h in range(2):
                for b in range(2):
                    nc.vector.tensor_tensor(
                        dst[b * S:(b + 1) * S, :, h, :], o[h * S:(h + 1) * S, :, b, :],
                        rtotal[h * S:(h + 1) * S, t, b, :].unsqueeze(2).broadcast_to([S, NP, dk]),
                        ALU.mult).then_inc(out_ready, 1)

        for b in range(B):
            soft(b)
            if b >= 2:
                sums(b - 2)
            if b >= 5 and b % 2:
                outputs(b // 2 - 2)
        sums(B - 2)
        sums(B - 1)
        for t in range(NT):
            if project:
                dve.wait_ge(proj_ps, t + 1)
                use(t, ps[:, 2 * (t % 2) + 1, :]).then_inc(proj_read, 1)
            if t < 2:
                outputs(t + 2)
            if project:
                dve.wait_ge(proj_read, t + 1)
                then(t)

    def scalar(act):
        def exps(b):
            t, two = divmod(b, 2)
            act.wait_ge(x_ready, b + 1)
            nc.scalar.activation(prob[:, t, :, two, :], prob[:, t, :, two, :], ACT.Exp,
                                 scale=scale).then_inc(exp_ready, 1)

        def copies(t):
            for g in range(2):
                act.wait_ge(t_ps, 2 * t + g + 1)
                nc.scalar.activation(probT[:, t, 4 * g:4 * g + 4, :],
                                     ps[:, 4 + g, :].rearrange("p (a q) -> p a q", q=P), ACT.Copy).then_inc(t_read, 1)

        def turned(t):
            if project:
                act.wait_ge(oT_ps, t + 1)
                nc.scalar.copy(outT[:, :, t * P:(t + 1) * P],
                               ps[:, 2 * (t % 2), 0:chunks * P].rearrange("p (k q) -> p k q", q=P)).then_inc(oT_ready, 1)

        for b in range(B):
            exps(b)
            if b >= 3 and b % 2 and b < B - 1:
                copies(b // 2 - 1)
        turned(0)
        copies(NT - 2)
        turned(1)
        copies(NT - 1)
        turned(2)
        turned(3)

    def gpsimd(pool):
        for b in range(B):
            t, two = divmod(b, 2)
            pool.wait_ge(max_ready, b + 1)
            x = prob[:, t, :, two, :]
            nc.gpsimd.tensor_tensor(x, x, biggest[:, t, two, :].unsqueeze(2).broadcast_to([P, NP, S]),
                                    ALU.subtract).then_inc(x_ready, 1)

    return tensor, scalar, vector, gpsimd


def self_attention(nc, io, keep):
    with ExitStack() as ctx:
        def sb(name, shape, dt=F32):
            return ctx.enter_context(nc.sbuf_tensor("s_" + name, shape, dt))

        def sem(name):
            return ctx.enter_context(nc.semaphore("s_" + name))

        out = sb("out", [P, NT, D])
        outT, hh, wo = sb("outT", [P, NK, T]), sb("hh", [P, NT, D]), sb("wo", [P, NK, D])
        norm = Norm(nc, ctx, "s_norm")
        rows, x1, h, x2 = keep["rows"], keep["x1"], keep["h"], keep["x2"]
        dve_done, wo_in = sem("dve_done"), sem("wo_in")

        def use(t, psum):
            return nc.vector.tensor_tensor(hh[:, t, :], hh[:, t, :], psum, ALU.add)

        chains = []

        def then(t):
            norm.tile_stats(nc, chains[0], hh, t)

        tensor, scalar, vector, gpsimd = attention(nc, ctx, "s", dict(keep, out=out), DH, SCALE, True, (wo, wo_in, outT, use, then))
        with nc.Block() as block:

            @block.sync
            def _(sp):
                sp.dma_start(wo[:], io["w2o"].rearrange("(k p) n -> p k n", p=P)).then_inc(wo_in, 16)

            block.tensor(tensor)
            block.gpsimd(gpsimd)

            @block.scalar
            def _(act):
                scalar(act)
                norm.scalar(nc, act)

            @block.vector
            def _(dve):
                chain = Chain(dve, dve_done)

                def row(r):
                    return rows[:, r, :].unsqueeze(1).broadcast_to([P, NT, D])

                chain.step(nc.vector.tensor_tensor(hh[:], h[:], row(R_B2O), ALU.add))
                chain.link(nc.vector.tensor_tensor(x1[:], x1[:], row(R_BETA), ALU.add))
                chains.append(chain)
                vector(dve)
                norm.vector(nc, dve, chain, hh, 1e-12, stats=False)
                for t in range(NT):
                    chain.step(nc.vector.scalar_tensor_tensor(out=hh[:, t, :], in0=hh[:, t, :], scalar=norm.mom[:, t, 0:1],
                                                              in1=rows[:, R_GAMMA, :], op0=ALU.subtract, op1=ALU.mult))
                chain.wait()
                for t in range(NT):
                    nc.vector.scalar_tensor_tensor(out=x2[:, t, :], in0=hh[:, t, :], scalar=norm.rstd[:, t:t + 1],
                                                   in1=x1[:, t, :], op0=ALU.mult, op1=ALU.add)


L = D // 2
DL = L // H
NL = L // P
E = 8
F = 2 * D
NF = F // P


def low_rank_stage(nc, io, keep):
    with ExitStack() as ctx:
        def sb(name, shape, dt=F32):
            return ctx.enter_context(nc.sbuf_tensor("l_" + name, shape, dt))

        def sem(name):
            return ctx.enter_context(nc.semaphore("l_" + name))

        down, wqk, wv = sb("down", [P, NK, L]), sb("wqk", [P, NL, 2 * L]), sb("wv", [P, NL, L])
        g, gT, cT, rot = sb("g", [P, NT, D]), sb("gT", [P, NK, T]), sb("cT", [P, NL, T]), sb("rot", [P, NT, 2 * L])
        prods = [keep["prob"][:, i].rearrange("p a b s -> p (a b s)").rearrange("p (h i) -> p h i", i=DL // 2)
                 for i in range(4)]
        norm, rms = Norm(nc, ctx, "l_norm"), Norm(nc, ctx, "l_rms")
        ps = ctx.enter_context(nc.psum_tensor("l_ps", [P, 8, 512], F32))
        qT_s = sb("qT_s", [P, 2, NL, T], F16)
        const, rows, x2, f, kT_s, qz, vz = (keep[n] for n in ("const", "rows", "x2", "f", "kT_s", "qz", "vz"))
        ident = const[:, C_IDENT:C_IDENT + P]
        w_in, dve_done, g_ready, gT_ps, gT_ready, c_ps, c_ready, qk_ps, v_ps = map(
            sem, ("w_in", "dve_done", "g_ready", "gT_psum", "gT_ready", "c_psum", "c_ready", "qk_psum", "v_psum"))
        rot_ready, rot_ps, hi_ready, lo_done = map(sem, ("rot_ready", "rot_psum", "hi_ready", "lo_done"))
        with nc.Block() as block:

            ACT_PADS = 10

            def pad_queries(ins, half, h):
                c, j = divmod(h, H // NL)
                src, row = qT_s[:, half, c, :].rearrange("p (b s) -> p b s", s=S), const[:, C_HEAD16 + j:C_HEAD16 + j + 1]
                if ins is nc.vector:
                    ins.tensor_scalar_mul(qz[:, half, :, h, :], src, row)
                else:
                    ins.activation(qz[:, half, :, h, :], src, ACT.Copy, scale=row)

            @block.sync
            def _(sp):
                sp.dma_start(down[:], io["w_down"].rearrange("(k p) n -> p k n", p=P)).then_inc(w_in, 16)
                sp.dma_start(wqk[:, :, 0:L], io["w3q"].rearrange("(k p) n -> p k n", p=P)).then_inc(w_in, 16)
                sp.dma_start(wqk[:, :, L:], io["w3k"].rearrange("(k p) n -> p k n", p=P)).then_inc(w_in, 16)
                sp.dma_start(wv[:], io["w3v"].rearrange("(k p) n -> p k n", p=P)).then_inc(w_in, 16)

            @block.tensor
            def _(pe):
                pe.wait_ge(g_ready, NT)
                for k in range(NK):
                    pe_transposes(nc, g, ps[:, k, :], k, ident).then_inc(gT_ps, 1)
                pe.wait_ge(w_in, 64)
                pe.wait_ge(gT_ready, NK)
                for c in range(NL):
                    pe_product(nc, ps[:, 4 + c, :], lambda k: down[:, k, c * P:(c + 1) * P],
                               lambda k: gT[:, k, :], NK).then_inc(c_ps, 1)
                pe.wait_ge(c_ready, NL)
                for t in range(NT):
                    pe_product(nc, ps[:, t, :], lambda k: cT[:, k, t * P:(t + 1) * P],
                               lambda k: wqk[:, k, :], NL).then_inc(qk_ps, 1)
                for t in range(NT):
                    pe_product(nc, ps[:, 6 + t // 2, (t % 2) * L:(t % 2 + 1) * L],
                               lambda k: cT[:, k, t * P:(t + 1) * P], lambda k: wv[:, k, :], NL).then_inc(v_ps, 1)
                pe.wait_ge(rot_ready, 2 * NT)
                for c in range(2 * NL):
                    pe_transposes(nc, rot, ps[:, c, :], c, ident).then_inc(rot_ps, 1)

            @block.scalar
            def _(act):
                norm.scalar(nc, act)
                rms.scalar(nc, act)
                for c in range(NL):
                    act.wait_ge(c_ps, c + 1)
                    nc.scalar.copy(cT[:, c, :], ps[:, 4 + c, :]).then_inc(c_ready, 1)
                for two in range(2):
                    act.wait_ge(v_ps, NT)
                    nc.scalar.activation(vz[:, two], ps[:, 6:8, :].rearrange("p a (b n) -> p (a b) n", n=L), ACT.Copy,
                                         scale=const[:, C_PARITY + two:C_PARITY + two + 1])
                for c in range(NL):
                    act.wait_ge(rot_ps, c + 1)
                    nc.scalar.copy(qT_s[:, 0, c, :], ps[:, c, :]).then_inc(hi_ready, 1)
                act.wait_ge(rot_ps, 2 * NL)
                nc.scalar.copy(kT_s[:, 0], ps[:, NL:2 * NL, :]).then_inc(hi_ready, 1)
                act.wait_ge(hi_ready, NL)
                for h in range(ACT_PADS):
                    pad_queries(nc.scalar, 0, h)

            @block.vector
            def _(dve):
                chain = Chain(dve, dve_done)
                norm.vector(nc, dve, chain, x2, 1e-5)
                for t in range(NT):
                    last = nc.vector.tensor_scalar(f[:, t, :], x2[:, t, :], norm.mom[:, t, 0:1],
                                                   norm.rstd[:, t:t + 1], ALU.subtract, ALU.mult)
                    if t < NT - 1:
                        last.then_inc(dve_done, 1)
                        chain.n += 1
                chain.link(last)
                rms.vector(nc, dve, chain, f, 1e-5, about_zero=True)
                for t in range(NT):
                    nc.vector.scalar_tensor_tensor(out=g[:, t, :], in0=f[:, t, :], scalar=rms.rstd[:, t:t + 1],
                                                   in1=rows[:, R_G1, :], op0=ALU.mult, op1=ALU.mult).then_inc(g_ready, 1)
                for k in range(NK):
                    dve.wait_ge(gT_ps, k + 1)
                    nc.vector.tensor_copy(gT[:, k, :], ps[:, k, :]).then_inc(gT_ready, 1)
                shape = [P, 2 * H, DL // 2]
                for t in range(NT):
                    dve.wait_ge(qk_ps, t + 1)
                    pairs = ps[:, t, :].rearrange("p (h i two) -> p h i two", i=DL // 2, two=2)
                    for n, (part, table) in enumerate(((0, C_COS), (1, C_SIN), (0, C_SIN), (1, C_COS))):
                        chain.step(nc.vector.tensor_tensor(
                            prods[n][:, t * 2 * H:(t + 1) * 2 * H, :], pairs[:, :, :, part],
                            const[:, table:table + DL // 2].unsqueeze(1).broadcast_to(shape), ALU.mult))
                    chain.wait()
                    turned = rot[:, t, :].rearrange("p (h i two) -> p h i two", i=DL // 2, two=2)
                    a, b, c, d = (prod[:, t * 2 * H:(t + 1) * 2 * H, :] for prod in prods)
                    nc.vector.tensor_tensor(turned[:, :, :, 0], a, b, ALU.subtract).then_inc(rot_ready, 1)
                    nc.vector.tensor_tensor(turned[:, :, :, 1], c, d, ALU.add).then_inc(rot_ready, 1)
                for c in range(NL):
                    dve.wait_ge(hi_ready, c + 1)
                    last = nc.vector.tensor_tensor(qT_s[:, 1, c, :], ps[:, c, :], qT_s[:, 0, c, :], ALU.subtract)
                    last.then_inc(lo_done, 1)
                dve.wait_ge(hi_ready, NL + 1)
                nc.vector.tensor_tensor(kT_s[:, 1], ps[:, NL:2 * NL, :], kT_s[:, 0], ALU.subtract)
                dve.wait_ge(lo_done, NL)
                for h in range(H):
                    pad_queries(nc.vector, 1, h)
                for h in range(ACT_PADS, H):
                    pad_queries(nc.vector, 0, h)


def causal_attention(nc, io, keep):
    with ExitStack() as ctx:
        tensor, scalar, vector, gpsimd = attention(nc, ctx, "c", keep, DL, float(DL) ** -0.5, False)
        with nc.Block() as block:
            block.tensor(tensor)
            block.scalar(scalar)
            block.vector(vector)
            block.gpsimd(gpsimd)

            @block.sync
            def _(sp):
                sp.dma_start(keep["up"][:], io["w_up"].rearrange("(k p) n -> p k n", p=P)).then_inc(keep["up_in"], 16)
                sp.dma_start(keep["router"][:], io["router"].rearrange("(k p) n -> p k n", p=P)).then_inc(keep["up_in"], 16)
                for i in range(SLOTS_W):
                    keep["pieces"].load(sp, 0, i, wait=False)


def router_stage(nc, io, keep):
    with ExitStack() as ctx:
        def sb(name, shape, dt=F32):
            return ctx.enter_context(nc.sbuf_tensor("g_" + name, shape, dt))

        def sem(name):
            return ctx.enter_context(nc.semaphore("g_" + name))

        up, router, w_in = keep["up"], keep["router"], keep["up_in"]
        outT, g, gT = sb("outT", [P, NL, T]), sb("g", [P, NT, D]), sb("gT", [P, NK, T])
        norm = Norm(nc, ctx, "g_norm")
        ps = ctx.enter_context(nc.psum_tensor("g_ps", [P, 8, 512], F32))
        const, rows, f, out, t_s, pieces = (keep[n] for n in ("const", "rows", "f", "out", "t_s", "pieces"))
        ident = const[:, C_IDENT:C_IDENT + P]
        dve_done, oT_ps, oT_ready, h_ps, g_ready, gT_ps, gT_ready, t_hi, logits = map(
            sem, ("dve_done", "oT_psum", "oT_ready", "h_psum", "g_ready", "gT_psum", "gT_ready", "t_hi", "logits"))
        with nc.Block() as block:

            @block.sync
            def _(sp):
                for i in range(SLOTS_W, N13):
                    pieces.load(sp, 0, i)

            @block.tensor
            def _(pe):
                for k in range(NL):
                    pe_transposes(nc, out, ps[:, k, :], k, ident).then_inc(oT_ps, 1)
                pe.wait_ge(w_in, 32)
                pe.wait_ge(oT_ready, NL)
                for t in range(NT):
                    pe_product(nc, ps[:, 4 + t, :], lambda k: outT[:, k, t * P:(t + 1) * P],
                               lambda k: up[:, k, :], NL).then_inc(h_ps, 1)
                pe.wait_ge(g_ready, NT)
                for k in range(NK):
                    pe_transposes(nc, g, ps[:, k, :], k, ident).then_inc(gT_ps, 1)
                pe.wait_ge(gT_ready, NK)
                for t in range(NT):
                    last = pe_product(nc, ps[:, 4, t * E:(t + 1) * E], lambda k: gT[:, k, t * P:(t + 1) * P],
                                      lambda k: router[:, k, :], NK)
                last.then_inc(logits, 1)

            @block.scalar
            def _(act):
                for k in range(NL):
                    act.wait_ge(oT_ps, k + 1)
                    nc.scalar.copy(outT[:, k, :], ps[:, k, :]).then_inc(oT_ready, 1)
                for i in range(4):
                    pieces.high(act, 0, i)
                norm.scalar(nc, act)
                for k in range(NK):
                    act.wait_ge(gT_ready, k + 1)
                    nc.scalar.copy(t_s[:, 0, k, :], gT[:, k, :]).then_inc(t_hi, 1)
                for i in range(4, N13):
                    pieces.high(act, 0, i)

            @block.vector
            def _(dve):
                chain = Chain(dve, dve_done)
                for i in range(4):
                    pieces.low(dve, 0, i)
                for t in range(NT):
                    dve.wait_ge(h_ps, t + 1)
                    chain.link(nc.vector.tensor_tensor(f[:, t, :], f[:, t, :], ps[:, 4 + t, :], ALU.add))
                    norm.tile_stats(nc, chain, f, t)
                norm.vector(nc, dve, chain, f, 1e-5, about_zero=True, stats=False)
                for t in range(NT):
                    nc.vector.scalar_tensor_tensor(out=g[:, t, :], in0=f[:, t, :], scalar=norm.rstd[:, t:t + 1],
                                                   in1=rows[:, R_G2, :], op0=ALU.mult, op1=ALU.mult).then_inc(g_ready, 1)
                for k in range(NK):
                    dve.wait_ge(gT_ps, k + 1)
                    nc.vector.tensor_copy(gT[:, k, :], ps[:, k, :]).then_inc(gT_ready, 1)
                for k in range(NK):
                    dve.wait_ge(t_hi, k + 1)
                    nc.vector.tensor_tensor(t_s[:, 1, k, :], gT[:, k, :], t_s[:, 0, k, :].bitcast(F32), ALU.subtract)
                for i in range(4, N13):
                    pieces.low(dve, 0, i)
                dve.wait_ge(logits, 1)
                nc.vector.tensor_copy(keep["logits"][:], ps[:, 4, 0:NT * E].rearrange("p (t e) -> p t e", e=E))


class Gates:

    def __init__(self, nc, ctx, room):
        def sb(name, shape, dt=F32):
            return ctx.enter_context(nc.sbuf_tensor("w_" + name, shape, dt))

        self.big, self.total, self.rtotal = (sb(n, [P, NT]) for n in ("big", "total", "rtotal"))
        self.pr, self.best, self.which_f = room[:, :, 0:E], room[:, :, E:2 * E], room[:, :, 2 * E:3 * E]
        self.hit, self.weight = [room[:, :, 3 * E:4 * E], room[:, :, 4 * E:5 * E]], sb("weight", [P, NT, 2])
        self.which = sb("which", [P, NT, 8], U32)
        self.shifted, self.exp_ready, self.done = (
            ctx.enter_context(nc.semaphore("w_" + n)) for n in ("shifted", "exp_ready", "done"))

    def scalar(self, nc, act):
        act.wait_ge(self.shifted, 1)
        nc.scalar.activation(self.pr, self.pr, ACT.Exp).then_inc(self.exp_ready, 1)

    def vector(self, nc, dve, const, lg, gates):
        chain = Chain(dve, self.done)
        big, total, rtotal, pr, hit, best, weight, which_f, which = (
            self.big, self.total, self.rtotal, self.pr, self.hit, self.best, self.weight, self.which_f, self.which)
        chain.link(nc.vector.reduce_max(big[:], lg[:], AX.X))
        nc.vector.tensor_tensor(pr, lg[:], big[:].unsqueeze(2).broadcast_to([P, NT, E]),
                                ALU.subtract).then_inc(self.shifted, 1)
        dve.wait_ge(self.exp_ready, 1)
        chain.link(nc.vector.reduce_sum(total[:], pr, AX.X))
        chain.link(nc.vector.reciprocal(rtotal[:], total[:]))
        chain.link(nc.vector.tensor_tensor(pr, pr, rtotal[:].unsqueeze(2).broadcast_to([P, NT, E]), ALU.mult))
        for t in range(NT):
            chain.link(nc.vector.max(best[:, t, :], pr[:, t, :]))
            chain.link(nc.vector.max_index(which[:, t, :], best[:, t, :], pr[:, t, :]))
        chain.link(nc.vector.tensor_copy(which_f, which[:]))
        chain.link(nc.vector.tensor_tensor(total[:], best[:, :, 0], best[:, :, 1], ALU.add))
        chain.link(nc.vector.reciprocal(rtotal[:], total[:]))
        chain.link(nc.vector.tensor_tensor(weight[:], best[:, :, 0:2], rtotal[:].unsqueeze(2).broadcast_to([P, NT, 2]),
                                           ALU.mult))
        for t in range(NT):
            for n in range(2):
                chain.link(nc.vector.tensor_scalar(hit[n][:, t, :], const[:, C_IOTA:C_IOTA + E],
                                                   which_f[:, t, n:n + 1], weight[:, t, n:n + 1],
                                                   ALU.is_equal, ALU.mult))
        chain.link(nc.vector.tensor_tensor(gates[:], hit[0], hit[1], ALU.add))


PIECE = 1024
N13, N2 = 2 * NK, NF // 2
PIECES = N13 + N2
SLOTS_W = 6


def expert_steps(more):
    out = []
    for fc in range(NF):
        out.append(("H", fc))
        if fc < N2:
            out.append(("W2", fc))
    pieces = [("W13", i) for i in range(N13)] if more else []
    return out + pieces[:2] + [("Y", 0)] + pieces[2:5] + [("Y", 1)] + pieces[5:] + [("Y", 2), ("Y", 3)]


class Pieces:

    def __init__(self, nc, io, ctx):
        def sem(name):
            return ctx.enter_context(nc.semaphore("e_" + name))

        self.nc, self.io = nc, io
        self.raw = ctx.enter_context(nc.sbuf_tensor("e_raw", [P, SLOTS_W, PIECE], F32))
        self.w13 = self.w2 = None
        self.staged = [sem(f"staged{i}") for i in range(SLOTS_W)]
        self.w_hi, self.w_lo = sem("w_hi"), sem("w_lo")

    def source(self, e, i):
        if i < NK:
            return self.io["w1"][e, i * P:(i + 1) * P, :]
        if i < N13:
            return self.io["w3"][e, (i - NK) * P:(i - NK + 1) * P, :]
        i -= N13
        return self.io["w2"][e, 2 * i * P:2 * (i + 1) * P, :].rearrange("(two p) n -> p two n", p=P)

    def halves(self, i, half):
        if i < N13:
            return self.w13[:, half, i, :]
        return self.w2[:, half, 2 * (i - N13):2 * (i - N13) + 2, :].rearrange("p a n -> p (a n)")

    def load(self, sp, e, i, wait=True):
        slot = i % SLOTS_W
        if wait:
            sp.wait_ge(self.w_lo, PIECES * e + i - SLOTS_W + 1)
        dst = self.raw[:, slot] if i < N13 else self.raw[:, slot].rearrange("p (a n) -> p a n", a=2)
        sp.dma_start(dst, self.source(e, i)).then_inc(self.staged[slot], 16)

    def high(self, act, e, i):
        act.wait_ge(self.staged[i % SLOTS_W], 32 * e + (16 if i < SLOTS_W else 32))
        self.nc.scalar.copy(self.halves(i, 0), self.raw[:, i % SLOTS_W]).then_inc(self.w_hi, 1)

    def low(self, dve, e, i):
        dve.wait_ge(self.w_hi, PIECES * e + i + 1)
        self.nc.vector.tensor_tensor(self.halves(i, 1), self.raw[:, i % SLOTS_W], self.halves(i, 0).bitcast(F32),
                                     ALU.subtract).then_inc(self.w_lo, 1)


def experts(nc, io, keep):
    with ExitStack() as ctx:
        def sb(name, shape, dt=F32):
            return ctx.enter_context(nc.sbuf_tensor("e_" + name, shape, dt))

        def sem(name):
            return ctx.enter_context(nc.semaphore("e_" + name))

        pieces = keep["pieces"]
        w13, w_lo = pieces.w13, pieces.w_lo
        w2 = sb("w2", [P, 2, NF, D], F32R)
        pieces.w2 = w2
        hid = sb("hid", [P, 2, NF, T], F32R)
        gated, full = keep["f"][:, 0:2], keep["f"][:, 2:4]
        router = Gates(nc, ctx, keep["out"])
        ps_h = ctx.enter_context(nc.psum_tensor("e_ps_h", [P, 4, 512], F32))
        ps_y = ctx.enter_context(nc.psum_tensor("e_ps_y", [P, NT, 512], F32))
        y, gates, t_s = keep["x2"], keep["gates"], keep["t_s"]
        h_ps, silu_ready, full_ready, hid_hi, hid_lo, y_ps, y_read, stored = map(
            sem, ("h_psum", "silu_ready", "full_ready", "hid_hi", "hid_lo", "y_psum", "y_read", "stored"))

        def loop(eng, first, body):
            first()
            with eng.Fori(0, E - 1) as e:
                body(e, True)
            body(E - 1, False)

        with nc.Block() as block:

            @block.sync
            def _(sp):
                for i in range(N13, PIECES):
                    pieces.load(sp, 0, i)
                with sp.Fori(1, E) as e:
                    for i in range(PIECES):
                        pieces.load(sp, e, i)
                sp.wait_ge(y_read, NT * E)
                sp.dma_start(io["out"].rearrange("(t two) s d -> (two s) t d", two=2), y[:]).then_inc(stored, 16)
                sp.wait_ge(stored, 16)

            @block.scalar
            def _(act):
                def first():
                    router.scalar(nc, act)

                def body(e, more):
                    for s in expert_steps(more):
                        if s[0] == "H":
                            fc = s[1]
                            act.wait_ge(h_ps, 2 * (NF * e + fc) + 1)
                            nc.scalar.activation(gated[:, fc % 2, :], ps_h[:, 2 * (fc % 2), :], ACT.Silu).then_inc(silu_ready, 1)
                            act.wait_ge(full_ready, NF * e + fc + 1)
                            nc.scalar.copy(hid[:, 0, fc, :], full[:, fc % 2, :]).then_inc(hid_hi, 1)
                        elif s[0] == "W2":
                            pieces.high(act, e, N13 + s[1])
                        elif s[0] == "W13":
                            if s[1] == 0:
                                act.wait_ge(h_ps, 2 * NF * (e + 1))
                            pieces.high(act, e + 1, s[1])

                loop(act, first, body)

            @block.vector
            def _(dve):
                def first():
                    nc.vector.tensor_tensor(y[:], y[:], keep["f"][:], ALU.add)
                    router.vector(nc, dve, keep["const"], keep["logits"], gates)

                def body(e, more):
                    for s in expert_steps(more):
                        if s[0] == "H":
                            fc = s[1]
                            dve.wait_ge(h_ps, 2 * (NF * e + fc) + 2)
                            dve.wait_ge(silu_ready, NF * e + fc + 1)
                            nc.vector.tensor_tensor(full[:, fc % 2, :], gated[:, fc % 2, :], ps_h[:, 2 * (fc % 2) + 1, :],
                                                    ALU.mult).then_inc(full_ready, 1)
                            dve.wait_ge(hid_hi, NF * e + fc + 1)
                            nc.vector.tensor_tensor(hid[:, 1, fc, :], full[:, fc % 2, :], hid[:, 0, fc, :].bitcast(F32),
                                                    ALU.subtract).then_inc(hid_lo, 1)
                        elif s[0] == "W2":
                            pieces.low(dve, e, N13 + s[1])
                        elif s[0] == "W13":
                            pieces.low(dve, e + 1, s[1])
                        else:
                            t = s[1]
                            dve.wait_ge(y_ps, NT * e + t + 1)
                            nc.vector.scalar_tensor_tensor(out=y[:, t, :], in0=ps_y[:, t, :],
                                                           scalar=gates[:, t, bass.ds(e, 1)], in1=y[:, t, :],
                                                           op0=ALU.mult, op1=ALU.add).then_inc(y_read, 1)
                            dve.wait_ge(y_read, NT * e + t + 1)

                loop(dve, first, body)

            @block.tensor
            def _(pe):
                def three(out, a, b, start, stop):
                    for n, (i, j) in enumerate(((1, 0), (0, 1), (0, 0))):
                        last = nc.tensor.matmul(out, a(i), b(j), start=(start and n == 0), stop=(stop and n == 2))
                    return last

                def body(e, more):
                    for s in expert_steps(more):
                        if s[0] == "H":
                            fc = s[1]
                            if fc == 0:
                                pe.wait_ge(w_lo, PIECES * e + N13)
                            if fc >= 2:
                                pe.wait_ge(full_ready, NF * e + fc - 1)
                            for side in range(2):
                                for k in range(NK):
                                    last = three(ps_h[:, 2 * (fc % 2) + side, :],
                                                 lambda i: w13[:, i, side * NK + k, fc * P:(fc + 1) * P],
                                                 lambda i: t_s[:, i, k, :], k == 0, k == NK - 1)
                                last.then_inc(h_ps, 1)
                        elif s[0] == "Y":
                            t = s[1]
                            if t == 0:
                                pe.wait_ge(w_lo, PIECES * (e + 1))
                            for fc in range(NF):
                                if t == 0:
                                    pe.wait_ge(hid_lo, NF * e + fc + 1)
                                last = three(ps_y[:, t, :], lambda i: hid[:, i, fc, t * P:(t + 1) * P],
                                             lambda i: w2[:, i, fc, :], fc == 0, fc == NF - 1)
                            last.then_inc(y_ps, 1)

                loop(pe, lambda: None, body)


INPUTS = ("x", "ctxT", "mask", "wqT", "wkT", "wvT", "woT", "bias_col", "bias_row", "const",
          "w2q", "w2k", "w2v", "w2o", "emb_fwd", "emb_rev",
          "w_down", "w3q", "w3k", "w3v", "w_up", "router", "w1", "w2", "w3")


def build(nc, io):
    with ExitStack() as ctx:
        def sb(name, shape, dt=F32):
            return ctx.enter_context(nc.sbuf_tensor(name, shape, dt))

        keep = {"const": sb("const", [P, C_ALL]), "bias": sb("bias", [P, B_ALL])}
        with ExitStack() as first:
            keep["ctx_raw"] = first.enter_context(nc.sbuf_tensor("ctx_raw", [P, CTX_SLOTS, NK, KC], F32))
            keep["ctx_s"] = first.enter_context(nc.sbuf_tensor("ctx_s", [P, 2, NK, KPAD], F32R))
            keep["qT"] = first.enter_context(nc.sbuf_tensor("qT", [P, NK, T], F32))
            keep["q_out"] = first.enter_context(nc.semaphore("q_out"))
            keep["ctx_hi"] = first.enter_context(nc.semaphore("ctx_hi"))
            keep["ctx_ready"] = [first.enter_context(nc.semaphore(f"ctx_ready{j}")) for j in range(NC)]
            keep["ctx_in"] = [first.enter_context(nc.semaphore(f"ctx_in{i}")) for i in range(CTX_SLOTS)]
            keep["wk"] = first.enter_context(nc.sbuf_tensor("wk_s", [P, 2, NK, D], F32R))
            keep["wv"] = first.enter_context(nc.sbuf_tensor("wv_s", [P, 2, NK, D], F32R))
            query_stage(nc, io, keep)
            cross_attention(nc, io, keep)
        keep["rows"] = sb("rows", [P, R_ALL, D])
        keep["x2"] = sb("x2", [P, NT, D])
        with ExitStack() as second:
            for n, shape, dt in (("x1", [P, NT, D], F32), ("h", [P, NT, D], F32), ("kT_s", [P, 2, NK, T], F16),
                                 ("qz", [P, 2, B, H, S], F16), ("vz", [P, 2, NT, D], F32), ("kz", [P, B, H, S], F32)):
                keep[n] = second.enter_context(nc.sbuf_tensor(n, shape, dt))
            for n in ("q_rel", "k_rel"):
                keep[n] = second.enter_context(nc.sbuf_tensor(n, [P, B * NP, S], F32))
                keep[n + "_in"] = [second.enter_context(nc.semaphore(f"{n}_in{g}")) for g in range(TURNED if n == "q_rel" else 1)]
            project_stage(nc, io, keep)
            keep["prob"] = keep["kz"][:, 0:B // 2].rearrange("p t h s -> p (t h s)").rearrange("p (t a two s) -> p t a two s", a=NP, two=2, s=S)
            keep["probT"] = keep["kz"][:, B // 2:].rearrange("p t h s -> p (t h s)").rearrange(
                "p (t a q) -> p t a q", a=NP, q=P)
            self_attention(nc, io, keep)
        keep["t_s"] = sb("t_s", [P, 2, NK, T], F32R)
        keep["gates"] = sb("gates", [P, NT, E])
        keep["logits"] = sb("logits", [P, NT, E])
        keep["f"], keep["out"] = sb("f", [P, NT, D]), sb("c_out", [P, NT, L])
        keep["up"], keep["router"] = sb("up", [P, NL, D]), sb("router", [P, NK, E])
        keep["up_in"] = ctx.enter_context(nc.semaphore("up_in"))
        keep["pieces"] = Pieces(nc, io, ctx)
        with ExitStack() as fourth:
            for n, shape, dt in (("kT_s", [P, 2, NL, T], F16), ("qz", [P, 2, B, H, S], F16), ("vz", [P, 2, NT, L], F32),
                                 ("prob", [P, NT, NP, 2, S], F32), ("probT", [P, NT, NP, P], F32)):
                keep[n] = fourth.enter_context(nc.sbuf_tensor("c_" + n, shape, dt))
            low_rank_stage(nc, io, keep)
            causal_attention(nc, io, keep)
        keep["pieces"].w13 = sb("e_w13", [P, 2, N13, PIECE], F32R)
        router_stage(nc, io, keep)
        experts(nc, io, keep)


def kernel(**inputs):
    import concourse.bacc as bacc
    from concourse.bass_utils import run_bass_kernel_spmd as run

    a = {k: np.asarray(v) for k, v in inputs.items()}

    def columns(name):
        return a[name].reshape(-1, P).T

    emb = a["L0_attn_dist_emb"]
    laid_out = {
        "x": a["x"].reshape(T, D),
        "ctxT": np.pad(a["ctx_1024"].transpose(0, 2, 1), ((0, 0), (0, 0), (0, KPAD - KEYS))),
        "mask": a["mask_Bx1xSxS2_ik1"].reshape(B, S, KEYS),
        "wqT": a["L0_xattn_WQ_w"].T, "wkT": a["L0_xattn_WK_w"].T, "wvT": a["L0_xattn_WV_w"].T,
        "woT": a["L0_xattn_WO_w"].T,
        "bias_col": np.concatenate([columns(n) for n in ("L0_xattn_WQ_b", "L0_xattn_WK_b", "L0_xattn_WV_b",
                                                        "L0_attn_bq", "L0_attn_bk")], axis=1),
        "bias_row": np.stack([a[n] for n in ("L0_xattn_WO_b", "L0_attn_bv", "L0_attn_bo", "L0_attn_ln_gamma",
                                            "L0_attn_ln_beta", "L0_ffn_g1", "L0_ffn_g2")]),
        "w2q": a["L0_attn_Wq"], "w2k": a["L0_attn_Wk"], "w2v": a["L0_attn_Wv"], "w2o": a["L0_attn_Wo"],
        "emb_fwd": np.tile(emb[EMB_BASE:EMB_BASE + P].T, (4, 1)),
        "emb_rev": np.tile(emb[EMB_BASE - 1:EMB_BASE - 1 + P][::-1].T, (4, 1)),
        "w_down": a["L0_ffn_w_down"], "w3q": a["L0_ffn_wq"], "w3k": a["L0_ffn_wk"], "w3v": a["L0_ffn_wv"],
        "w_up": a["L0_ffn_w_up"], "router": a["L0_ffn_router_w"],
        "w1": a["L0_ffn_w1"], "w2": a["L0_ffn_w2"], "w3": a["L0_ffn_w3"],
        "const": constants(),
    }
    nc = bacc.Bacc("TRN2", target_bir_lowering=False, num_devices=1)
    io, arrays = {}, {}
    for name, value in laid_out.items():
        value = np.ascontiguousarray(value)
        arrays["in_" + name] = value
        io[name] = nc.dram_tensor("in_" + name, value.shape, mybir.dt.from_np(value.dtype), kind="ExternalInput").ap()
    io["qT"] = nc.dram_tensor("scratch_qT", (P, NK, T), F32, kind="Internal").ap()
    io["attn"] = nc.dram_tensor("scratch_attn", (B, S, D), F32, kind="Internal").ap()
    for n in ("q_rel", "k_rel"):
        io[n] = nc.dram_tensor("scratch_" + n, (B * NP, P, P), F32, kind="Internal").ap()
    io["out"] = nc.dram_tensor("out", (B, S, D), F32, kind="ExternalOutput").ap()
    build(nc, io)
    result = run(nc, [arrays], core_ids=[0])
    return result.results[0]["out"]
```
